# Optimizing a Trainium2 kernel written in Bass

```python
import numpy as np
import jax
import jax.numpy as jnp

def _softmax(x, axis=-1):
    return jax.nn.softmax(x, axis=axis)

def _gelu(x):
    return jax.nn.gelu(x, approximate=True)

def _silu(x):
    return jax.nn.silu(x)

def _sigmoid(x):
    return jax.nn.sigmoid(x)

def _layernorm(x, axis=-1, eps=1e-05):
    m = jnp.mean(x, axis=axis, keepdims=True)
    v = jnp.var(x, axis=axis, keepdims=True)
    return (x - m) / jnp.sqrt(v + eps)

def _scatter_add(tgt, idx, src, axis=0):
    return tgt.at[idx].add(src)

def _segment_sum(src, seg, n):
    return jax.ops.segment_sum(src, seg, n)
kernel_name = 'mk_sandwich_d2_jaxref_r4_c20565'

def setup_inputs(seed: int=0):
    np.random.seed(seed)
    _w = jnp.asarray

    def _L0_attn_setup():
        import jax, jax.numpy as jnp
        import numpy as np
        import math
        B, T, D, H = (4, 512, 256, 16)
        HD = D // H
        ROPE_BASE = 10000.0

        def apply_rope(x):
            t, hd = (x.shape[2], x.shape[3])
            half = hd // 2
            theta = 1.0 / ROPE_BASE ** (jnp.arange(0, hd, 2, dtype=jnp.float32) / hd)
            pos = jnp.arange(1, t + 1, dtype=jnp.float32)
            ang = pos[:, None] * theta[None, :]
            ang = jnp.concatenate([ang, ang], axis=-1)
            sin, cos = (jnp.sin(ang), jnp.cos(ang))
            rot = jnp.concatenate([-x[..., half:], x[..., :half]], axis=-1)
            return x * cos[None, None, :, :] + rot * sin[None, None, :, :]
        key = jax.random.key(seed)
        ks = jax.random.split(key, 9)
        s = 1.0 / math.sqrt(D)
        return {'x': jax.random.normal(ks[0], (B, T, D), dtype=jnp.float32), 'Wq': jax.random.normal(ks[1], (D, D), dtype=jnp.float32) * s, 'bq': jax.random.normal(ks[2], (D,), dtype=jnp.float32) * 0.01, 'Wk': jax.random.normal(ks[3], (D, D), dtype=jnp.float32) * s, 'bk': jax.random.normal(ks[4], (D,), dtype=jnp.float32) * 0.01, 'Wv': jax.random.normal(ks[5], (D, D), dtype=jnp.float32) * s, 'bv': jax.random.normal(ks[6], (D,), dtype=jnp.float32) * 0.01, 'Wo': jax.random.normal(ks[7], (D, D), dtype=jnp.float32) * s, 'bo': jax.random.normal(ks[8], (D,), dtype=jnp.float32) * 0.01}
    _L0_attn_in = _L0_attn_setup()

    def _L0_ffn_setup():
        import jax, jax.numpy as jnp
        import numpy as np
        DIM = 256
        HIDDEN = 768
        SCALE = 1.0 / 127.0

        def _dequant(w_int, dtype):
            return w_int.astype(dtype) * jnp.asarray(SCALE, dtype)
        key = jax.random.key(seed)
        k_x, k_g, k_u, k_d = jax.random.split(key, 4)
        x = jax.random.normal(k_x, (4, 512, DIM), dtype=jnp.float32)
        w_gate = jax.random.randint(k_g, (HIDDEN, DIM), -127, 128, dtype=jnp.int32)
        w_up = jax.random.randint(k_u, (HIDDEN, DIM), -127, 128, dtype=jnp.int32)
        w_down = jax.random.randint(k_d, (DIM, HIDDEN), -127, 128, dtype=jnp.int32)
        return {'x': x, 'w_gate': w_gate, 'w_up': w_up, 'w_down': w_down}
    _L0_ffn_in = _L0_ffn_setup()

    def _L1_attn_setup():
        import jax, jax.numpy as jnp
        import numpy as np
        B, N, D = (2, 512, 256)
        H, DH = (16, 64)
        SOFTCLAMP = 50.0
        SCALE = DH ** (-0.5)
        key = jax.random.key(seed)
        ks = jax.random.split(key, 5)
        std = D ** (-0.5)
        return {'x': jax.random.normal(ks[0], (B, N, D), dtype=jnp.float32), 'Wq': jax.random.normal(ks[1], (H * DH, D), dtype=jnp.float32) * std, 'Wk': jax.random.normal(ks[2], (H * DH, D), dtype=jnp.float32) * std, 'Wv': jax.random.normal(ks[3], (H * DH, D), dtype=jnp.float32) * std, 'Wo': jax.random.normal(ks[4], (D, H * DH), dtype=jnp.float32) * std}
    _L1_attn_in = _L1_attn_setup()

    def _L1_ffn_setup():
        import jax, jax.numpy as jnp
        import numpy as np
        DIM = 256

        def _reference_tuple_inner(x, W_r, W_k, W_v, mu_r, mu_k):
            B, T, C = x.shape
            x_prev = jnp.concatenate([jnp.zeros((B, 1, C), x.dtype), x[:, :-1, :]], axis=1)
            xr = mu_r * x + (1.0 - mu_r) * x_prev
            xk = mu_k * x + (1.0 - mu_k) * x_prev
            r = jax.nn.sigmoid(jnp.einsum('btc,dc->btd', xr, W_r))
            k = jnp.einsum('btc,dc->btd', xk, W_k)
            k_act = jnp.square(jax.nn.relu(k))
            out = r * jnp.einsum('btc,dc->btd', k_act, W_v)
            new_state = x[:, -1, :]
            return (out, new_state)
        key = jax.random.key(seed)
        ks = jax.random.split(key, 6)
        B, T, C = (8, 512, DIM)
        x = jax.random.normal(ks[0], (B, T, C), dtype=jnp.float32)
        s = 1.0 / np.sqrt(C)
        W_r = jax.random.uniform(ks[1], (C, C), jnp.float32, -s, s)
        W_k = jax.random.uniform(ks[2], (C, C), jnp.float32, -s, s)
        W_v = jax.random.uniform(ks[3], (C, C), jnp.float32, -s, s)
        mu_r = jax.random.uniform(ks[4], (C,), jnp.float32)
        mu_k = jax.random.uniform(ks[5], (C,), jnp.float32)
        return {'x': x, 'W_r': W_r, 'W_k': W_k, 'W_v': W_v, 'mu_r': mu_r, 'mu_k': mu_k}
    _L1_ffn_in = _L1_ffn_setup()
    _d = {'L0_attn_x': _L0_attn_in['x'], 'L0_attn_Wq': _L0_attn_in['Wq'], 'L0_attn_bq': _L0_attn_in['bq'], 'L0_attn_Wk': _L0_attn_in['Wk'], 'L0_attn_bk': _L0_attn_in['bk'], 'L0_attn_Wv': _L0_attn_in['Wv'], 'L0_attn_bv': _L0_attn_in['bv'], 'L0_attn_Wo': _L0_attn_in['Wo'], 'L0_attn_bo': _L0_attn_in['bo'], 'L0_ffn_w_gate': _L0_ffn_in['w_gate'], 'L0_ffn_w_up': _L0_ffn_in['w_up'], 'L0_ffn_w_down': _L0_ffn_in['w_down'], 'L1_attn_Wq': _L1_attn_in['Wq'], 'L1_attn_Wk': _L1_attn_in['Wk'], 'L1_attn_Wv': _L1_attn_in['Wv'], 'L1_attn_Wo': _L1_attn_in['Wo'], 'L1_ffn_W_r': _L1_ffn_in['W_r'], 'L1_ffn_W_k': _L1_ffn_in['W_k'], 'L1_ffn_W_v': _L1_ffn_in['W_v'], 'L1_ffn_mu_r': _L1_ffn_in['mu_r'], 'L1_ffn_mu_k': _L1_ffn_in['mu_k']}
    _x0 = _d['L0_attn_x']
    _d['L0_attn_x'] = jax.random.normal(jax.random.fold_in(jax.random.key(seed), 1), (8, 512, 256), dtype=_x0.dtype)
    del _x0
    return _d

def reference(L0_attn_x, L0_attn_Wq, L0_attn_bq, L0_attn_Wk, L0_attn_bk, L0_attn_Wv, L0_attn_bv, L0_attn_Wo, L0_attn_bo, L0_ffn_w_gate, L0_ffn_w_up, L0_ffn_w_down, L1_attn_Wq, L1_attn_Wk, L1_attn_Wv, L1_attn_Wo, L1_ffn_W_r, L1_ffn_W_k, L1_ffn_W_v, L1_ffn_mu_r, L1_ffn_mu_k):

    def _L0_attn_ref(x, Wq, bq, Wk, bk, Wv, bv, Wo, bo):
        import jax, jax.numpy as jnp
        import numpy as np
        import math
        B, T, D, H = (4, 512, 256, 16)
        HD = D // H
        ROPE_BASE = 10000.0

        def apply_rope(x):
            t, hd = (x.shape[2], x.shape[3])
            half = hd // 2
            theta = 1.0 / ROPE_BASE ** (jnp.arange(0, hd, 2, dtype=jnp.float32) / hd)
            pos = jnp.arange(1, t + 1, dtype=jnp.float32)
            ang = pos[:, None] * theta[None, :]
            ang = jnp.concatenate([ang, ang], axis=-1)
            sin, cos = (jnp.sin(ang), jnp.cos(ang))
            rot = jnp.concatenate([-x[..., half:], x[..., :half]], axis=-1)
            return x * cos[None, None, :, :] + rot * sin[None, None, :, :]
        b, t, d = x.shape
        h, hd = (H, HD)
        q = x @ Wq.T + bq
        k = x @ Wk.T + bk
        v = x @ Wv.T + bv
        split = lambda z: z.reshape(b, t, h, hd).transpose(0, 2, 1, 3)
        q, k, v = (split(q), split(k), split(v))
        q = apply_rope(q)
        k = apply_rope(k)
        scale = math.sqrt(hd)
        att = jnp.einsum('bhqd,bhkd->bhqk', q, k) / scale
        mask = jnp.tril(jnp.ones((t, t), dtype=bool))
        att = jnp.where(mask[None, None, :, :], att, -jnp.inf)
        att = jax.nn.softmax(att, axis=-1)
        y = jnp.einsum('bhqk,bhkd->bhqd', att, v)
        y = y.transpose(0, 2, 1, 3).reshape(b, t, d)
        y = y @ Wo.T + bo
        return y

    def _L0_ffn_ref(x, w_gate, w_up, w_down):
        import jax, jax.numpy as jnp
        import numpy as np
        DIM = 256
        HIDDEN = 768
        SCALE = 1.0 / 127.0

        def _dequant(w_int, dtype):
            return w_int.astype(dtype) * jnp.asarray(SCALE, dtype)
        wg = _dequant(w_gate, x.dtype)
        wu = _dequant(w_up, x.dtype)
        wd = _dequant(w_down, x.dtype)
        gate = jnp.einsum('bsd,hd->bsh', x, wg)
        up = jnp.einsum('bsd,hd->bsh', x, wu)
        h = jax.nn.silu(gate) * up
        return jnp.einsum('bsh,dh->bsd', h, wd)

    def _L1_attn_ref(x, Wq, Wk, Wv, Wo):
        import jax, jax.numpy as jnp
        import numpy as np
        B, N, D = (2, 512, 256)
        H, DH = (16, 64)
        SOFTCLAMP = 50.0
        SCALE = DH ** (-0.5)
        b, n, _ = x.shape
        q = jnp.einsum('bnd,fd->bnf', x, Wq).reshape(b, n, H, DH).transpose(0, 2, 1, 3)
        k = jnp.einsum('bnd,fd->bnf', x, Wk).reshape(b, n, H, DH).transpose(0, 2, 1, 3)
        v = jnp.einsum('bnd,fd->bnf', x, Wv).reshape(b, n, H, DH).transpose(0, 2, 1, 3)
        sim = jnp.einsum('bhid,bhjd->bhij', q, k) * SCALE
        sim = SOFTCLAMP * jnp.tanh(sim / SOFTCLAMP)
        causal = jnp.tril(jnp.ones((n, n), dtype=bool))
        sim = jnp.where(causal, sim, jnp.finfo(sim.dtype).min)
        attn = jax.nn.softmax(sim, axis=-1)
        out = jnp.einsum('bhij,bhjd->bhid', attn, v)
        out = out.transpose(0, 2, 1, 3).reshape(b, n, H * DH)
        return jnp.einsum('bnf,df->bnd', out, Wo)

    def _L1_ffn_ref(x, W_r, W_k, W_v, mu_r, mu_k):
        import jax, jax.numpy as jnp
        import numpy as np
        DIM = 256

        def _reference_tuple_inner(x, W_r, W_k, W_v, mu_r, mu_k):
            B, T, C = x.shape
            x_prev = jnp.concatenate([jnp.zeros((B, 1, C), x.dtype), x[:, :-1, :]], axis=1)
            xr = mu_r * x + (1.0 - mu_r) * x_prev
            xk = mu_k * x + (1.0 - mu_k) * x_prev
            r = jax.nn.sigmoid(jnp.einsum('btc,dc->btd', xr, W_r))
            k = jnp.einsum('btc,dc->btd', xk, W_k)
            k_act = jnp.square(jax.nn.relu(k))
            out = r * jnp.einsum('btc,dc->btd', k_act, W_v)
            new_state = x[:, -1, :]
            return (out, new_state)
        return _reference_tuple_inner(x, W_r, W_k, W_v, mu_r, mu_k)[0]
    x = L0_attn_x
    x = x + _layernorm(_L0_attn_ref(_layernorm(x, axis=-1), L0_attn_Wq, L0_attn_bq, L0_attn_Wk, L0_attn_bk, L0_attn_Wv, L0_attn_bv, L0_attn_Wo, L0_attn_bo), axis=-1)
    x = x + _layernorm(_L0_ffn_ref(_layernorm(x, axis=-1), L0_ffn_w_gate, L0_ffn_w_up, L0_ffn_w_down), axis=-1)
    x = x + _layernorm(_L1_attn_ref(_layernorm(x, axis=-1), L1_attn_Wq, L1_attn_Wk, L1_attn_Wv, L1_attn_Wo), axis=-1)
    x = x + _layernorm(_L1_ffn_ref(_layernorm(x, axis=-1), L1_ffn_W_r, L1_ffn_W_k, L1_ffn_W_v, L1_ffn_mu_r, L1_ffn_mu_k), axis=-1)
    return x

_drawn_inputs = setup_inputs


def setup_inputs(seed=0):
    import zlib

    import numpy as np

    out = dict(_drawn_inputs(seed))
    spreads = {}
    factors = {'L0_attn_bq': 6.671, 'L0_attn_bk': 8.0}
    for name, (base, spread) in spreads.items():
        noise = np.random.default_rng([zlib.crc32(name.encode()), seed]).standard_normal(out[name].shape)
        drawn = base * np.exp(spread * noise) if base else spread * noise
        out[name] = jnp.asarray(drawn.astype(out[name].dtype))
    for name, factor in factors.items():
        out[name] = (out[name] * factor).astype(out[name].dtype)
    return out
```

```python
import numpy as np
import concourse.bass as bass
from concourse import mybir
from contextlib import ExitStack

F32 = mybir.dt.float32
F32R = mybir.dt.float32r
I32 = mybir.dt.int32
BF16 = mybir.dt.bfloat16
ALU = mybir.AluOpType
ACT = mybir.ActivationFunctionType

BATCH, T, D = 8, 512, 256
P = 128
NT = T // P
NC = D // P
EPS = 1e-5
BANK = 512

H0, HD0 = 16, 16
ROW0 = 64
KMAX = 3 * HD0
HID = 768
NM = HID // P
WSCALE = 1.0 / 127.0

H1, HD1 = 16, 64
F1 = H1 * HD1
NP1 = H1 // 2
CLAMP = 50.0

PAIRS = 8
PSLOTS = 4
UNITS = 5
MASKED = -1.0e30


class Signal:

    def __init__(self, sem, per, before=0):
        self.sem, self.per, self.before = sem, per, before

    def at(self, i, n):
        return i * self.per + n + self.before


class Ring:

    def __init__(self, banks, full, free):
        self.banks, self.full, self.free = banks, full, free
        free.before = len(banks)

    def bank(self, n):
        return self.banks[n % len(self.banks)]

    def claim(self, i, n):
        return self.free.at(i, n - len(self.banks) + 1)

    def arrived(self, i, n):
        return self.full.at(i, n + 1)


def unit_cols(e, kt):
    if kt == 0:
        return 2 * e, 0, 512
    if kt == 1:
        return 2 * e + 1, 0, 384
    if kt == 3:
        return 2 * e + 1, 384, 512
    return 4, 256 * e, 256 * e + 256


def split_terms(hi, lo, whi, wlo):
    return ((hi, whi), (lo, whi), (hi, wlo))


def uses(names):
    return {name: n for n, name in enumerate(names)}


def hold(nc, holder, ones):
    nc.gpsimd.tensor_tensor(holder, ones[:, 0:1], ones[:, 1:2], ALU.mult)


def mask_pair(pool, nc, probs, done):
    for part in (probs[:, :, 0:P], probs[:, 1:4:2, 384:512], probs[:, 4:5, 256:384]):
        n = part.shape[1]
        nc.gpsimd.affine_select(out=part, in_=part, compare_op=ALU.is_ge, fill=0.0, base=0,
                                pattern=[[0, n], [1, P]], channel_multiplier=-1).then_inc(done.sem, 1)


def program(nc, a):
    x_mid = nc.dram_tensor("x_mid", (BATCH, T, D), F32, kind="Internal").ap()
    tok = lambda ap, i: ap[i].rearrange("(t p) d -> p t d", p=P)
    with ExitStack() as ctx:
        psum = ctx.enter_context(nc.psum_tensor("psum", [P, 8, BANK], F32))
        banks = [psum[:, b, :] for b in range(8)]
        ident = ctx.enter_context(nc.sbuf_tensor("ident", [P, P], F32))
        expo = ctx.enter_context(nc.sbuf_tensor("expo", [P, NT], F32))
        for phase in (phase1, phase2):
            with ExitStack() as inner:
                phase(nc, inner, a, x_mid, tok, banks, ident, expo)


def load_split(nc, sp, act, dve, plan, staging, sems):
    loaded, hi_done, lo_done = sems
    slots = len(staging)
    if sp is not None:
        for n, (src, hi, lo, integer) in enumerate(plan):
            if n >= slots:
                sp.wait_ge(lo_done, n - slots + 1)
            dst = staging[n % slots][:, :src.shape[1]]
            sp.dma_start(dst.bitcast(I32) if integer else dst, src).then_inc(loaded[n % slots], 16)
    for eng in (act, dve):
        if eng is None:
            continue
        for n, (src, hi, lo, integer) in enumerate(plan):
            raw = staging[n % slots][:, :src.shape[1]]
            raw = raw.bitcast(I32) if integer else raw
            eng.wait_ge(loaded[n % slots], 16 * (n // slots + 1))
            if act is not None:
                nc.scalar.activation(hi, raw, ACT.Copy).then_inc(hi_done, 1)
            else:
                eng.wait_ge(hi_done, n + 1)
                nc.vector.tensor_tensor(lo, raw, hi.bitcast(F32), ALU.subtract).then_inc(lo_done, 1)


class Norm:

    def __init__(self, nc, sb, sig, expo, count):
        self.nc, self.expo = nc, expo
        self.stats = sb("stats", [P, NT, 6])
        self.mv = sb("mv", [P, NT, 2])
        self.veps = sb("veps", [P, NT])
        self.rstd = sb("rstd", [P, NT])
        self.holder = sb("holder", [P, 1])
        self.stats_ready = sig("stats_ready", count * NT)
        self.mv_ready = sig("mv_ready", count * NT)
        self.var_ready = sig("var_ready", count)
        self.rstd_ready = sig("rstd_ready", count)

    def vector(self, dve, i, n, src, eps, before=None):
        nc = self.nc
        for t in range(NT):
            if before:
                before(t)
            nc.vector.bn_stats(self.stats[:, t, :], src(t)).then_inc(self.stats_ready.sem, 1)
        dve.wait_ge(self.stats_ready.sem, self.stats_ready.at(i, (n + 1) * NT))
        nc.vector.memset(self.holder[:], 0.0)
        for t in range(NT):
            nc.vector.bn_aggr(self.mv[:, t, :], self.stats[:, t, :]).then_inc(self.mv_ready.sem, 1)
        dve.wait_ge(self.mv_ready.sem, self.mv_ready.at(i, (n + 1) * NT))
        nc.vector.tensor_scalar(self.veps[:], self.mv[:, :, 1], eps, None,
                                ALU.add).then_inc(self.var_ready.sem, 1)
        dve.wait_ge(self.rstd_ready.sem, self.rstd_ready.at(i, n + 1))

    def apply(self, out, src, t):
        return self.nc.vector.tensor_scalar(out, src, self.mv[:, t, 0:1], self.rstd[:, t:t + 1],
                                            ALU.subtract, ALU.mult)

    def gpsimd(self, pool, i, n):
        pool.wait_ge(self.var_ready.sem, self.var_ready.at(i, n + 1))
        self.nc.gpsimd.tensor_tensor(self.rstd[:], self.veps[:], self.expo[:],
                                     ALU.pow).then_inc(self.rstd_ready.sem, 1)


def phase1(nc, ctx, a, x_mid, tok, banks, ident, expo):
    def sb(name, shape, dt=F32):
        return ctx.enter_context(nc.sbuf_tensor("l0_" + name, shape, dt))

    def sem(name):
        return ctx.enter_context(nc.semaphore("l0_" + name))

    def sig(name, per):
        return Signal(sem(name), per)

    wqkv = [sb("wqkv" + s, [P, NC, 3 * D], F32R) for s in ("_hi", "_lo")]
    wo = [sb("wo" + s, [P, NC, D], F32R) for s in ("_hi", "_lo")]
    wgu = [sb("wgu" + s, [P, NC, 2 * HID], F32R) for s in ("_hi", "_lo")]
    wd = [sb("wd" + s, [P, NM, D], F32R) for s in ("_hi", "_lo")]
    b_qkv = sb("b_qkv", [P, 3 * D])
    b_o = sb("b_o", [P, D])
    cos = sb("cos", [P, NT, HD0])
    sin = sb("sin", [P, NT, HD0])
    causal = sb("causal", [P, P], BF16)
    identb = sb("identb", [P, P], BF16)
    xin = sb("xin", [P, NT, D])
    xn = sb("xn", [P, NT, D])
    xT = [sb("xT" + s, [P, NC, T], F32R) for s in ("_hi", "_lo")]
    qkb = sb("qkb", [P, 2, 2 * D])
    rot = sb("rot", [P, 2 * D])
    rop = sb("rop", [P, 2 * D])
    stackq = sb("stackq", [P, H0 * ROW0])
    stackk = sb("stackk", [P, H0 * ROW0])
    qT = sb("qT", [P, PAIRS, T], F32R)
    kT = sb("kT", [P, PAIRS, T], F32R)
    v0 = sb("v0", [P, NT, H0, 32])
    rowmax = sb("rowmax", [P, NT, H0])
    maxT = sb("maxT", [4, 2, T], F32R)
    outT = sb("outT", [P, T])
    rden = sb("rden", [P, NT, 4])
    att = sb("att", [P, NT, D])
    x1 = sb("x1", [P, NT, D])
    x2 = sb("x2", [P, NT, D])
    th = sb("th", [P, 2, T])
    gated = sb("gated", [P, 2, T])
    hid = sb("hid", [P, 2, T])
    pool_holder = sb("pool_holder", [P, PAIRS])
    dve_holder = sb("dve_holder", [P, len(banks)])
    act_holder = sb("act_holder", [P, len(banks)])
    with nc.sbuf_tensor("l0_probs", [P, PSLOTS, UNITS, BANK], F32) as probs:
        pass
    hT = [sb("hT" + s, [P, NM, T], F32R) for s in ("_hi", "_lo")]
    sb("hT_rest", [P, PSLOTS * UNITS * BANK - 2 * NM * T])
    staging = [probs[:, s // 2, :, :].rearrange("p a b -> p (a b)")[:, 1280 * (s % 2):1280 * (s % 2) + 768]
               for s in range(8)]

    d_names = [(k, t) for t in range(NT) for k in ("qk", "v")]
    s_names = [("stack", t, k, half) for t in range(NT) for k in ("q", "k") for half in range(2)]
    for step in range(6):
        if step >= 2:
            d_names.append(("pv", step - 2))
        for j in range(4):
            if step < 4:
                d_names += [("max", 4 * step + j, t) for t in range(NT)]
            if j == 0 and 1 <= step < 5:
                s_names.append(("maxT", step - 1))
            if j == 1 and step >= 2:
                d_names.append(("outT", step - 2))
            if j >= 2 and 1 <= step < 5:
                s_names += [("score", 2 * (step - 1) + j - 2, u) for u in range(UNITS)]
    d_names += [("o", 0), ("o", 1)]
    for m in range(NM):
        d_names += [("gate", m), ("up", m)]
    d_names += [("down", 0), ("down", 1)]
    du, su = uses(d_names), uses(s_names)
    tu = uses([(k, c) for k in ("x", "att", "x1") for c in range(NC)])
    assert len(du) % 3 == 0 and len(su) % 3 == 0

    ring_t = Ring(banks[0:2], sig("transposed", len(tu)), sig("split_done", len(tu)))
    ring_d = Ring(banks[2:5], sig("d_full", len(du)), sig("d_free", len(du)))
    ring_s = Ring(banks[5:8], sig("s_full", len(su)), sig("s_free", len(su)))
    hi_done = sig("hi_done", len(tu))
    x_loaded = sig("x_loaded", 16)
    x_stored = sig("x_stored", 16)
    xn_ready = sig("xn_ready", 2 * NT)
    x1_ready = sig("x1_ready", 1)
    x2_ready = sig("x2_ready", 1)
    rot_ready = sig("rot_ready", 2 * NT)
    rop_ready = sig("rop_ready", NT)
    stack_hi = sig("stack_hi", 2 * NT)
    stack_ready = sig("stack_ready", 2 * NT)
    max_ready = sig("max_ready", H0 * NT)
    max_placed = sig("max_placed", 64 * 4)
    masked = sig("masked", 3 * PAIRS)
    outT_ready = sig("outT_ready", 4)
    th_ready = sig("th_ready", NM)
    hid_hi = sig("hid_hi", NM)
    hid_split = sig("hid_split", NM)
    rope_cos = sig("rope_cos", NT)
    rden_ready = sig("rden_ready", 4)
    normed = sig("normed", NT + NT // 2)

    w_loaded = [sem(f"w_loaded{n}") for n in range(8)]
    w_sems = (w_loaded, sem("w_hi"), sem("w_lo"))
    c_loaded = sem("c_loaded")
    consts = sem("consts")
    norm = Norm(nc, sb, sig, expo, 4)
    plan = []
    for c in range(NC):
        plan.append((a["wqkv"][c * P:(c + 1) * P, :], wqkv[0][:, c, :], wqkv[1][:, c, :], False))
    for c in range(NC):
        plan.append((a["wo"][c * P:(c + 1) * P, :], wo[0][:, c, :], wo[1][:, c, :], False))
    for c in range(NC):
        for g in range(2):
            cols = slice(g * HID, (g + 1) * HID)
            plan.append((a["wgu"][c * P:(c + 1) * P, cols], wgu[0][:, c, cols], wgu[1][:, c, cols], True))
    for m in range(NM):
        plan.append((a["wd"][m * P:(m + 1) * P, :], wd[0][:, m, :], wd[1][:, m, :], True))

    block = ctx.enter_context(nc.Block())

    @block.sync
    def _(sp):
        sp.dma_start(xin[:], tok(a["x"], 0)).then_inc(x_loaded.sem, 16)
        load_split(nc, sp, None, None, plan, staging, w_sems)

        def maxima(i):
            for g in range(4):
                sp.wait_ge(ring_s.free.sem, ring_s.free.at(i, su["maxT", g] + 1))
                for j in range(4):
                    row = ROW0 * (j % 2) + KMAX
                    sp.dma_start(qT[row:row + 1, 2 * g + j // 2, :].bitcast(F32),
                                 maxT[j:j + 1, g % 2, :].bitcast(F32)).then_inc(max_placed.sem, 16)

        def body(i, last=False):
            maxima(i)
            sp.wait_ge(x1_ready.sem, x1_ready.at(i, 1))
            if not last:
                sp.dma_start(xin[:], tok(a["x"], i + 1)).then_inc(x_loaded.sem, 16)
            sp.wait_ge(x2_ready.sem, x2_ready.at(i, 1))
            sp.dma_start(tok(x_mid, i), x2[:]).then_inc(x_stored.sem, 16)

        with sp.Fori(0, BATCH - 1) as i:
            body(i)
        body(BATCH - 1, last=True)
        sp.wait_ge(x_stored.sem, x_stored.at(BATCH, 0))

    @block.gpsimd
    def _(pool):
        nc.gpsimd.memset(ident[:], 0.0).then_inc(consts, 1)
        nc.gpsimd.memset(causal[:], 0.0).then_inc(consts, 1)
        nc.gpsimd.memset(identb[:], 0.0).then_inc(consts, 1)
        nc.gpsimd.memset(expo[:], -0.5).then_inc(consts, 1)
        nc.gpsimd.memset(v0[:], 1.0).then_inc(consts, 1)
        nc.gpsimd.memset(stackq[:], 0.0).then_inc(consts, 1)
        nc.gpsimd.memset(stackk[:], 0.0).then_inc(consts, 1)
        pool.wait_ge(consts, 7)
        for eye in (ident, identb):
            nc.gpsimd.affine_select(out=eye[:], in_=eye[:], compare_op=ALU.not_equal, fill=1.0, base=0,
                                    pattern=[[-1, P]], channel_multiplier=1).then_inc(consts, 1)
        nc.gpsimd.affine_select(out=causal[:], in_=causal[:], compare_op=ALU.is_ge, fill=MASKED, base=0,
                                pattern=[[-1, P]], channel_multiplier=1).then_inc(consts, 1)
        ones = stackk[:].rearrange("p (h r) -> p h r", r=ROW0)[:, :, KMAX:KMAX + 1]
        nc.gpsimd.memset(ones, 1.0).then_inc(consts, 1)
        pool.wait_ge(c_loaded, 64)

        def body(i):
            norm.gpsimd(pool, i, 0)
            for t in range(NT):
                pool.wait_ge(ring_d.free.sem, ring_d.free.at(i, du["qk", t] + 1))
                if t:
                    pool.wait_ge(rop_ready.sem, rop_ready.at(i, t))
                x = qkb[:, t % 2, :].rearrange("p (h e r) -> p h e r", e=2, r=HD0 // 2)
                r = rot[:].rearrange("p (h e r) -> p h e r", e=2, r=HD0 // 2)
                for e in range(2):
                    s = sin[:, t, 8 * e:8 * e + 8].unsqueeze(1).broadcast_to([P, 2 * H0, 8])
                    nc.gpsimd.tensor_tensor(r[:, :, e, :], x[:, :, 1 - e, :], s,
                                            ALU.mult).then_inc(rot_ready.sem, 1)
                pool.wait_ge(stack_hi.sem, stack_hi.at(i, 2 * t + 2))
                for k, (stack, lo) in enumerate(((stackq, 1), (stackk, 2))):
                    st = stack[:].rearrange("p (h r) -> p h r", r=ROW0)
                    full = rop[:, k * D:(k + 1) * D].rearrange("p (h r) -> p h r", r=HD0)
                    nc.gpsimd.tensor_tensor(st[:, :, lo * HD0:(lo + 1) * HD0].bitcast(F32R), full,
                                            st[:, :, 0:HD0], ALU.subtract).then_inc(stack_ready.sem, 1)
            for p in range(PAIRS):
                pool.wait_ge(ring_s.free.sem, ring_s.free.at(i, su["score", p, UNITS - 1] + 1))
                hold(nc, pool_holder[:, p:p + 1], expo)
                mask_pair(pool, nc, probs[:, p % PSLOTS, :, :], masked)
            norm.gpsimd(pool, i, 1)
            norm.gpsimd(pool, i, 2)
            for m in range(NM):
                pool.wait_ge(hid_hi.sem, hid_hi.at(i, m + 1))
                nc.gpsimd.tensor_tensor(hT[1][:, m, :], hid[:, m % 2, :], hT[0][:, m, :].bitcast(F32),
                                        ALU.subtract).then_inc(hid_split.sem, 1)
            norm.gpsimd(pool, i, 3)

        with pool.Fori(0, BATCH) as i:
            body(i)

    @block.scalar
    def _(act):
        act.dma_start(b_qkv[:], a["b_qkv"].partition_broadcast(P)).then_inc(c_loaded, 16)
        act.dma_start(b_o[:], a["b_o"].partition_broadcast(P)).then_inc(c_loaded, 16)
        act.dma_start(cos[:], a["cos"].rearrange("(t p) r -> p t r", p=P)).then_inc(c_loaded, 16)
        act.dma_start(sin[:], a["sin"].rearrange("(t p) r -> p t r", p=P)).then_inc(c_loaded, 16)
        load_split(nc, None, act, None, plan, staging, w_sems)

        act.wait_ge(consts, 11)
        for b in range(len(ring_s.banks)):
            nc.scalar.activation(act_holder[:, b:b + 1], expo[:, 0:1], ACT.Copy).then_inc(ring_s.free.sem, 1)

        def high(i, kind):
            for c in range(NC):
                n = tu[kind, c]
                act.wait_ge(ring_t.full.sem, ring_t.arrived(i, n))
                nc.scalar.activation(xT[0][:, c, :], ring_t.bank(n), ACT.Copy).then_inc(hi_done.sem, 1)

        def body(i):
            high(i, "x")
            for t in range(NT):
                act.wait_ge(rop_ready.sem, rop_ready.at(i, t + 1))
                if t:
                    act.wait_ge(ring_s.full.sem, ring_s.arrived(i, su["stack", t - 1, "k", 1]))
                for k, (stack, step) in enumerate(((stackq, 2), (stackk, 1))):
                    st = stack[:].rearrange("p (h s r) -> p h s r", s=ROW0 // HD0, r=HD0)
                    full = rop[:, k * D:(k + 1) * D].rearrange("p (h r) -> p h r", r=HD0)
                    nc.scalar.activation(st[:, :, 0:step + 1:step, :].bitcast(F32R),
                                         full.unsqueeze(2).broadcast_to([P, H0, 2, HD0]),
                                         ACT.Copy).then_inc(stack_hi.sem, 1)
                for k, dst in (("q", qT), ("k", kT)):
                    for half in range(2):
                        n = su["stack", t, k, half]
                        act.wait_ge(ring_s.full.sem, ring_s.arrived(i, n))
                        nc.scalar.activation(dst[:, 4 * half:4 * half + 4, t * P:(t + 1) * P],
                                             ring_s.bank(n).rearrange("p (a b) -> p a b", b=P),
                                             ACT.Copy).then_inc(ring_s.free.sem, 1)
            for step in range(1, 5):
                g = step - 1
                n = su["maxT", g]
                act.wait_ge(ring_s.full.sem, ring_s.arrived(i, n))
                nc.scalar.activation(maxT[:, g % 2, :], ring_s.bank(n)[0:4, :], ACT.Copy,
                                     scale=-1.0).then_inc(ring_s.free.sem, 1)
                for p in (2 * g, 2 * g + 1):
                    if p >= PSLOTS:
                        act.wait_ge(ring_d.full.sem, ring_d.full.at(i, du["pv", p // 2 - 2] + 1))
                    for u in range(UNITS):
                        n = su["score", p, u]
                        act.wait_ge(ring_s.full.sem, ring_s.arrived(i, n))
                        nc.scalar.activation(probs[:, p % PSLOTS, u, :], ring_s.bank(n), ACT.Exp,
                                             scale=HD0 ** -0.5).then_inc(ring_s.free.sem, 1)
            high(i, "att")
            high(i, "x1")

            def hidden_high(m):
                act.wait_ge(ring_d.free.sem, ring_d.free.at(i, du["up", m] + 1))
                nc.scalar.activation(hT[0][:, m, :], hid[:, m % 2, :], ACT.Copy).then_inc(hid_hi.sem, 1)

            for m in range(NM):
                n = du["gate", m]
                act.wait_ge(ring_d.full.sem, ring_d.arrived(i, n))
                if m >= 2:
                    act.wait_ge(ring_d.free.sem, ring_d.free.at(i, du["gate", m - 2] + 1))
                nc.scalar.activation(th[:, m % 2, :], ring_d.bank(n), ACT.Tanh,
                                     scale=0.5 * WSCALE).then_inc(th_ready.sem, 1)
                if m >= 1:
                    hidden_high(m - 1)
            hidden_high(NM - 1)

        with act.Fori(0, BATCH) as i:
            body(i)

    @block.vector
    def _(dve):
        load_split(nc, None, None, dve, plan, staging, w_sems)
        dve.wait_ge(c_loaded, 64)
        dve.wait_ge(consts, 11)

        for b in range(len(ring_t.banks)):
            nc.vector.memset(dve_holder[:, b:b + 1], 0.0).then_inc(ring_t.free.sem, 1)
        for b in range(len(ring_d.banks)):
            nc.vector.memset(dve_holder[:, len(ring_t.banks) + b:len(ring_t.banks) + b + 1], 0.0).then_inc(ring_d.free.sem, 1)

        def low(i, kind):
            for c in range(NC):
                n = tu[kind, c]
                dve.wait_ge(hi_done.sem, hi_done.at(i, n + 1))
                nc.vector.tensor_tensor(xT[1][:, c, :], ring_t.bank(n), xT[0][:, c, :].bitcast(F32),
                                        ALU.subtract).then_inc(ring_t.free.sem, 1)

        def body(i, first=False):
            dve.wait_ge(x_loaded.sem, x_loaded.at(i, 16))
            norm.vector(dve, i, 0, lambda t: xin[:, t, :], EPS)
            for t in range(NT):
                norm.apply(xn[:, t, :], xin[:, t, :], t).then_inc(xn_ready.sem, 1)
            low(i, "x")
            for t in range(NT):
                n = du["qk", t]
                dve.wait_ge(ring_d.full.sem, ring_d.arrived(i, n))
                if t >= 2:
                    dve.wait_ge(rot_ready.sem, rot_ready.at(i, 2 * (t - 1)))
                nc.vector.tensor_tensor(qkb[:, t % 2, :], ring_d.bank(n), b_qkv[:, 0:2 * D], ALU.add).then_inc(ring_d.free.sem, 1)
                n = du["v", t]
                dve.wait_ge(ring_d.full.sem, ring_d.arrived(i, n))
                nc.vector.tensor_tensor(
                    v0[:, t, :, 0:HD0], ring_d.bank(n)[:, 0:D].rearrange("p (h r) -> p h r", r=HD0),
                    b_qkv[:, 2 * D:3 * D].rearrange("p (h r) -> p h r", r=HD0), ALU.add).then_inc(ring_d.free.sem, 1)
                if t:
                    dve.wait_ge(stack_ready.sem, stack_ready.at(i, 2 * t))
                dve.wait_ge(ring_d.free.sem, ring_d.free.at(i, du["qk", t] + 1))
                c16 = cos[:, t, :].unsqueeze(1).broadcast_to([P, 2 * H0, HD0])
                nc.vector.tensor_tensor(rop[:].rearrange("p (h r) -> p h r", r=HD0),
                                                   qkb[:, t % 2, :].rearrange("p (h r) -> p h r", r=HD0),
                                                   c16, ALU.mult).then_inc(rope_cos.sem, 1)
                dve.wait_ge(rot_ready.sem, rot_ready.at(i, 2 * t + 2))
                dve.wait_ge(rope_cos.sem, rope_cos.at(i, t + 1))
                nc.vector.tensor_tensor(rop[:], rop[:], rot[:], ALU.add).then_inc(rop_ready.sem, 1)
            for step in range(6):
                if step >= 2:
                    g = step - 2
                    n = du["pv", g]
                    dve.wait_ge(ring_d.full.sem, ring_d.arrived(i, n))
                    nc.vector.tensor_copy(outT[:], ring_d.bank(n)).then_inc(ring_d.free.sem, 1)
                for j in range(4):
                    if step < 4:
                        for t in range(NT):
                            h = 4 * step + j
                            n = du["max", h, t]
                            cols = (t + 1) * P
                            dve.wait_ge(ring_d.full.sem, ring_d.arrived(i, n))
                            nc.vector.tensor_reduce(rowmax[:, t, h:h + 1], ring_d.bank(n)[:, 0:cols],
                                                         mybir.AxisListType.X, ALU.max).then_inc(ring_d.free.sem, 1)
                    if j == 1 and step >= 2:
                        n = du["outT", g]
                        dve.wait_ge(ring_d.full.sem, ring_d.arrived(i, n))
                        view = ring_d.bank(n).rearrange("p (t j r) -> p t j r", t=NT, r=32)
                        nc.vector.reciprocal(rden[:].unsqueeze(3), view[:, :, :, HD0:HD0 + 1]).then_inc(rden_ready.sem, 1)
                        dve.wait_ge(rden_ready.sem, rden_ready.at(i, g + 1))
                        dst = att[:, :, 64 * g:64 * g + 64].rearrange("p t (j r) -> p t j r", r=HD0)
                        nc.vector.tensor_tensor(dst, view[:, :, :, 0:HD0],
                                                     rden[:].unsqueeze(3).broadcast_to([P, NT, 4, HD0]), ALU.mult).then_inc(ring_d.free.sem, 1)
            low(i, "att")
            for b in range(2):
                n = du["o", b]
                dve.wait_ge(ring_d.full.sem, ring_d.arrived(i, n))
                nc.vector.tensor_tensor(xn[:, 2 * b:2 * b + 2, :],
                                             ring_d.bank(n).rearrange("p (t d) -> p t d", d=D),
                                             b_o[:].unsqueeze(1).broadcast_to([P, 2, D]), ALU.add).then_inc(ring_d.free.sem, 1)
            dve.wait_ge(ring_d.free.sem, ring_d.free.at(i, du["o", 1] + 1))
            norm.vector(dve, i, 1, lambda t: xn[:, t, :], EPS)
            for t in range(NT):
                norm.apply(xn[:, t, :], xn[:, t, :], t).then_inc(normed.sem, 1)
            dve.wait_ge(normed.sem, normed.at(i, NT))
            nc.vector.tensor_tensor(x1[:], xin[:], xn[:], ALU.add).then_inc(x1_ready.sem, 1)
            dve.wait_ge(x1_ready.sem, x1_ready.at(i, 1))
            norm.vector(dve, i, 2, lambda t: x1[:, t, :], EPS)
            for t in range(NT):
                norm.apply(xn[:, t, :], x1[:, t, :], t).then_inc(xn_ready.sem, 1)
            low(i, "x1")
            for m in range(NM):
                n = du["gate", m]
                dve.wait_ge(th_ready.sem, th_ready.at(i, m + 1))
                if m >= 2:
                    dve.wait_ge(ring_d.free.sem, ring_d.free.at(i, du["up", m - 2] + 1))
                nc.vector.scalar_tensor_tensor(out=gated[:, m % 2, :], in0=th[:, m % 2, :], scalar=1.0,
                                                    in1=ring_d.bank(n), op0=ALU.add, op1=ALU.mult).then_inc(ring_d.free.sem, 1)
                n = du["up", m]
                dve.wait_ge(ring_d.full.sem, ring_d.arrived(i, n))
                if m >= 2:
                    dve.wait_ge(hid_split.sem, hid_split.at(i, m - 1))
                dve.wait_ge(ring_d.free.sem, ring_d.free.at(i, du["gate", m] + 1))
                nc.vector.tensor_tensor(hid[:, m % 2, :], ring_d.bank(n), gated[:, m % 2, :], ALU.mult).then_inc(ring_d.free.sem, 1)
            unit = 2.0 / WSCALE ** 3
            half = lambda t: ring_d.bank(du["down", t // 2])[:, (t % 2) * D:(t % 2 + 1) * D]
            norm.vector(dve, i, 3, half, EPS * unit * unit,
                        lambda t: t % 2 or dve.wait_ge(ring_d.full.sem, ring_d.arrived(i, du["down", t // 2])))
            for t in range(NT):
                ins = norm.apply(xn[:, t, :], half(t), t)
                ins.then_inc(ring_d.free.sem, 1) if t % 2 else ins.then_inc(normed.sem, 1)
            dve.wait_ge(normed.sem, normed.at(i, NT + NT // 2))
            dve.wait_ge(ring_d.free.sem, ring_d.free.at(i, du["down", 1] + 1))
            if not first:
                dve.wait_ge(x_stored.sem, x_stored.at(i, 0))
            nc.vector.tensor_tensor(x2[:], x1[:], xn[:], ALU.add).then_inc(x2_ready.sem, 1)

        body(0, first=True)
        with dve.Fori(1, BATCH) as i:
            body(i)

    @block.tensor
    def _(pe):
        pe.wait_ge(consts, 11)
        pe.wait_ge(w_sems[2], len(plan))

        def transposes(i, kind, src, ready):
            for c in range(NC):
                n = tu[kind, c]
                pe.wait_ge(ring_t.free.sem, ring_t.claim(i, n))
                for t in range(NT):
                    ready(t)
                    last = nc.tensor.transpose(ring_t.bank(n)[:, t * P:(t + 1) * P], src[:, t, c * P:(c + 1) * P], ident[:])
                last.then_inc(ring_t.full.sem, 1)

        def product(out, terms, chunks):
            todo = [(l, r, c) for c in range(chunks) for l, r in terms]
            for k, (l, r, c) in enumerate(todo):
                last = nc.tensor.matmul(out, l(c), r(c), start=(k == 0), stop=(k == len(todo) - 1))
            return last

        def token_major(out, x, w, t, cols, chunks):
            return product(out, [(lambda c, p=p: p[:, c, t * P:(t + 1) * P], lambda c, q=q: q[:, c, cols])
                                 for p, q in split_terms(*x, *w)], chunks)

        def body(i):
            transposes(i, "x", xn, lambda t: pe.wait_ge(xn_ready.sem, xn_ready.at(i, t + 1)))
            pe.wait_ge(ring_t.free.sem, ring_t.free.at(i, NC))
            for t in range(NT):
                n = du["qk", t]
                pe.wait_ge(ring_d.free.sem, ring_d.claim(i, n))
                token_major(ring_d.bank(n), xT, wqkv, t, slice(0, 2 * D), NC).then_inc(ring_d.full.sem, 1)
                n = du["v", t]
                pe.wait_ge(ring_d.free.sem, ring_d.claim(i, n))
                token_major(ring_d.bank(n)[:, 0:D], xT, wqkv, t, slice(2 * D, 3 * D), NC).then_inc(ring_d.full.sem, 1)
            for t in range(NT):
                pe.wait_ge(stack_ready.sem, stack_ready.at(i, 2 * t + 2))
                for k, stack in (("q", stackq), ("k", stackk)):
                    for half in range(2):
                        n = su["stack", t, k, half]
                        pe.wait_ge(ring_s.free.sem, ring_s.claim(i, n))
                        for b in range(4):
                            p = 4 * half + b
                            last = nc.tensor.transpose(ring_s.bank(n)[:, b * P:(b + 1) * P],
                                                       stack[:, p * P:(p + 1) * P], ident[:])
                        last.then_inc(ring_s.full.sem, 1)
            pe.wait_ge(ring_s.free.sem, ring_s.free.at(i, su["stack", NT - 1, "k", 1] + 1))
            pe.wait_ge(ring_d.free.sem, ring_d.free.at(i, du["v", NT - 1] + 1))
            for step in range(6):
                if step >= 2:
                    g = step - 2
                    n = du["pv", g]
                    pe.wait_ge(ring_d.free.sem, ring_d.claim(i, n))
                    pe.wait_ge(masked.sem, masked.at(i, 3 * (2 * g + 2)))
                    for kt in range(NT):
                        for j in range(4):
                            h = 4 * g + j
                            u, c0, c1 = unit_cols(j // 2, kt)
                            last = nc.tensor.matmul(ring_d.bank(n)[32 * j:32 * j + 32, kt * P:T], v0[:, kt, h, :],
                                                    probs[:, (2 * g + j % 2) % PSLOTS, u, c0:c1], start=(kt == 0),
                                                    stop=(kt == NT - 1), tile_position=(0, 32 * j))
                    last.then_inc(ring_d.full.sem, 1)
                for j in range(4):
                    if step < 4:
                        h = 4 * step + j
                        rows = slice(ROW0 * (h % 2), ROW0 * (h % 2) + KMAX)
                        for t in range(NT):
                            n = du["max", h, t]
                            pe.wait_ge(ring_d.free.sem, ring_d.claim(i, n))
                            nc.tensor.matmul(ring_d.bank(n)[:, 0:(t + 1) * P], qT[rows, h // 2, t * P:(t + 1) * P],
                                             kT[rows, h // 2, 0:(t + 1) * P], start=True, stop=False)
                            nc.tensor.matmul(ring_d.bank(n)[:, t * P:(t + 1) * P], identb[:], causal[:],
                                                  start=False, stop=True).then_inc(ring_d.full.sem, 1)
                    if j == 0 and 1 <= step < 5:
                        g = step - 1
                        n = su["maxT", g]
                        pe.wait_ge(ring_s.free.sem, ring_s.claim(i, n))
                        pe.wait_ge(ring_d.free.sem, ring_d.free.at(i, du["max", 4 * g + 3, NT - 1] + 1))
                        for t in range(NT):
                            last = nc.tensor.transpose(ring_s.bank(n)[0:4, t * P:(t + 1) * P],
                                                       rowmax[:, t, 4 * g:4 * g + 4], ident[:])
                        last.then_inc(ring_s.full.sem, 1)
                    if j == 1 and step >= 2:
                        n = du["outT", step - 2]
                        pe.wait_ge(ring_d.free.sem, ring_d.claim(i, n))
                        pe.wait_ge(ring_d.free.sem, ring_d.free.at(i, du["pv", step - 2] + 1))
                        for t in range(NT):
                            last = nc.tensor.transpose(ring_d.bank(n)[:, t * P:(t + 1) * P],
                                                       outT[:, t * P:(t + 1) * P], ident[:])
                        last.then_inc(ring_d.full.sem, 1)
                    if j >= 2 and 1 <= step < 5:
                        p = 2 * (step - 1) + j - 2
                        pe.wait_ge(max_placed.sem, max_placed.at(i, 64 * step))
                        for u in range(UNITS):
                            n = su["score", p, u]
                            pe.wait_ge(ring_s.free.sem, ring_s.claim(i, n))
                            rows = slice(ROW0 * (p % 2), ROW0 * (p % 2) + KMAX + 1)
                            for e in range(2):
                                at = 2 * (p // 2) + e
                                for kt in range(NT):
                                    unit, c0, c1 = unit_cols(e, kt)
                                    if unit == u:
                                        last = nc.tensor.matmul(ring_s.bank(n)[:, c0:c1], kT[rows, at, kt * P:(kt + 1) * P],
                                                                qT[rows, at, kt * P:T], start=True, stop=True)
                            last.then_inc(ring_s.full.sem, 1)
            pe.wait_ge(ring_d.free.sem, ring_d.free.at(i, du["outT", 3] + 1))
            transposes(i, "att", att, lambda t: None)
            pe.wait_ge(ring_t.free.sem, ring_t.free.at(i, 2 * NC))
            for b in range(2):
                n = du["o", b]
                pe.wait_ge(ring_d.free.sem, ring_d.claim(i, n))
                for t in (2 * b, 2 * b + 1):
                    last = token_major(ring_d.bank(n)[:, (t % 2) * D:(t % 2 + 1) * D], xT, wo, t, slice(0, D), NC)
                last.then_inc(ring_d.full.sem, 1)
            transposes(i, "x1", xn, lambda t: pe.wait_ge(xn_ready.sem, xn_ready.at(i, NT + t + 1)))
            pe.wait_ge(ring_t.free.sem, ring_t.free.at(i, 3 * NC))
            for m in range(NM):
                for k in range(2):
                    n = du[("gate", "up")[k], m]
                    pe.wait_ge(ring_d.free.sem, ring_d.claim(i, n))
                    cols = slice(k * HID + m * P, k * HID + (m + 1) * P)
                    product(ring_d.bank(n), [(lambda c, q=q: q[:, c, cols], lambda c, p=p: p[:, c, :])
                                                  for p, q in split_terms(*xT, *wgu)], NC).then_inc(ring_d.full.sem, 1)
            pe.wait_ge(hid_split.sem, hid_split.at(i, NM))
            for b in range(2):
                n = du["down", b]
                pe.wait_ge(ring_d.free.sem, ring_d.claim(i, n))
                for t in (2 * b, 2 * b + 1):
                    last = token_major(ring_d.bank(n)[:, (t % 2) * D:(t % 2 + 1) * D], hT, wd, t, slice(0, D), NM)
                last.then_inc(ring_d.full.sem, 1)

        with pe.Fori(0, BATCH) as i:
            body(i)


def phase2(nc, ctx, a, x_mid, tok, banks, ident, expo):
    def sb(name, shape, dt=F32):
        return ctx.enter_context(nc.sbuf_tensor("l1_" + name, shape, dt))

    def sem(name):
        return ctx.enter_context(nc.semaphore("l1_" + name))

    def sig(name, per):
        return Signal(sem(name), per)

    wq = [sb("wq" + s, [P, NC, F1], F32R) for s in ("_hi", "_lo")]
    wk = [sb("wk" + s, [P, NC, F1], F32R) for s in ("_hi", "_lo")]
    wv = [sb("wv" + s, [P, NC, F1], F32R) for s in ("_hi", "_lo")]
    wo = [sb("wo" + s, [P, NP1, D], F32R) for s in ("_hi", "_lo")]
    wrkv = [sb("wrkv" + s, [P, NC, 3 * D], F32R) for s in ("_hi", "_lo")]
    mu = sb("mu", [P, 2, NC])
    xin = sb("xin", [P, NT, D])
    xn = sb("xn", [P, NT, D])
    xT = [sb("xT" + s, [P, NC, T], F32R) for s in ("_hi", "_lo")]
    qs = sb("qs", [P, 2, 2, T], F32R)
    ks = sb("ks", [P, 2, 2, T], F32R)
    kl = sb("kl", [P, 2, 2, T], F32R)
    v1 = sb("v1", [P, NT, H1, HD1 + 1])
    probs = sb("probs", [P, 2, UNITS, BANK])
    rden = sb("rden", [P, 2, NT])
    att = sb("att", [P, 2, NT, P])
    attT = [sb("attT" + s, [P, NP1, T], F32R) for s in ("_hi", "_lo")]
    x3 = sb("x3", [P, NT, D])
    x4 = sb("x4", [P, NT, D])
    xs = sb("xs", [P, NC, T + 1])
    dx = sb("dx", [P, NC, T])
    flat = [t[:].rearrange("p a b -> p (a b)") for t in attT]
    view = lambda t, n: t[:, n * NC * T:(n + 1) * NC * T].rearrange("p (c t) -> p c t", c=NC)
    mixr = [view(flat[0], 0), view(flat[0], 1)]
    mixk = [view(flat[0], 2), view(flat[0], 3)]
    mix = [probs[:, s, 0:NC, :] for s in range(2)]
    kact = [view(flat[1], 2), view(flat[1], 3)]
    sig_r = probs[:, 0, 2:4, :].rearrange("p a (t d) -> p (a t) d", d=D)
    relu = dx
    pool_holder = sb("pool_holder", [P, PAIRS])
    dve_holder = sb("dve_holder", [P, len(banks)])
    act_holder = sb("act_holder", [P, len(banks)])
    staging = [probs[:, s // 2, :, :].rearrange("p a b -> p (a b)")[:, 1280 * (s % 2):1280 * (s % 2) + 1024]
               for s in range(4)]

    d_names = [("v", t, b) for t in range(NT) for b in range(2)]
    s_names, t_names = [], [("x", 0), ("x", 1)]
    for step in range(NP1 + 3):
        if step < NP1:
            d_names += [("q", step), ("k", step)]
        if 1 <= step <= NP1:
            s_names += [("score", step - 1, u) for u in range(UNITS)]
        if 2 <= step <= NP1 + 1:
            d_names += [("pv", step - 2, e) for e in range(2)]
        if step >= 3:
            t_names.append(("att", step - 3))
    d_names += [("o", 0), ("o", 1)]
    t_names += [("x3", 0), ("x3", 1)]
    d_names += [("r", 0), ("r", 1), ("key", 0), ("key", 1), ("out", 0), ("out", 1)]
    du, su, tu = uses(d_names), uses(s_names), uses(t_names)
    assert len(du) % 3 == 0 and len(su) % 4 == 0

    ring_t = Ring(banks[0:1], sig("transposed", len(tu)), sig("split_done", len(tu)))
    ring_d = Ring(banks[1:4], sig("d_full", len(du)), sig("d_free", len(du)))
    ring_s = Ring(banks[4:8], sig("s_full", len(su)), sig("s_free", len(su)))
    hi_done = sig("hi_done", len(tu) - NC)
    x_loaded = sig("x_loaded", 16)
    x_stored = sig("x_stored", 16)
    xn_ready = sig("xn_ready", 2 * NT)
    x3_ready = sig("x3_ready", 1)
    x4_ready = sig("x4_ready", 1)
    proj_hi = sig("proj_hi", 4 * NP1)
    stack_ready = sig("stack_ready", 6 * NP1)
    exped = sig("exped", 2 * NP1)
    masked = sig("masked", 3 * NP1)
    mix_ready = sig("mix_ready", 4)
    mix_hi = sig("mix_hi", 4)
    mix_split = sig("mix_split", 4)
    gate_ready = sig("gate_ready", 2)
    sq_ready = sig("sq_ready", 2)
    kact_hi = sig("kact_hi", 2)
    kact_split = sig("kact_split", 2)
    rden_ready = sig("rden_ready", 2 * NP1)
    normed = sig("normed", NT // 2 + NT)
    dx_ready = sig("dx_ready", NC)
    w_loaded = [sem(f"w_loaded{n}") for n in range(4)]
    w_sems = (w_loaded, sem("w_hi"), sem("w_lo"))
    c_loaded = sem("c_loaded")
    consts = sem("consts")
    norm = Norm(nc, sb, sig, expo, 4)
    plan = []
    for name, dst in (("wq1", wq), ("wk1", wk), ("wv1", wv), ("wrkv", wrkv)):
        for c in range(NC):
            plan.append((a[name][c * P:(c + 1) * P, :], dst[0][:, c, :], dst[1][:, c, :], False))
    for c in range(NP1):
        plan.append((a["wo1"][c * P:(c + 1) * P, :], wo[0][:, c, :], wo[1][:, c, :], False))

    block = ctx.enter_context(nc.Block())

    @block.sync
    def _(sp):
        sp.dma_start(xin[:], tok(x_mid, 0)).then_inc(x_loaded.sem, 16)
        load_split(nc, sp, None, None, plan, staging, w_sems)

        def body(i, last=False):
            sp.wait_ge(x3_ready.sem, x3_ready.at(i, 1))
            if not last:
                sp.dma_start(xin[:], tok(x_mid, i + 1)).then_inc(x_loaded.sem, 16)
            sp.wait_ge(x4_ready.sem, x4_ready.at(i, 1))
            sp.dma_start(tok(a["out"], i), x4[:]).then_inc(x_stored.sem, 16)

        with sp.Fori(0, BATCH - 1) as i:
            body(i)
        body(BATCH - 1, last=True)
        sp.wait_ge(x_stored.sem, x_stored.at(BATCH, 0))

    @block.gpsimd
    def _(pool):
        nc.gpsimd.memset(v1[:, :, :, HD1:HD1 + 1], 1.0).then_inc(consts, 1)
        nc.gpsimd.memset(xs[:, :, 0:1], 0.0).then_inc(consts, 1)

        def body(i):
            norm.gpsimd(pool, i, 0)
            for p in range(NP1):
                pool.wait_ge(exped.sem, exped.at(i, 2 * p + 2))
                hold(nc, pool_holder[:, p:p + 1], expo)
                mask_pair(pool, nc, probs[:, p % 2, :, :], masked)
            norm.gpsimd(pool, i, 1)
            norm.gpsimd(pool, i, 2)
            norm.gpsimd(pool, i, 3)

        with pool.Fori(0, BATCH) as i:
            body(i)

    @block.scalar
    def _(act):
        act.dma_start(mu[:], a["mu"]).then_inc(c_loaded, 16)
        load_split(nc, None, act, None, plan, staging, w_sems)

        for b in range(len(ring_s.banks)):
            nc.scalar.activation(act_holder[:, b:b + 1], expo[:, 0:1], ACT.Copy).then_inc(ring_s.free.sem, 1)

        def body(i):
            for c in range(NC):
                n = tu["x", c]
                act.wait_ge(ring_t.full.sem, ring_t.arrived(i, n))
                nc.scalar.activation(xT[0][:, c, :], ring_t.bank(n), ACT.Copy).then_inc(hi_done.sem, 1)
            for step in range(NP1 + 3):
                if step < NP1:
                    p, slot = step, step % 2
                    for k, (name, dst) in enumerate((("q", qs), ("k", ks))):
                        n = du[name, p]
                        act.wait_ge(ring_d.full.sem, ring_d.arrived(i, n))
                        for e in range(2):
                            half = slice(64 * e, 64 * e + 64)
                            nc.scalar.activation(dst[half, slot, e, :], ring_d.bank(n)[half, :],
                                                 ACT.Copy).then_inc(proj_hi.sem, 1)
                if 1 <= step <= NP1:
                    p = step - 1
                    if p >= 2:
                        act.wait_ge(ring_d.full.sem, ring_d.arrived(i, du["pv", p - 2, 1]))
                    for u in range(UNITS):
                        n = su["score", p, u]
                        act.wait_ge(ring_s.full.sem, ring_s.arrived(i, n))
                        nc.scalar.activation(probs[:, p % 2, u, :], ring_s.bank(n), ACT.Tanh,
                                             scale=HD1 ** -0.5 / CLAMP).then_inc(ring_s.free.sem, 1)
                    act.wait_ge(ring_s.free.sem, ring_s.free.at(i, su["score", p, UNITS - 1] + 1))
                    for part in (probs[:, p % 2, 0:3, :], probs[:, p % 2, 3:5, :]):
                        nc.scalar.activation(part, part, ACT.Exp, scale=CLAMP).then_inc(exped.sem, 1)
                if step >= 3:
                    n = tu["att", step - 3]
                    act.wait_ge(ring_t.full.sem, ring_t.arrived(i, n))
                    nc.scalar.activation(attT[0][:, step - 3, :], ring_t.bank(n), ACT.Copy).then_inc(hi_done.sem, 1)
            for c in range(NC):
                for k, dst in enumerate((mixr, mixk)):
                    act.wait_ge(mix_ready.sem, mix_ready.at(i, 2 * c + k + 1))
                    nc.scalar.activation(dst[0][:, c, :], mix[k][:, c, :], ACT.Copy).then_inc(mix_hi.sem, 1)
            for b in range(2):
                half = sig_r[:, 2 * b:2 * b + 2, :]
                act.wait_ge(ring_d.free.sem, ring_d.free.at(i, du["r", b] + 1))
                nc.scalar.activation(half, half, ACT.Tanh, scale=0.5).then_inc(gate_ready.sem, 1)
            for c in range(NC):
                act.wait_ge(sq_ready.sem, sq_ready.at(i, c + 1))
                nc.scalar.activation(kact[0][:, c, :], relu[:, c, :], ACT.Copy).then_inc(kact_hi.sem, 1)

        with act.Fori(0, BATCH) as i:
            body(i)

    @block.vector
    def _(dve):
        load_split(nc, None, None, dve, plan, staging, w_sems)
        dve.wait_ge(c_loaded, 16)
        dve.wait_ge(consts, 2)

        for b in range(len(ring_t.banks)):
            nc.vector.memset(dve_holder[:, b:b + 1], 0.0).then_inc(ring_t.free.sem, 1)
        for b in range(len(ring_d.banks)):
            nc.vector.memset(dve_holder[:, len(ring_t.banks) + b:len(ring_t.banks) + b + 1], 0.0).then_inc(ring_d.free.sem, 1)

        def low(i, n, dst, hi):
            dve.wait_ge(hi_done.sem, hi_done.at(i, n + 1))
            nc.vector.tensor_tensor(dst, ring_t.bank(n), hi.bitcast(F32), ALU.subtract).then_inc(ring_t.free.sem, 1)

        def body(i, first=False):
            dve.wait_ge(x_loaded.sem, x_loaded.at(i, 16))
            norm.vector(dve, i, 0, lambda t: xin[:, t, :], EPS)
            for t in range(NT):
                norm.apply(xn[:, t, :], xin[:, t, :], t).then_inc(xn_ready.sem, 1)
            for c in range(NC):
                low(i, tu["x", c], xT[1][:, c, :], xT[0][:, c, :])
            for t in range(NT):
                for b in range(2):
                    n = du["v", t, b]
                    dve.wait_ge(ring_d.full.sem, ring_d.arrived(i, n))
                    nc.vector.tensor_copy(v1[:, t, 8 * b:8 * b + 8, 0:HD1],
                                               ring_d.bank(n).rearrange("p (h r) -> p h r", r=HD1)).then_inc(ring_d.free.sem, 1)
            for step in range(NP1 + 3):
                if step < NP1:
                    p, slot = step, step % 2
                    halves = [(slice(64 * e, 64 * e + 64), slice(64 - 64 * e, 128 - 64 * e)) for e in range(2)]
                    n = du["q", p]
                    dve.wait_ge(proj_hi.sem, proj_hi.at(i, 4 * p + 2))
                    for e, (half, other) in enumerate(halves):
                        nc.vector.tensor_tensor(qs[other, slot, e, :], ring_d.bank(n)[half, :], qs[half, slot, e, :].bitcast(F32),
                                                ALU.subtract).then_inc((stack_ready, ring_d.free)[e].sem, 1)
                    n = du["k", p]
                    dve.wait_ge(proj_hi.sem, proj_hi.at(i, 4 * p + 4))
                    for e, (half, other) in enumerate(halves):
                        nc.vector.tensor_copy(ks[other, slot, e, :],
                                              ks[half, slot, e, :].bitcast(F32)).then_inc(stack_ready.sem, 1)
                    for e, (half, other) in enumerate(halves):
                        nc.vector.tensor_tensor(kl[half, slot, e, :], ring_d.bank(n)[half, :], ks[half, slot, e, :].bitcast(F32),
                                                ALU.subtract).then_inc((stack_ready, ring_d.free)[e].sem, 1)
                    dve.wait_ge(ring_d.free.sem, ring_d.free.at(i, n + 1))
                    for e, (half, other) in enumerate(halves):
                        nc.vector.tensor_copy(kl[other, slot, e, :],
                                              kl[half, slot, e, :].bitcast(F32)).then_inc(stack_ready.sem, 1)
                if 2 <= step <= NP1 + 1:
                    p = step - 2
                    for e in range(2):
                        n = du["pv", p, e]
                        dve.wait_ge(ring_d.full.sem, ring_d.arrived(i, n))
                        bank = ring_d.bank(n)[:, 0:NT * (HD1 + 1)].rearrange("p (t r) -> p t r", t=NT)
                        nc.vector.reciprocal(rden[:, e, :].unsqueeze(2), bank[:, :, HD1:HD1 + 1]).then_inc(rden_ready.sem, 1)
                        dve.wait_ge(rden_ready.sem, rden_ready.at(i, 2 * p + e + 1))
                        nc.vector.tensor_tensor(att[:, p % 2, :, 64 * e:64 * e + 64], bank[:, :, 0:HD1],
                                                     rden[:, e, :].unsqueeze(2).broadcast_to([P, NT, HD1]), ALU.mult).then_inc(ring_d.free.sem, 1)
                if step >= 3:
                    low(i, tu["att", step - 3], attT[1][:, step - 3, :], attT[0][:, step - 3, :])
            post = lambda name: (lambda t: ring_d.bank(du[name, t // 2])[:, (t % 2) * D:(t % 2 + 1) * D])
            arrive = lambda name: (lambda t: t % 2 or dve.wait_ge(ring_d.full.sem, ring_d.arrived(i, du[name, t // 2])))
            norm.vector(dve, i, 1, post("o"), EPS, arrive("o"))
            for t in range(NT):
                ins = norm.apply(xn[:, t, :], post("o")(t), t)
                ins.then_inc(ring_d.free.sem, 1) if t % 2 else ins.then_inc(normed.sem, 1)
            dve.wait_ge(normed.sem, normed.at(i, NT // 2))
            dve.wait_ge(ring_d.free.sem, ring_d.free.at(i, du["o", 1] + 1))
            nc.vector.tensor_tensor(x3[:], xin[:], xn[:], ALU.add).then_inc(x3_ready.sem, 1)
            dve.wait_ge(x3_ready.sem, x3_ready.at(i, 1))
            norm.vector(dve, i, 2, lambda t: x3[:, t, :], EPS)
            for t in range(NT):
                norm.apply(xn[:, t, :], x3[:, t, :], t).then_inc(xn_ready.sem, 1)
            for c in range(NC):
                n = tu["x3", c]
                dve.wait_ge(ring_t.full.sem, ring_t.arrived(i, n))
                nc.vector.tensor_copy(xs[:, c, 1:T + 1], ring_t.bank(n)).then_inc(ring_t.free.sem, 1)
                dve.wait_ge(ring_t.free.sem, ring_t.free.at(i, n + 1))
                nc.vector.tensor_tensor(dx[:, c, :], xs[:, c, 1:T + 1], xs[:, c, 0:T], ALU.subtract).then_inc(dx_ready.sem, 1)
                dve.wait_ge(dx_ready.sem, dx_ready.at(i, c + 1))
                for k in range(2):
                    nc.vector.scalar_tensor_tensor(out=mix[k][:, c, :], in0=dx[:, c, :], scalar=mu[:, k, c:c + 1],
                                                   in1=xs[:, c, 0:T], op0=ALU.mult, op1=ALU.add).then_inc(mix_ready.sem, 1)
                for k, dst in enumerate((mixr, mixk)):
                    dve.wait_ge(mix_hi.sem, mix_hi.at(i, 2 * c + k + 1))
                    nc.vector.tensor_tensor(dst[1][:, c, :], mix[k][:, c, :], dst[0][:, c, :].bitcast(F32),
                                            ALU.subtract).then_inc(mix_split.sem, 1)
            for b in range(2):
                n = du["r", b]
                dve.wait_ge(ring_d.full.sem, ring_d.arrived(i, n))
                nc.vector.tensor_copy(sig_r[:, 2 * b:2 * b + 2, :].rearrange("p t d -> p (t d)"), ring_d.bank(n)).then_inc(ring_d.free.sem, 1)
            for c in range(NC):
                n = du["key", c]
                dve.wait_ge(ring_d.full.sem, ring_d.arrived(i, n))
                nc.vector.tensor_scalar(relu[:, c, :], ring_d.bank(n), 0.0, None, ALU.max).then_inc(ring_d.free.sem, 1)
                dve.wait_ge(ring_d.free.sem, ring_d.free.at(i, n + 1))
                nc.vector.tensor_tensor(relu[:, c, :], relu[:, c, :], relu[:, c, :], ALU.mult).then_inc(sq_ready.sem, 1)
            for c in range(NC):
                dve.wait_ge(kact_hi.sem, kact_hi.at(i, c + 1))
                nc.vector.tensor_tensor(kact[1][:, c, :], relu[:, c, :], kact[0][:, c, :].bitcast(F32),
                                        ALU.subtract).then_inc(kact_split.sem, 1)
            for b in range(2):
                n = du["out", b]
                dve.wait_ge(gate_ready.sem, gate_ready.at(i, b + 1))
                dve.wait_ge(ring_d.full.sem, ring_d.arrived(i, n))
                nc.vector.scalar_tensor_tensor(out=xn[:, 2 * b:2 * b + 2, :].rearrange("p t d -> p (t d)"),
                                                    in0=sig_r[:, 2 * b:2 * b + 2, :].rearrange("p t d -> p (t d)"), scalar=1.0,
                                                    in1=ring_d.bank(n), op0=ALU.add, op1=ALU.mult).then_inc(ring_d.free.sem, 1)
            dve.wait_ge(ring_d.free.sem, ring_d.free.at(i, du["out", 1] + 1))
            norm.vector(dve, i, 3, lambda t: xn[:, t, :], 4 * EPS)
            for t in range(NT):
                norm.apply(xn[:, t, :], xn[:, t, :], t).then_inc(normed.sem, 1)
            dve.wait_ge(normed.sem, normed.at(i, NT // 2 + NT))
            if not first:
                dve.wait_ge(x_stored.sem, x_stored.at(i, 0))
            nc.vector.tensor_tensor(x4[:], x3[:], xn[:], ALU.add).then_inc(x4_ready.sem, 1)

        body(0, first=True)
        with dve.Fori(1, BATCH) as i:
            body(i)

    @block.tensor
    def _(pe):
        pe.wait_ge(consts, 2)
        pe.wait_ge(w_sems[2], len(plan))

        def product(out, terms, chunks):
            todo = [(l, r, c) for c in range(chunks) for l, r in terms]
            for k, (l, r, c) in enumerate(todo):
                last = nc.tensor.matmul(out, l(c), r(c), start=(k == 0), stop=(k == len(todo) - 1))
            return last

        def token_major(out, x, w, t, cols, chunks):
            return product(out, [(lambda c, p=p: p[:, c, t * P:(t + 1) * P], lambda c, q=q: q[:, c, cols])
                                 for p, q in split_terms(*x, *w)], chunks)

        def width_major(out, x, w, cols, chunks):
            return product(out, [(lambda c, q=q: q[:, c, cols], lambda c, p=p: p[:, c, :])
                                 for p, q in split_terms(*x, *w)], chunks)

        def transposes(i, n, src, ready=lambda t: None):
            pe.wait_ge(ring_t.free.sem, ring_t.claim(i, n))
            for t in range(NT):
                ready(t)
                last = nc.tensor.transpose(ring_t.bank(n)[:, t * P:(t + 1) * P], src(t), ident[:])
            last.then_inc(ring_t.full.sem, 1)

        def body(i):
            for c in range(NC):
                transposes(i, tu["x", c], lambda t: xn[:, t, c * P:(c + 1) * P], lambda t: pe.wait_ge(xn_ready.sem, xn_ready.at(i, t + 1)))
            pe.wait_ge(ring_t.free.sem, ring_t.free.at(i, NC))
            for t in range(NT):
                for b in range(2):
                    n = du["v", t, b]
                    pe.wait_ge(ring_d.free.sem, ring_d.claim(i, n))
                    token_major(ring_d.bank(n), xT, wv, t, slice(b * 512, b * 512 + 512), NC).then_inc(ring_d.full.sem, 1)
            for step in range(NP1 + 3):
                if step < NP1:
                    for name, w in (("q", wq), ("k", wk)):
                        n = du[name, step]
                        pe.wait_ge(ring_d.free.sem, ring_d.claim(i, n))
                        width_major(ring_d.bank(n), xT, w, slice(step * P, (step + 1) * P), NC).then_inc(ring_d.full.sem, 1)
                if 1 <= step <= NP1:
                    p, slot = step - 1, (step - 1) % 2
                    pe.wait_ge(stack_ready.sem, stack_ready.at(i, 6 * p + 6))
                    for u in range(UNITS):
                        n = su["score", p, u]
                        pe.wait_ge(ring_s.free.sem, ring_s.claim(i, n))
                        for e in range(2):
                            for kt in range(NT):
                                unit, c0, c1 = unit_cols(e, kt)
                                if unit == u:
                                    out = ring_s.bank(n)[:, c0:c1]
                                    nc.tensor.matmul(out, ks[:, slot, e, kt * P:(kt + 1) * P], qs[:, slot, e, kt * P:T],
                                                     start=True, stop=False)
                                    last = nc.tensor.matmul(out, kl[:, slot, e, kt * P:(kt + 1) * P], qs[:, slot, e, kt * P:T],
                                                            start=False, stop=True)
                        last.then_inc(ring_s.full.sem, 1)
                if 2 <= step <= NP1 + 1:
                    p = step - 2
                    pe.wait_ge(masked.sem, masked.at(i, 3 * p + 3))
                    for e in range(2):
                        n = du["pv", p, e]
                        pe.wait_ge(ring_d.free.sem, ring_d.claim(i, n))
                        for qt in range(NT):
                            out = ring_d.bank(n)[:, qt * (HD1 + 1):(qt + 1) * (HD1 + 1)]
                            for kt in range(qt + 1):
                                u, c0, c1 = unit_cols(e, kt)
                                at = c0 + (qt - kt) * P
                                last = nc.tensor.matmul(out, probs[:, p % 2, u, at:at + P], v1[:, kt, 2 * p + e, :],
                                                        start=(kt == 0), stop=(kt == qt))
                        last.then_inc(ring_d.full.sem, 1)
                if step >= 3:
                    p = step - 3
                    pe.wait_ge(ring_d.free.sem, ring_d.free.at(i, du["pv", p, 1] + 1))
                    transposes(i, tu["att", p], lambda t: att[:, p % 2, t, :])
            pe.wait_ge(ring_t.free.sem, ring_t.free.at(i, tu["att", NP1 - 1] + 1))
            for b in range(2):
                n = du["o", b]
                pe.wait_ge(ring_d.free.sem, ring_d.claim(i, n))
                for t in (2 * b, 2 * b + 1):
                    last = token_major(ring_d.bank(n)[:, (t % 2) * D:(t % 2 + 1) * D], attT, wo, t, slice(0, D), NP1)
                last.then_inc(ring_d.full.sem, 1)
            for c in range(NC):
                transposes(i, tu["x3", c], lambda t: xn[:, t, c * P:(c + 1) * P], lambda t: pe.wait_ge(xn_ready.sem, xn_ready.at(i, NT + t + 1)))
            pe.wait_ge(mix_split.sem, mix_split.at(i, 4))
            for b in range(2):
                n = du["r", b]
                pe.wait_ge(ring_d.free.sem, ring_d.claim(i, n))
                for t in (2 * b, 2 * b + 1):
                    last = token_major(ring_d.bank(n)[:, (t % 2) * D:(t % 2 + 1) * D], mixr, wrkv, t, slice(0, D), NC)
                last.then_inc(ring_d.full.sem, 1)
            for c in range(NC):
                n = du["key", c]
                pe.wait_ge(ring_d.free.sem, ring_d.claim(i, n))
                width_major(ring_d.bank(n), mixk, wrkv, slice(D + c * P, D + (c + 1) * P), NC).then_inc(ring_d.full.sem, 1)
            pe.wait_ge(kact_split.sem, kact_split.at(i, 2))
            for b in range(2):
                n = du["out", b]
                pe.wait_ge(ring_d.free.sem, ring_d.claim(i, n))
                for t in (2 * b, 2 * b + 1):
                    last = token_major(ring_d.bank(n)[:, (t % 2) * D:(t % 2 + 1) * D], kact, wrkv, t, slice(2 * D, 3 * D), NC)
                last.then_inc(ring_d.full.sem, 1)

        with pe.Fori(0, BATCH) as i:
            body(i)


def kernel(**inputs):
    import concourse.bacc as bacc
    from concourse.bass_utils import run_bass_kernel_spmd

    x = {k: np.asarray(v) for k, v in inputs.items()}
    theta = (1.0 / np.float32(10000.0) ** (np.arange(0, HD0, 2, dtype=np.float32) / HD0)).astype(np.float32)
    angle = np.arange(1, T + 1, dtype=np.float32)[:, None] * theta[None, :]
    cos, sin = np.cos(angle), np.sin(angle)
    arrays = {
        "x": x["L0_attn_x"],
        "wqkv": np.concatenate([x["L0_attn_Wq"].T, x["L0_attn_Wk"].T, x["L0_attn_Wv"].T], axis=1),
        "b_qkv": np.concatenate([x["L0_attn_bq"], x["L0_attn_bk"], x["L0_attn_bv"]]),
        "wo": x["L0_attn_Wo"].T, "b_o": x["L0_attn_bo"],
        "cos": np.concatenate([cos, cos], axis=1), "sin": np.concatenate([-sin, sin], axis=1),
        "wgu": np.concatenate([x["L0_ffn_w_gate"].T, x["L0_ffn_w_up"].T], axis=1), "wd": x["L0_ffn_w_down"].T,
        "wq1": x["L1_attn_Wq"].T, "wk1": x["L1_attn_Wk"].T, "wv1": x["L1_attn_Wv"].T, "wo1": x["L1_attn_Wo"].T,
        "wrkv": np.concatenate([x["L1_ffn_W_r"].T, x["L1_ffn_W_k"].T, x["L1_ffn_W_v"].T], axis=1),
        "mu": np.stack([x["L1_ffn_mu_r"], x["L1_ffn_mu_k"]]).reshape(2, NC, P).transpose(2, 0, 1),
    }
    arrays = {f"in_{k}": np.ascontiguousarray(v) for k, v in arrays.items()}
    nc = bacc.Bacc("TRN2", target_bir_lowering=False, num_devices=1)
    a = {k[3:]: nc.dram_tensor(k, v.shape, mybir.dt.from_np(v.dtype), kind="ExternalInput").ap() for k, v in arrays.items()}
    a["out"] = nc.dram_tensor("out_x", (BATCH, T, D), F32, kind="ExternalOutput").ap()
    program(nc, a)
    return run_bass_kernel_spmd(nc, [arrays], core_ids=[0]).results[0]["out_x"]
```

```python
import numpy as np
import concourse.bass as bass
from concourse import mybir
from contextlib import ExitStack

F32 = mybir.dt.float32
F32R = mybir.dt.float32r
I32 = mybir.dt.int32
BF16 = mybir.dt.bfloat16
ALU = mybir.AluOpType
ACT = mybir.ActivationFunctionType

BATCH, T, D = 8, 512, 256
P = 128
NT = T // P
NC = D // P
EPS = 1e-5
BANK = 512

H0, HD0 = 16, 16
ROW0 = 64
KMAX = 3 * HD0
HID = 768
NM = HID // P
WSCALE = 1.0 / 127.0

H1, HD1 = 16, 64
F1 = H1 * HD1
NP1 = H1 // 2
CLAMP = 50.0

PAIRS = 8
PSLOTS = 3
UNITS = 5
MASKED = -1.0e30


class Signal:

    def __init__(self, sem, per, before=0):
        self.sem, self.per, self.before = sem, per, before

    def at(self, i, n):
        return i * self.per + n + self.before


class Ring:

    def __init__(self, banks, full, free):
        self.banks, self.full, self.free = banks, full, free
        free.before = len(banks)

    def bank(self, n):
        return self.banks[n % len(self.banks)]

    def claim(self, i, n):
        return self.free.at(i, n - len(self.banks) + 1)

    def arrived(self, i, n):
        return self.full.at(i, n + 1)


def unit_cols(e, kt):
    if kt == 0:
        return 2 * e, 0, 512
    if kt == 1:
        return 2 * e + 1, 0, 384
    if kt == 3:
        return 2 * e + 1, 384, 512
    return 4, 256 * e, 256 * e + 256


def split_terms(hi, lo, whi, wlo):
    return ((hi, whi), (lo, whi), (hi, wlo))


def uses(names):
    return {name: n for n, name in enumerate(names)}


def hold(nc, holder, ones):
    nc.gpsimd.tensor_tensor(holder, ones[:, 0:1], ones[:, 1:2], ALU.mult)


def mask_pair(pool, nc, probs, done):
    for part in (probs[:, :, 0:P], probs[:, 1:4:2, 384:512], probs[:, 4:5, 256:384]):
        n = part.shape[1]
        nc.gpsimd.affine_select(out=part, in_=part, compare_op=ALU.is_ge, fill=0.0, base=0,
                                pattern=[[0, n], [1, P]], channel_multiplier=-1).then_inc(done.sem, 1)


def program(nc, a):
    x_mid = nc.dram_tensor("x_mid", (BATCH, T, D), F32, kind="Internal").ap()
    tok = lambda ap, i: ap[i].rearrange("(t p) d -> p t d", p=P)
    with ExitStack() as ctx:
        psum = ctx.enter_context(nc.psum_tensor("psum", [P, 8, BANK], F32))
        banks = [psum[:, b, :] for b in range(8)]
        ident = ctx.enter_context(nc.sbuf_tensor("ident", [P, P], F32))
        expo = ctx.enter_context(nc.sbuf_tensor("expo", [P, NT], F32))
        for phase in (phase1, phase2):
            with ExitStack() as inner:
                phase(nc, inner, a, x_mid, tok, banks, ident, expo)


def load_split(nc, sp, act, dve, plan, staging, sems):
    loaded, hi_done, lo_done = sems
    slots = len(staging)
    if sp is not None:
        for n, (src, hi, lo, integer) in enumerate(plan):
            if n >= slots:
                sp.wait_ge(lo_done, n - slots + 1)
            dst = staging[n % slots][:, :src.shape[1]]
            sp.dma_start(dst.bitcast(I32) if integer else dst, src).then_inc(loaded[n % slots], 16)
    for eng in (act, dve):
        if eng is None:
            continue
        for n, (src, hi, lo, integer) in enumerate(plan):
            raw = staging[n % slots][:, :src.shape[1]]
            raw = raw.bitcast(I32) if integer else raw
            eng.wait_ge(loaded[n % slots], 16 * (n // slots + 1))
            if act is not None:
                nc.scalar.activation(hi, raw, ACT.Copy).then_inc(hi_done, 1)
            else:
                eng.wait_ge(hi_done, n + 1)
                nc.vector.tensor_tensor(lo, raw, hi.bitcast(F32), ALU.subtract).then_inc(lo_done, 1)


class Norm:

    def __init__(self, nc, sb, sig, expo, name, count):
        self.nc, self.expo = nc, expo
        self.stats = sb(name + "_stats", [P, NT, 6])
        self.mv = sb(name + "_mv", [P, NT, 2])
        self.veps = sb(name + "_veps", [P, NT])
        self.rstd = sb(name + "_rstd", [P, NT])
        self.holder = sb(name + "_holder", [P, 1])
        self.stats_ready = sig(name + "_stats_ready", count * NT)
        self.mv_ready = sig(name + "_mv_ready", count * NT)
        self.var_ready = sig(name + "_var_ready", count)
        self.rstd_ready = sig(name + "_rstd_ready", count)

    def statistics(self, dve, i, n, src, eps):
        nc = self.nc
        for t in range(NT):
            nc.vector.bn_stats(self.stats[:, t, :], src(t)).then_inc(self.stats_ready.sem, 1)
        dve.wait_ge(self.stats_ready.sem, self.stats_ready.at(i, (n + 1) * NT))
        nc.vector.memset(self.holder[:], 0.0)
        for t in range(NT):
            nc.vector.bn_aggr(self.mv[:, t, :], self.stats[:, t, :]).then_inc(self.mv_ready.sem, 1)
        dve.wait_ge(self.mv_ready.sem, self.mv_ready.at(i, (n + 1) * NT))
        nc.vector.tensor_scalar(self.veps[:], self.mv[:, :, 1], eps, None,
                                ALU.add).then_inc(self.var_ready.sem, 1)

    def gpsimd(self, pool, i, n):
        pool.wait_ge(self.var_ready.sem, self.var_ready.at(i, n + 1))
        self.nc.gpsimd.tensor_tensor(self.rstd[:], self.veps[:], self.expo[:],
                                     ALU.pow).then_inc(self.rstd_ready.sem, 1)

    def apply(self, out, src, t):
        return self.nc.vector.tensor_scalar(out, src, self.mv[:, t, 0:1], self.rstd[:, t:t + 1],
                                            ALU.subtract, ALU.mult)


def product(nc, out, terms, chunks):
    todo = [(l, r, c) for c in range(chunks) for l, r in terms]
    for k, (l, r, c) in enumerate(todo):
        last = nc.tensor.matmul(out, l(c), r(c), start=(k == 0), stop=(k == len(todo) - 1))
    return last


def token_major(nc, out, x, w, t, cols, chunks):
    return product(nc, out, [(lambda c, p=p: p[:, c, t * P:(t + 1) * P], lambda c, q=q: q[:, c, cols])
                             for p, q in split_terms(*x, *w)], chunks)


def width_major(nc, out, x, w, cols, chunks):
    return product(nc, out, [(lambda c, q=q: q[:, c, cols], lambda c, p=p: p[:, c, :])
                             for p, q in split_terms(*x, *w)], chunks)


def phase1(nc, ctx, a, x_mid, tok, banks, ident, expo):
    def sb(name, shape, dt=F32):
        return ctx.enter_context(nc.sbuf_tensor("l0_" + name, shape, dt))

    def sem(name):
        return ctx.enter_context(nc.semaphore("l0_" + name))

    def sig(name, per):
        return Signal(sem(name), per)

    wqkv = [sb("wqkv" + s, [P, NC, 3 * D], F32R) for s in ("_hi", "_lo")]
    wo = [sb("wo" + s, [P, NC, D], F32R) for s in ("_hi", "_lo")]
    wgu = [sb("wgu" + s, [P, NC, 2 * HID], F32R) for s in ("_hi", "_lo")]
    wd = [sb("wd" + s, [P, NM, D], F32R) for s in ("_hi", "_lo")]
    b_qkv = sb("b_qkv", [P, 3 * D])
    b_o = sb("b_o", [P, D])
    cos = sb("cos", [P, NT, HD0])
    sin = sb("sin", [P, NT, HD0])
    causal = sb("causal", [P, P], BF16)
    identb = sb("identb", [P, P], BF16)
    xin = sb("xin", [P, NT, D])
    stackq = sb("stackq", [P, H0 * ROW0])
    stackk = sb("stackk", [P, H0 * ROW0])
    qT = sb("qT", [P, PAIRS, T], F32R)
    kT = sb("kT", [P, PAIRS, T], F32R)
    v0 = sb("v0", [P, NT, H0, 32])
    rowmax = sb("rowmax", [P, NT, H0])
    maxT = sb("maxT", [4, 2, T], F32R)
    outT = sb("outT", [P, T])
    rden = sb("rden", [P, NT, 4])
    att = sb("att", [P, NT, D])
    yT = [sb("yT" + s, [P, NC, T], F32R) for s in ("_hi", "_lo")]
    xn = sb("xn", [P, NT, D])
    x1 = sb("x1", [P, NT, D])
    gated = sb("gated", [P, 2, T])
    hid = sb("hid", [P, 2, T])
    pool_holder = sb("pool_holder", [P, PAIRS])
    dve_holder = sb("dve_holder", [P, len(banks)])
    act_holder = sb("act_holder", [P, len(banks)])
    norm_x = Norm(nc, sb, sig, expo, "x", 1)
    norm_f = Norm(nc, sb, sig, expo, "f", 3)
    with nc.sbuf_tensor("l0_staging", [P, 2 * NM, T], F32) as raw:
        pass
    hT = [sb("hT" + s, [P, NM, T], F32R) for s in ("_hi", "_lo")]
    slots = 2 * NM * T // HID
    staging = [raw[:].rearrange("p a b -> p (a b)")[:, s * HID:(s + 1) * HID] for s in range(slots)]
    with nc.sbuf_tensor("l0_probs", [P, PSLOTS, UNITS, BANK], F32) as probs:
        pass
    qkb = sb("qkb", [P, 2, 2 * D])
    rot = sb("rot", [P, 2, 2 * D])
    rop = sb("rop", [P, 2, 2 * D])
    xT = [sb("xT" + s, [P, NC, T], F32R) for s in ("_hi", "_lo")]
    sb("probs_rest", [P, PSLOTS * UNITS * BANK - 12 * D - 2 * NC * T])

    front = [("x_stats",), ("att_T", 0), ("att_T", 1), ("x_norm",), ("o", 0), ("o", 1),
             ("x_T", 0), ("x_T", 1), ("x_T", 2), ("x_T", 3), ("o_stats",), ("qkv", 0), ("o_norm",),
             ("x1_stats",), ("qkv", 1), ("rope", 0), ("x1_norm",), ("stack", 0), ("x1_T", 0), ("x1_T", 1),
             ("rope", 1), ("qkv", 2), ("gate_up", 0), ("stack", 1), ("rope", 2), ("qkv", 3), ("gate_up", 1),
             ("stack", 2), ("rope", 3), ("gate_up", 2), ("stack", 3)]
    fill = {(0, 0): [("gate_up", 3)], (0, 2): [("gate_up", 4)], (1, 0): [("gate_up", 5)],
            (2, 0): [("down", 0)], (2, 1): [("down", 1)], (3, 0): [("x2_stats",)], (3, 1): [("x2_norm",)]}
    heads = []
    for step in range(6):
        for j in range(4):
            if step < 4:
                heads.append(("max", 4 * step + j))
            if j == 0 and 1 <= step < 5:
                heads.append(("maxT", step - 1))
            heads += fill.get((step, j), [])
            if j == 1 and step >= 2:
                heads.append(("pv", step - 2))
            if j == 3 and step >= 2:
                heads.append(("outT", step - 2))
            if j >= 2 and 1 <= step < 5:
                heads.append(("score", 2 * (step - 1) + j - 2))
    order = front + heads
    ffn = {"att_T", "o", "o_stats", "o_norm", "x1_stats", "x1_norm", "x1_T", "gate_up", "down", "x2_stats", "x2_norm"}
    attention = {name for name, *_ in order} - ffn

    def run(pieces, stages):
        for name, *k in order:
            for names, i in stages:
                if name in names and name in pieces:
                    pieces[name](i, *k)

    def program(eng, pieces):
        run(pieces, [(attention, 0)])
        with eng.Fori(1, BATCH) as i:
            run(pieces, [(attention, i), (ffn, i - 1)])
        run(pieces, [(ffn, BATCH - 1)])

    d_names, s_names, e_names = [], [], []
    for name, *k in order:
        if name in ("x_T", "pv", "outT"):
            d_names.append((name, *k))
        elif name == "qkv":
            d_names += [("qk", *k), ("v", *k)]
        elif name == "max":
            d_names += [("max", *k, t) for t in range(NT)]
        elif name == "stack":
            s_names += [("stack", *k, which, half) for which in ("q", "k") for half in range(2)]
        elif name == "maxT":
            s_names.append(("maxT", *k))
        elif name == "score":
            s_names += [("score", *k, u) for u in range(UNITS)]
        elif name in ("att_T", "x1_T", "o", "down"):
            e_names.append((name, *k))
        elif name == "gate_up":
            e_names += [("gate", *k), ("up", *k)]
    du, su, eu = uses(d_names), uses(s_names), uses(e_names)
    ring_d = Ring(banks[0:3], sig("d_full", len(du)), sig("d_free", len(du)))
    ring_s = Ring(banks[3:6], sig("s_full", len(su)), sig("s_free", len(su)))
    ring_e = Ring(banks[6:8], sig("e_full", len(eu)), sig("e_free", len(eu)))
    x_loaded = sig("x_loaded", 16)
    res_loaded = sig("res_loaded", 16)
    x_stored = sig("x_stored", 16)
    xn_ready = sig("xn_ready", NT)
    xT_hi = sig("xT_hi", NT)
    yn_ready = sig("yn_ready", NT)
    yT_hi = sig("yT_hi", 2 * NC)
    x1_ready = sig("x1_ready", 1)
    x2_ready = sig("x2_ready", 1)
    rope_cos = sig("rope_cos", NT)
    rot_ready = sig("rot_ready", 2 * NT)
    rop_ready = sig("rop_ready", NT)
    stack_hi = sig("stack_hi", 2 * NT)
    stack_ready = sig("stack_ready", 2 * NT)
    max_placed = sig("max_placed", 64 * 4)
    masked = sig("masked", 3 * PAIRS)
    rden_ready = sig("rden_ready", 4)
    normed = sig("normed", NT + NT // 2)
    th_ready = sig("th_ready", NM)
    hid_hi = sig("hid_hi", NM)
    hid_split = sig("hid_split", NM)

    w_loaded = [sem(f"w_loaded{n}") for n in range(slots)]
    w_hi, w_lo = sem("w_hi"), sem("w_lo")
    w_sems = (w_loaded, w_hi, w_lo)
    c_loaded = sem("c_loaded")
    consts = sem("consts")
    plan = []
    for c in range(NC):
        plan.append((a["wqkv"][c * P:(c + 1) * P, :], wqkv[0][:, c, :], wqkv[1][:, c, :], False))
    for c in range(NC):
        plan.append((a["wo"][c * P:(c + 1) * P, :], wo[0][:, c, :], wo[1][:, c, :], False))
    for c in range(NC):
        for g in range(2):
            cols = slice(g * HID, (g + 1) * HID)
            plan.append((a["wgu"][c * P:(c + 1) * P, cols], wgu[0][:, c, cols], wgu[1][:, c, cols], True))
    for m in range(NM):
        plan.append((a["wd"][m * P:(m + 1) * P, :], wd[0][:, m, :], wd[1][:, m, :], True))

    block = ctx.enter_context(nc.Block())

    @block.sync
    def _(sp):
        sp.dma_start(xin[:], tok(a["x"], 0)).then_inc(x_loaded.sem, 16)
        load_split(nc, sp, None, None, plan, staging, w_sems)

        def maxima(i):
            for g in range(4):
                sp.wait_ge(ring_s.free.sem, ring_s.free.at(i, su["maxT", g] + 1))
                for j in range(4):
                    row = ROW0 * (j % 2) + KMAX
                    sp.dma_start(qT[row:row + 1, 2 * g + j // 2, :].bitcast(F32),
                                 maxT[j:j + 1, g % 2, :].bitcast(F32)).then_inc(max_placed.sem, 16)

        def next_x(i):
            sp.wait_ge(ring_d.full.sem, ring_d.arrived(i, du["x_T", NT - 1]))
            sp.dma_start(xin[:], tok(a["x"], i + 1)).then_inc(x_loaded.sem, 16)

        def store(i):
            sp.wait_ge(x2_ready.sem, x2_ready.at(i, 1))
            sp.dma_start(tok(x_mid, i), x1[:]).then_inc(x_stored.sem, 16)

        def residual(i, first=False):
            if not first:
                sp.wait_ge(x_stored.sem, x_stored.at(i, 0))
            sp.dma_start(x1[:], tok(a["x"], i)).then_inc(res_loaded.sem, 16)

        next_x(0)
        maxima(0)
        residual(0, first=True)
        with sp.Fori(1, BATCH - 1) as i:
            next_x(i)
            maxima(i)
            store(i - 1)
            residual(i)
        maxima(BATCH - 1)
        store(BATCH - 2)
        residual(BATCH - 1)
        store(BATCH - 1)
        sp.wait_ge(x_stored.sem, x_stored.at(BATCH, 0))

    @block.gpsimd
    def _(pool):
        nc.gpsimd.memset(ident[:], 0.0).then_inc(consts, 1)
        nc.gpsimd.memset(causal[:], 0.0).then_inc(consts, 1)
        nc.gpsimd.memset(identb[:], 0.0).then_inc(consts, 1)
        nc.gpsimd.memset(expo[:], -0.5).then_inc(consts, 1)
        nc.gpsimd.memset(v0[:], 1.0).then_inc(consts, 1)
        nc.gpsimd.memset(stackq[:], 0.0).then_inc(consts, 1)
        nc.gpsimd.memset(stackk[:], 0.0).then_inc(consts, 1)
        pool.wait_ge(consts, 7)
        for eye in (ident, identb):
            nc.gpsimd.affine_select(out=eye[:], in_=eye[:], compare_op=ALU.not_equal, fill=1.0, base=0,
                                    pattern=[[-1, P]], channel_multiplier=1).then_inc(consts, 1)
        nc.gpsimd.affine_select(out=causal[:], in_=causal[:], compare_op=ALU.is_ge, fill=MASKED, base=0,
                                pattern=[[-1, P]], channel_multiplier=1).then_inc(consts, 1)
        ones = stackk[:].rearrange("p (h r) -> p h r", r=ROW0)[:, :, KMAX:KMAX + 1]
        nc.gpsimd.memset(ones, 1.0).then_inc(consts, 1)
        pool.wait_ge(c_loaded, 64)

        def qkv(i, t):
            pool.wait_ge(ring_d.free.sem, ring_d.free.at(i, du["qk", t] + 1))
            if t >= 2:
                pool.wait_ge(rop_ready.sem, rop_ready.at(i, t - 1))
            x = qkb[:, t % 2, :].rearrange("p (h e r) -> p h e r", e=2, r=HD0 // 2)
            r = rot[:, t % 2, :].rearrange("p (h e r) -> p h e r", e=2, r=HD0 // 2)
            for e in range(2):
                s = sin[:, t, 8 * e:8 * e + 8].unsqueeze(1).broadcast_to([P, 2 * H0, 8])
                nc.gpsimd.tensor_tensor(r[:, :, e, :], x[:, :, 1 - e, :], s, ALU.mult).then_inc(rot_ready.sem, 1)

        def rope(i, t):
            pool.wait_ge(stack_hi.sem, stack_hi.at(i, 2 * t + 2))
            for k, (stack, lo) in enumerate(((stackq, 1), (stackk, 2))):
                st = stack[:].rearrange("p (h r) -> p h r", r=ROW0)
                full = rop[:, t % 2, k * D:(k + 1) * D].rearrange("p (h r) -> p h r", r=HD0)
                nc.gpsimd.tensor_tensor(st[:, :, lo * HD0:(lo + 1) * HD0].bitcast(F32R), full,
                                        st[:, :, 0:HD0], ALU.subtract).then_inc(stack_ready.sem, 1)

        def score(i, p):
            pool.wait_ge(ring_s.free.sem, ring_s.free.at(i, su["score", p, UNITS - 1] + 1))
            hold(nc, pool_holder[:, p:p + 1], expo)
            mask_pair(pool, nc, probs[:, p % PSLOTS, :, :], masked)

        def gate_up(i, m):
            pool.wait_ge(hid_hi.sem, hid_hi.at(i, m + 1))
            nc.gpsimd.tensor_tensor(hT[1][:, m, :], hid[:, m % 2, :], hT[0][:, m, :].bitcast(F32),
                                    ALU.subtract).then_inc(hid_split.sem, 1)

        program(pool, {
            "x_stats": lambda i: norm_x.gpsimd(pool, i, 0), "qkv": qkv, "rope": rope, "score": score,
            "o_stats": lambda i: norm_f.gpsimd(pool, i, 0), "x1_stats": lambda i: norm_f.gpsimd(pool, i, 1),
            "gate_up": gate_up, "x2_stats": lambda i: norm_f.gpsimd(pool, i, 2)})

    @block.scalar
    def _(act):
        act.dma_start(b_qkv[:], a["b_qkv"].partition_broadcast(P)).then_inc(c_loaded, 16)
        act.dma_start(b_o[:], a["b_o"].partition_broadcast(P)).then_inc(c_loaded, 16)
        act.dma_start(cos[:], a["cos"].rearrange("(t p) r -> p t r", p=P)).then_inc(c_loaded, 16)
        act.dma_start(sin[:], a["sin"].rearrange("(t p) r -> p t r", p=P)).then_inc(c_loaded, 16)
        load_split(nc, None, act, None, plan, staging, w_sems)
        act.wait_ge(consts, 11)
        for b in range(len(ring_s.banks)):
            nc.scalar.activation(act_holder[:, b:b + 1], expo[:, 0:1], ACT.Copy).then_inc(ring_s.free.sem, 1)

        def x_T(i, t):
            n = du["x_T", t]
            act.wait_ge(ring_d.full.sem, ring_d.arrived(i, n))
            nc.scalar.activation(xT[0][:, :, t * P:(t + 1) * P],
                                 ring_d.bank(n)[:, 0:NC * P].rearrange("p (c q) -> p c q", c=NC),
                                 ACT.Copy).then_inc(xT_hi.sem, 1)

        def rope(i, t):
            act.wait_ge(rop_ready.sem, rop_ready.at(i, t + 1))
            if t:
                act.wait_ge(ring_s.full.sem, ring_s.arrived(i, su["stack", t - 1, "k", 1]))
            for k, (stack, step) in enumerate(((stackq, 2), (stackk, 1))):
                st = stack[:].rearrange("p (h s r) -> p h s r", s=ROW0 // HD0, r=HD0)
                full = rop[:, t % 2, k * D:(k + 1) * D].rearrange("p (h r) -> p h r", r=HD0)
                nc.scalar.activation(st[:, :, 0:step + 1:step, :].bitcast(F32R),
                                     full.unsqueeze(2).broadcast_to([P, H0, 2, HD0]),
                                     ACT.Copy).then_inc(stack_hi.sem, 1)

        def stack(i, t):
            for k, dst in (("q", qT), ("k", kT)):
                for half in range(2):
                    n = su["stack", t, k, half]
                    act.wait_ge(ring_s.full.sem, ring_s.arrived(i, n))
                    nc.scalar.activation(dst[:, 4 * half:4 * half + 4, t * P:(t + 1) * P],
                                         ring_s.bank(n).rearrange("p (a b) -> p a b", b=P),
                                         ACT.Copy).then_inc(ring_s.free.sem, 1)

        def row_max(i, g):
            n = su["maxT", g]
            act.wait_ge(ring_s.full.sem, ring_s.arrived(i, n))
            nc.scalar.activation(maxT[:, g % 2, :], ring_s.bank(n)[0:4, :], ACT.Copy,
                                 scale=-1.0).then_inc(ring_s.free.sem, 1)

        def score(i, p):
            if p >= PSLOTS:
                act.wait_ge(ring_d.full.sem, ring_d.arrived(i, du["pv", (p - PSLOTS) // 2]))
            for u in range(UNITS):
                n = su["score", p, u]
                act.wait_ge(ring_s.full.sem, ring_s.arrived(i, n))
                nc.scalar.activation(probs[:, p % PSLOTS, u, :], ring_s.bank(n), ACT.Exp,
                                     scale=HD0 ** -0.5).then_inc(ring_s.free.sem, 1)

        def y_T(name):
            def high(i, c):
                n = eu[name, c]
                act.wait_ge(ring_e.full.sem, ring_e.arrived(i, n))
                nc.scalar.activation(yT[0][:, c, :], ring_e.bank(n), ACT.Copy).then_inc(yT_hi.sem, 1)
            return high

        def hidden_high(i, m):
            act.wait_ge(ring_e.free.sem, ring_e.free.at(i, eu["up", m] + 1))
            nc.scalar.activation(hT[0][:, m, :], hid[:, m % 2, :], ACT.Copy).then_inc(hid_hi.sem, 1)

        def gate_up(i, m):
            n = eu["gate", m]
            act.wait_ge(ring_e.full.sem, ring_e.arrived(i, n))
            if m >= 2:
                act.wait_ge(ring_e.free.sem, ring_e.free.at(i, eu["up", m - 2] + 1))
            nc.scalar.activation(gated[:, m % 2, :], ring_e.bank(n), ACT.Tanh,
                                 scale=0.5 * WSCALE).then_inc(th_ready.sem, 1)
            hidden_high(i, m)

        program(act, {"x_T": x_T, "rope": rope, "stack": stack, "maxT": row_max, "score": score,
                      "att_T": y_T("att_T"), "x1_T": y_T("x1_T"), "gate_up": gate_up})

    @block.vector
    def _(dve):
        load_split(nc, None, None, dve, plan, staging, w_sems)
        dve.wait_ge(c_loaded, 64)
        dve.wait_ge(consts, 11)

        for b in range(len(ring_d.banks)):
            nc.vector.memset(dve_holder[:, b:b + 1], 0.0).then_inc(ring_d.free.sem, 1)
        for b in range(len(ring_d.banks), len(ring_d.banks) + len(ring_e.banks)):
            nc.vector.memset(dve_holder[:, b:b + 1], 0.0).then_inc(ring_e.free.sem, 1)

        def x_stats(i):
            dve.wait_ge(x_loaded.sem, x_loaded.at(i, 16))
            norm_x.statistics(dve, i, 0, lambda t: xin[:, t, :], EPS)

        def x_norm(i):
            dve.wait_ge(norm_x.rstd_ready.sem, norm_x.rstd_ready.at(i, 1))
            for t in range(NT):
                norm_x.apply(xin[:, t, :], xin[:, t, :], t).then_inc(xn_ready.sem, 1)

        def x_T(i, t):
            n = du["x_T", t]
            dve.wait_ge(xT_hi.sem, xT_hi.at(i, t + 1))
            cols = slice(t * P, (t + 1) * P)
            nc.vector.tensor_tensor(xT[1][:, :, cols], ring_d.bank(n)[:, 0:NC * P].rearrange("p (c q) -> p c q", c=NC),
                                    xT[0][:, :, cols].bitcast(F32), ALU.subtract).then_inc(ring_d.free.sem, 1)

        def qkv(i, t):
            n = du["qk", t]
            dve.wait_ge(ring_d.full.sem, ring_d.arrived(i, n))
            if t >= 2:
                dve.wait_ge(rot_ready.sem, rot_ready.at(i, 2 * (t - 1)))
            nc.vector.tensor_tensor(qkb[:, t % 2, :], ring_d.bank(n), b_qkv[:, 0:2 * D], ALU.add).then_inc(ring_d.free.sem, 1)
            n = du["v", t]
            dve.wait_ge(ring_d.full.sem, ring_d.arrived(i, n))
            nc.vector.tensor_tensor(
                v0[:, t, :, 0:HD0], ring_d.bank(n)[:, 0:D].rearrange("p (h r) -> p h r", r=HD0),
                b_qkv[:, 2 * D:3 * D].rearrange("p (h r) -> p h r", r=HD0), ALU.add).then_inc(ring_d.free.sem, 1)
            if t >= 2:
                dve.wait_ge(stack_ready.sem, stack_ready.at(i, 2 * (t - 1)))
            dve.wait_ge(ring_d.free.sem, ring_d.free.at(i, du["qk", t] + 1))
            c16 = cos[:, t, :].unsqueeze(1).broadcast_to([P, 2 * H0, HD0])
            nc.vector.tensor_tensor(rop[:, t % 2, :].rearrange("p (h r) -> p h r", r=HD0),
                                    qkb[:, t % 2, :].rearrange("p (h r) -> p h r", r=HD0),
                                    c16, ALU.mult).then_inc(rope_cos.sem, 1)

        def rope(i, t):
            dve.wait_ge(rot_ready.sem, rot_ready.at(i, 2 * t + 2))
            dve.wait_ge(rope_cos.sem, rope_cos.at(i, t + 1))
            nc.vector.tensor_tensor(rop[:, t % 2, :], rop[:, t % 2, :], rot[:, t % 2, :], ALU.add).then_inc(rop_ready.sem, 1)

        def row_max(i, h):
            for t in range(NT):
                n = du["max", h, t]
                dve.wait_ge(ring_d.full.sem, ring_d.arrived(i, n))
                nc.vector.tensor_reduce(rowmax[:, t, h:h + 1], ring_d.bank(n)[:, 0:(t + 1) * P],
                                        mybir.AxisListType.X, ALU.max).then_inc(ring_d.free.sem, 1)

        def pv(i, g):
            n = du["pv", g]
            dve.wait_ge(ring_d.full.sem, ring_d.arrived(i, n))
            nc.vector.tensor_copy(outT[:], ring_d.bank(n)).then_inc(ring_d.free.sem, 1)

        def out_T(i, g):
            n = du["outT", g]
            dve.wait_ge(ring_d.full.sem, ring_d.arrived(i, n))
            view = ring_d.bank(n).rearrange("p (t j r) -> p t j r", t=NT, r=32)
            nc.vector.reciprocal(rden[:].unsqueeze(3), view[:, :, :, HD0:HD0 + 1]).then_inc(rden_ready.sem, 1)
            dve.wait_ge(rden_ready.sem, rden_ready.at(i, g + 1))
            dst = att[:, :, 64 * g:64 * g + 64].rearrange("p t (j r) -> p t j r", r=HD0)
            nc.vector.tensor_tensor(dst, view[:, :, :, 0:HD0], rden[:].unsqueeze(3).broadcast_to([P, NT, 4, HD0]),
                                    ALU.mult).then_inc(ring_d.free.sem, 1)

        def y_T(name):
            def low(i, c):
                n = eu[name, c]
                dve.wait_ge(yT_hi.sem, yT_hi.at(i, (0 if name == "att_T" else NC) + c + 1))
                nc.vector.tensor_tensor(yT[1][:, c, :], ring_e.bank(n), yT[0][:, c, :].bitcast(F32),
                                        ALU.subtract).then_inc(ring_e.free.sem, 1)
            return low

        def o(i, b):
            n = eu["o", b]
            dve.wait_ge(ring_e.full.sem, ring_e.arrived(i, n))
            nc.vector.tensor_tensor(xn[:, 2 * b:2 * b + 2, :], ring_e.bank(n).rearrange("p (t d) -> p t d", d=D),
                                    b_o[:].unsqueeze(1).broadcast_to([P, 2, D]), ALU.add).then_inc(ring_e.free.sem, 1)

        def o_stats(i):
            dve.wait_ge(ring_e.free.sem, ring_e.free.at(i, eu["o", 1] + 1))
            norm_f.statistics(dve, i, 0, lambda t: xn[:, t, :], EPS)

        def o_norm(i):
            dve.wait_ge(norm_f.rstd_ready.sem, norm_f.rstd_ready.at(i, 1))
            for t in range(NT):
                norm_f.apply(xn[:, t, :], xn[:, t, :], t).then_inc(normed.sem, 1)
            dve.wait_ge(res_loaded.sem, res_loaded.at(i, 16))
            dve.wait_ge(normed.sem, normed.at(i, NT))
            nc.vector.tensor_tensor(x1[:], x1[:], xn[:], ALU.add).then_inc(x1_ready.sem, 1)

        def x1_stats(i):
            dve.wait_ge(x1_ready.sem, x1_ready.at(i, 1))
            norm_f.statistics(dve, i, 1, lambda t: x1[:, t, :], EPS)

        def x1_norm(i):
            dve.wait_ge(norm_f.rstd_ready.sem, norm_f.rstd_ready.at(i, 2))
            for t in range(NT):
                norm_f.apply(xn[:, t, :], x1[:, t, :], t).then_inc(yn_ready.sem, 1)

        def gate_up(i, m):
            n = eu["gate", m]
            dve.wait_ge(th_ready.sem, th_ready.at(i, m + 1))
            nc.vector.scalar_tensor_tensor(out=gated[:, m % 2, :], in0=gated[:, m % 2, :], scalar=1.0, in1=ring_e.bank(n),
                                           op0=ALU.add, op1=ALU.mult).then_inc(ring_e.free.sem, 1)
            n = eu["up", m]
            dve.wait_ge(ring_e.full.sem, ring_e.arrived(i, n))
            if m >= 2:
                dve.wait_ge(hid_split.sem, hid_split.at(i, m - 1))
            dve.wait_ge(ring_e.free.sem, ring_e.free.at(i, eu["gate", m] + 1))
            nc.vector.tensor_tensor(hid[:, m % 2, :], ring_e.bank(n), gated[:, m % 2, :], ALU.mult).then_inc(ring_e.free.sem, 1)

        unit = 2.0 / WSCALE ** 3
        half = lambda t: ring_e.bank(eu["down", t // 2])[:, (t % 2) * D:(t % 2 + 1) * D]

        def x2_stats(i):
            dve.wait_ge(ring_e.full.sem, ring_e.arrived(i, eu["down", 1]))
            norm_f.statistics(dve, i, 2, half, EPS * unit * unit)

        def x2_norm(i):
            dve.wait_ge(norm_f.rstd_ready.sem, norm_f.rstd_ready.at(i, 3))
            for t in range(NT):
                norm_f.apply(xn[:, t, :], half(t), t).then_inc((normed, ring_e.free)[t % 2].sem, 1)
            dve.wait_ge(normed.sem, normed.at(i, NT + NT // 2))
            dve.wait_ge(ring_e.free.sem, ring_e.free.at(i, eu["down", 1] + 1))
            nc.vector.tensor_tensor(x1[:], x1[:], xn[:], ALU.add).then_inc(x2_ready.sem, 1)

        program(dve, {
            "x_stats": x_stats, "x_norm": x_norm, "x_T": x_T, "qkv": qkv, "rope": rope, "max": row_max, "pv": pv,
            "outT": out_T, "att_T": y_T("att_T"), "x1_T": y_T("x1_T"), "o": o, "o_stats": o_stats, "o_norm": o_norm,
            "x1_stats": x1_stats, "x1_norm": x1_norm, "gate_up": gate_up, "x2_stats": x2_stats, "x2_norm": x2_norm})

    @block.tensor
    def _(pe):
        pe.wait_ge(consts, 11)
        pe.wait_ge(w_lo, len(plan))

        def x_T(i, t):
            n = du["x_T", t]
            pe.wait_ge(ring_d.free.sem, ring_d.claim(i, n))
            pe.wait_ge(xn_ready.sem, xn_ready.at(i, t + 1))
            for c in range(NC):
                last = nc.tensor.transpose(ring_d.bank(n)[:, c * P:(c + 1) * P], xin[:, t, c * P:(c + 1) * P], ident[:])
            last.then_inc(ring_d.full.sem, 1)

        def qkv(i, t):
            pe.wait_ge(ring_d.free.sem, ring_d.free.at(i, du["x_T", t] + 1))
            for n, cols in ((du["qk", t], slice(0, 2 * D)), (du["v", t], slice(2 * D, 3 * D))):
                pe.wait_ge(ring_d.free.sem, ring_d.claim(i, n))
                last = token_major(nc, ring_d.bank(n)[:, 0:cols.stop - cols.start], xT, wqkv, t, cols, NC)
                last.then_inc(ring_d.full.sem, 1)

        def stack(i, t):
            pe.wait_ge(stack_ready.sem, stack_ready.at(i, 2 * t + 2))
            for k, st in (("q", stackq), ("k", stackk)):
                for half in range(2):
                    n = su["stack", t, k, half]
                    pe.wait_ge(ring_s.free.sem, ring_s.claim(i, n))
                    for b in range(4):
                        p = 4 * half + b
                        last = nc.tensor.transpose(ring_s.bank(n)[:, b * P:(b + 1) * P], st[:, p * P:(p + 1) * P], ident[:])
                    last.then_inc(ring_s.full.sem, 1)

        def row_max(i, h):
            if h == 0:
                pe.wait_ge(ring_s.free.sem, ring_s.free.at(i, su["stack", NT - 1, "k", 1] + 1))
            rows = slice(ROW0 * (h % 2), ROW0 * (h % 2) + KMAX)
            for t in range(NT):
                n = du["max", h, t]
                pe.wait_ge(ring_d.free.sem, ring_d.claim(i, n))
                nc.tensor.matmul(ring_d.bank(n)[:, 0:(t + 1) * P], qT[rows, h // 2, t * P:(t + 1) * P],
                                 kT[rows, h // 2, 0:(t + 1) * P], start=True, stop=False)
                nc.tensor.matmul(ring_d.bank(n)[:, t * P:(t + 1) * P], identb[:], causal[:],
                                 start=False, stop=True).then_inc(ring_d.full.sem, 1)

        def max_T(i, g):
            n = su["maxT", g]
            pe.wait_ge(ring_s.free.sem, ring_s.claim(i, n))
            pe.wait_ge(ring_d.free.sem, ring_d.free.at(i, du["max", 4 * g + 3, NT - 1] + 1))
            for t in range(NT):
                last = nc.tensor.transpose(ring_s.bank(n)[0:4, t * P:(t + 1) * P], rowmax[:, t, 4 * g:4 * g + 4], ident[:])
            last.then_inc(ring_s.full.sem, 1)

        def score(i, p):
            pe.wait_ge(max_placed.sem, max_placed.at(i, 64 * (p // 2 + 1)))
            for u in range(UNITS):
                n = su["score", p, u]
                pe.wait_ge(ring_s.free.sem, ring_s.claim(i, n))
                rows = slice(ROW0 * (p % 2), ROW0 * (p % 2) + KMAX + 1)
                for e in range(2):
                    at = 2 * (p // 2) + e
                    for kt in range(NT):
                        unit, c0, c1 = unit_cols(e, kt)
                        if unit == u:
                            last = nc.tensor.matmul(ring_s.bank(n)[:, c0:c1], kT[rows, at, kt * P:(kt + 1) * P],
                                                    qT[rows, at, kt * P:T], start=True, stop=True)
                last.then_inc(ring_s.full.sem, 1)

        def pv(i, g):
            n = du["pv", g]
            pe.wait_ge(ring_d.free.sem, ring_d.claim(i, n))
            pe.wait_ge(masked.sem, masked.at(i, 3 * (2 * g + 2)))
            for kt in range(NT):
                for j in range(4):
                    h = 4 * g + j
                    u, c0, c1 = unit_cols(j // 2, kt)
                    last = nc.tensor.matmul(ring_d.bank(n)[32 * j:32 * j + 32, kt * P:T], v0[:, kt, h, :],
                                            probs[:, (2 * g + j % 2) % PSLOTS, u, c0:c1], start=(kt == 0),
                                            stop=(kt == NT - 1), tile_position=(0, 32 * j))
            last.then_inc(ring_d.full.sem, 1)

        def out_T(i, g):
            n = du["outT", g]
            pe.wait_ge(ring_d.free.sem, ring_d.claim(i, n))
            pe.wait_ge(ring_d.free.sem, ring_d.free.at(i, du["pv", g] + 1))
            for t in range(NT):
                last = nc.tensor.transpose(ring_d.bank(n)[:, t * P:(t + 1) * P], outT[:, t * P:(t + 1) * P], ident[:])
            last.then_inc(ring_d.full.sem, 1)

        def y_T(name, src):
            def transposes(i, c):
                n = eu[name, c]
                pe.wait_ge(ring_e.free.sem, ring_e.claim(i, n))
                if name == "att_T":
                    pe.wait_ge(ring_d.free.sem, ring_d.free.at(i, du["outT", 3] + 1))
                else:
                    pe.wait_ge(yn_ready.sem, yn_ready.at(i, NT))
                for t in range(NT):
                    last = nc.tensor.transpose(ring_e.bank(n)[:, t * P:(t + 1) * P], src[:, t, c * P:(c + 1) * P], ident[:])
                last.then_inc(ring_e.full.sem, 1)
            return transposes

        def o(i, b):
            n = eu["o", b]
            pe.wait_ge(ring_e.free.sem, ring_e.claim(i, n))
            pe.wait_ge(ring_e.free.sem, ring_e.free.at(i, eu["att_T", NC - 1] + 1))
            for t in (2 * b, 2 * b + 1):
                last = token_major(nc, ring_e.bank(n)[:, (t % 2) * D:(t % 2 + 1) * D], yT, wo, t, slice(0, D), NC)
            last.then_inc(ring_e.full.sem, 1)

        def gate_up(i, m):
            pe.wait_ge(ring_e.free.sem, ring_e.free.at(i, eu["x1_T", NC - 1] + 1))
            for k, name in enumerate(("gate", "up")):
                n = eu[name, m]
                pe.wait_ge(ring_e.free.sem, ring_e.claim(i, n))
                cols = slice(k * HID + m * P, k * HID + (m + 1) * P)
                width_major(nc, ring_e.bank(n), yT, wgu, cols, NC).then_inc(ring_e.full.sem, 1)

        def down(i, b):
            n = eu["down", b]
            pe.wait_ge(ring_e.free.sem, ring_e.claim(i, n))
            pe.wait_ge(hid_split.sem, hid_split.at(i, NM))
            for t in (2 * b, 2 * b + 1):
                last = token_major(nc, ring_e.bank(n)[:, (t % 2) * D:(t % 2 + 1) * D], hT, wd, t, slice(0, D), NM)
            last.then_inc(ring_e.full.sem, 1)

        program(pe, {"x_T": x_T, "qkv": qkv, "stack": stack, "max": row_max, "maxT": max_T, "score": score, "pv": pv,
                     "outT": out_T, "att_T": y_T("att_T", att), "x1_T": y_T("x1_T", xn), "o": o, "gate_up": gate_up,
                     "down": down})


def phase2(nc, ctx, a, x_mid, tok, banks, ident, expo):
    def sb(name, shape, dt=F32):
        return ctx.enter_context(nc.sbuf_tensor("l1_" + name, shape, dt))

    def sem(name):
        return ctx.enter_context(nc.semaphore("l1_" + name))

    def sig(name, per):
        return Signal(sem(name), per)

    wq = [sb("wq" + s, [P, NC, F1], F32R) for s in ("_hi", "_lo")]
    wk = [sb("wk" + s, [P, NC, F1], F32R) for s in ("_hi", "_lo")]
    wv = [sb("wv" + s, [P, NC, F1], F32R) for s in ("_hi", "_lo")]
    wo = [sb("wo" + s, [P, NP1, D], F32R) for s in ("_hi", "_lo")]
    wrkv = [sb("wrkv" + s, [P, NC, 3 * D], F32R) for s in ("_hi", "_lo")]
    mu = sb("mu", [P, 2, NC])
    xin = sb("xin", [P, NT, D])
    xn = sb("xn", [P, NT, D])
    xT = [sb("xT" + s, [P, NC, T], F32R) for s in ("_hi", "_lo")]
    qs = sb("qs", [P, 2, 2, T], F32R)
    ks = sb("ks", [P, 2, 2, T], F32R)
    kl = sb("kl", [P, 2, 2, T], F32R)
    v1 = sb("v1", [P, NT, H1, HD1 + 1])
    probs = sb("probs", [P, 2, UNITS, BANK])
    rden = sb("rden", [P, 2, NT])
    att = sb("att", [P, 2, NT, P])
    attT = [sb("attT" + s, [P, NP1, T], F32R) for s in ("_hi", "_lo")]
    x3 = sb("x3", [P, NT, D])
    x4 = sb("x4", [P, NT, D])
    xs = sb("xs", [P, NC, T + 1])
    dx = sb("dx", [P, NC, T])
    flat = [t[:].rearrange("p a b -> p (a b)") for t in attT]
    view = lambda t, n: t[:, n * NC * T:(n + 1) * NC * T].rearrange("p (c t) -> p c t", c=NC)
    mixr = [view(flat[0], 0), view(flat[0], 1)]
    mixk = [view(flat[0], 2), view(flat[0], 3)]
    mix = [probs[:, s, 0:NC, :] for s in range(2)]
    kact = [view(flat[1], 2), view(flat[1], 3)]
    sig_r = probs[:, 0, 2:4, :].rearrange("p a (t d) -> p (a t) d", d=D)
    relu = dx
    pool_holder = sb("pool_holder", [P, PAIRS])
    dve_holder = sb("dve_holder", [P, len(banks)])
    act_holder = sb("act_holder", [P, len(banks)])
    staging = [probs[:, s // 2, :, :].rearrange("p a b -> p (a b)")[:, 1280 * (s % 2):1280 * (s % 2) + 1024]
               for s in range(4)]

    d_names = [("v", t, b) for t in range(NT) for b in range(2)]
    s_names, t_names = [], [("x", 0), ("x", 1)]
    for step in range(NP1 + 3):
        if step < NP1:
            d_names += [("q", step), ("k", step)]
        if 1 <= step <= NP1:
            s_names += [("score", step - 1, u) for u in range(UNITS)]
        if 2 <= step <= NP1 + 1:
            d_names += [("pv", step - 2, e) for e in range(2)]
        if step >= 3:
            t_names.append(("att", step - 3))
    d_names += [("o", 0), ("o", 1)]
    t_names += [("x3", 0), ("x3", 1)]
    d_names += [("r", 0), ("r", 1), ("key", 0), ("key", 1), ("out", 0), ("out", 1)]
    du, su, tu = uses(d_names), uses(s_names), uses(t_names)
    assert len(du) % 3 == 0 and len(su) % 4 == 0

    ring_t = Ring(banks[0:1], sig("transposed", len(tu)), sig("split_done", len(tu)))
    ring_d = Ring(banks[1:4], sig("d_full", len(du)), sig("d_free", len(du)))
    ring_s = Ring(banks[4:8], sig("s_full", len(su)), sig("s_free", len(su)))
    hi_done = sig("hi_done", len(tu) - NC)
    x_loaded = sig("x_loaded", 16)
    x_stored = sig("x_stored", 16)
    xn_ready = sig("xn_ready", 2 * NT)
    x3_ready = sig("x3_ready", 1)
    x4_ready = sig("x4_ready", 1)
    proj_hi = sig("proj_hi", 4 * NP1)
    stack_ready = sig("stack_ready", 6 * NP1)
    exped = sig("exped", 2 * NP1)
    masked = sig("masked", 3 * NP1)
    mix_ready = sig("mix_ready", 4)
    mix_hi = sig("mix_hi", 4)
    mix_split = sig("mix_split", 4)
    gate_ready = sig("gate_ready", 2)
    sq_ready = sig("sq_ready", 2)
    kact_hi = sig("kact_hi", 2)
    kact_split = sig("kact_split", 2)
    rden_ready = sig("rden_ready", 2 * NP1)
    normed = sig("normed", NT // 2 + NT)
    dx_ready = sig("dx_ready", NC)
    w_loaded = [sem(f"w_loaded{n}") for n in range(4)]
    w_sems = (w_loaded, sem("w_hi"), sem("w_lo"))
    c_loaded = sem("c_loaded")
    consts = sem("consts")
    norm = Norm(nc, sb, sig, expo, "n", 4)
    plan = []
    for name, dst in (("wq1", wq), ("wk1", wk), ("wv1", wv), ("wrkv", wrkv)):
        for c in range(NC):
            plan.append((a[name][c * P:(c + 1) * P, :], dst[0][:, c, :], dst[1][:, c, :], False))
    for c in range(NP1):
        plan.append((a["wo1"][c * P:(c + 1) * P, :], wo[0][:, c, :], wo[1][:, c, :], False))

    block = ctx.enter_context(nc.Block())

    @block.sync
    def _(sp):
        sp.dma_start(xin[:], tok(x_mid, 0)).then_inc(x_loaded.sem, 16)
        load_split(nc, sp, None, None, plan, staging, w_sems)

        def body(i, last=False):
            sp.wait_ge(x3_ready.sem, x3_ready.at(i, 1))
            if not last:
                sp.dma_start(xin[:], tok(x_mid, i + 1)).then_inc(x_loaded.sem, 16)
            sp.wait_ge(x4_ready.sem, x4_ready.at(i, 1))
            sp.dma_start(tok(a["out"], i), x4[:]).then_inc(x_stored.sem, 16)

        with sp.Fori(0, BATCH - 1) as i:
            body(i)
        body(BATCH - 1, last=True)
        sp.wait_ge(x_stored.sem, x_stored.at(BATCH, 0))

    @block.gpsimd
    def _(pool):
        nc.gpsimd.memset(v1[:, :, :, HD1:HD1 + 1], 1.0).then_inc(consts, 1)
        nc.gpsimd.memset(xs[:, :, 0:1], 0.0).then_inc(consts, 1)

        def body(i):
            norm.gpsimd(pool, i, 0)
            for p in range(NP1):
                pool.wait_ge(exped.sem, exped.at(i, 2 * p + 2))
                hold(nc, pool_holder[:, p:p + 1], expo)
                mask_pair(pool, nc, probs[:, p % 2, :, :], masked)
            norm.gpsimd(pool, i, 1)
            norm.gpsimd(pool, i, 2)
            norm.gpsimd(pool, i, 3)

        with pool.Fori(0, BATCH) as i:
            body(i)

    @block.scalar
    def _(act):
        act.dma_start(mu[:], a["mu"]).then_inc(c_loaded, 16)
        load_split(nc, None, act, None, plan, staging, w_sems)

        for b in range(len(ring_s.banks)):
            nc.scalar.activation(act_holder[:, b:b + 1], expo[:, 0:1], ACT.Copy).then_inc(ring_s.free.sem, 1)

        def body(i):
            for c in range(NC):
                n = tu["x", c]
                act.wait_ge(ring_t.full.sem, ring_t.arrived(i, n))
                nc.scalar.activation(xT[0][:, c, :], ring_t.bank(n), ACT.Copy).then_inc(hi_done.sem, 1)
            for step in range(NP1 + 3):
                if step < NP1:
                    p, slot = step, step % 2
                    for k, (name, dst) in enumerate((("q", qs), ("k", ks))):
                        n = du[name, p]
                        act.wait_ge(ring_d.full.sem, ring_d.arrived(i, n))
                        for e in range(2):
                            half = slice(64 * e, 64 * e + 64)
                            nc.scalar.activation(dst[half, slot, e, :], ring_d.bank(n)[half, :],
                                                 ACT.Copy).then_inc(proj_hi.sem, 1)
                if 1 <= step <= NP1:
                    p = step - 1
                    if p >= 2:
                        act.wait_ge(ring_d.full.sem, ring_d.arrived(i, du["pv", p - 2, 1]))
                    for u in range(UNITS):
                        n = su["score", p, u]
                        act.wait_ge(ring_s.full.sem, ring_s.arrived(i, n))
                        nc.scalar.activation(probs[:, p % 2, u, :], ring_s.bank(n), ACT.Tanh,
                                             scale=HD1 ** -0.5 / CLAMP).then_inc(ring_s.free.sem, 1)
                    act.wait_ge(ring_s.free.sem, ring_s.free.at(i, su["score", p, UNITS - 1] + 1))
                    for part in (probs[:, p % 2, 0:3, :], probs[:, p % 2, 3:5, :]):
                        nc.scalar.activation(part, part, ACT.Exp, scale=CLAMP).then_inc(exped.sem, 1)
                if step >= 3:
                    n = tu["att", step - 3]
                    act.wait_ge(ring_t.full.sem, ring_t.arrived(i, n))
                    nc.scalar.activation(attT[0][:, step - 3, :], ring_t.bank(n), ACT.Copy).then_inc(hi_done.sem, 1)
            for c in range(NC):
                for k, dst in enumerate((mixr, mixk)):
                    act.wait_ge(mix_ready.sem, mix_ready.at(i, 2 * c + k + 1))
                    nc.scalar.activation(dst[0][:, c, :], mix[k][:, c, :], ACT.Copy).then_inc(mix_hi.sem, 1)
            for b in range(2):
                half = sig_r[:, 2 * b:2 * b + 2, :]
                act.wait_ge(ring_d.free.sem, ring_d.free.at(i, du["r", b] + 1))
                nc.scalar.activation(half, half, ACT.Tanh, scale=0.5).then_inc(gate_ready.sem, 1)
            for c in range(NC):
                act.wait_ge(sq_ready.sem, sq_ready.at(i, c + 1))
                nc.scalar.activation(kact[0][:, c, :], relu[:, c, :], ACT.Copy).then_inc(kact_hi.sem, 1)

        with act.Fori(0, BATCH) as i:
            body(i)

    @block.vector
    def _(dve):
        load_split(nc, None, None, dve, plan, staging, w_sems)
        dve.wait_ge(c_loaded, 16)
        dve.wait_ge(consts, 2)

        for b in range(len(ring_t.banks)):
            nc.vector.memset(dve_holder[:, b:b + 1], 0.0).then_inc(ring_t.free.sem, 1)
        for b in range(len(ring_d.banks)):
            nc.vector.memset(dve_holder[:, len(ring_t.banks) + b:len(ring_t.banks) + b + 1], 0.0).then_inc(ring_d.free.sem, 1)

        def low(i, n, dst, hi):
            dve.wait_ge(hi_done.sem, hi_done.at(i, n + 1))
            nc.vector.tensor_tensor(dst, ring_t.bank(n), hi.bitcast(F32), ALU.subtract).then_inc(ring_t.free.sem, 1)

        def body(i, first=False):
            dve.wait_ge(x_loaded.sem, x_loaded.at(i, 16))
            norm.statistics(dve, i, 0, lambda t: xin[:, t, :], EPS)
            dve.wait_ge(norm.rstd_ready.sem, norm.rstd_ready.at(i, 1))
            for t in range(NT):
                norm.apply(xn[:, t, :], xin[:, t, :], t).then_inc(xn_ready.sem, 1)
            for c in range(NC):
                low(i, tu["x", c], xT[1][:, c, :], xT[0][:, c, :])
            for t in range(NT):
                for b in range(2):
                    n = du["v", t, b]
                    dve.wait_ge(ring_d.full.sem, ring_d.arrived(i, n))
                    nc.vector.tensor_copy(v1[:, t, 8 * b:8 * b + 8, 0:HD1],
                                               ring_d.bank(n).rearrange("p (h r) -> p h r", r=HD1)).then_inc(ring_d.free.sem, 1)
            for step in range(NP1 + 3):
                if step < NP1:
                    p, slot = step, step % 2
                    halves = [(slice(64 * e, 64 * e + 64), slice(64 - 64 * e, 128 - 64 * e)) for e in range(2)]
                    n = du["q", p]
                    dve.wait_ge(proj_hi.sem, proj_hi.at(i, 4 * p + 2))
                    for e, (half, other) in enumerate(halves):
                        nc.vector.tensor_tensor(qs[other, slot, e, :], ring_d.bank(n)[half, :], qs[half, slot, e, :].bitcast(F32),
                                                ALU.subtract).then_inc((stack_ready, ring_d.free)[e].sem, 1)
                    n = du["k", p]
                    dve.wait_ge(proj_hi.sem, proj_hi.at(i, 4 * p + 4))
                    for e, (half, other) in enumerate(halves):
                        nc.vector.tensor_copy(ks[other, slot, e, :],
                                              ks[half, slot, e, :].bitcast(F32)).then_inc(stack_ready.sem, 1)
                    for e, (half, other) in enumerate(halves):
                        nc.vector.tensor_tensor(kl[half, slot, e, :], ring_d.bank(n)[half, :], ks[half, slot, e, :].bitcast(F32),
                                                ALU.subtract).then_inc((stack_ready, ring_d.free)[e].sem, 1)
                    dve.wait_ge(ring_d.free.sem, ring_d.free.at(i, n + 1))
                    for e, (half, other) in enumerate(halves):
                        nc.vector.tensor_copy(kl[other, slot, e, :],
                                              kl[half, slot, e, :].bitcast(F32)).then_inc(stack_ready.sem, 1)
                if 2 <= step <= NP1 + 1:
                    p = step - 2
                    for e in range(2):
                        n = du["pv", p, e]
                        dve.wait_ge(ring_d.full.sem, ring_d.arrived(i, n))
                        bank = ring_d.bank(n)[:, 0:NT * (HD1 + 1)].rearrange("p (t r) -> p t r", t=NT)
                        nc.vector.reciprocal(rden[:, e, :].unsqueeze(2), bank[:, :, HD1:HD1 + 1]).then_inc(rden_ready.sem, 1)
                        dve.wait_ge(rden_ready.sem, rden_ready.at(i, 2 * p + e + 1))
                        nc.vector.tensor_tensor(att[:, p % 2, :, 64 * e:64 * e + 64], bank[:, :, 0:HD1],
                                                     rden[:, e, :].unsqueeze(2).broadcast_to([P, NT, HD1]), ALU.mult).then_inc(ring_d.free.sem, 1)
                if step >= 3:
                    low(i, tu["att", step - 3], attT[1][:, step - 3, :], attT[0][:, step - 3, :])
            post = lambda name: (lambda t: ring_d.bank(du[name, t // 2])[:, (t % 2) * D:(t % 2 + 1) * D])
            for b in range(2):
                dve.wait_ge(ring_d.full.sem, ring_d.arrived(i, du["o", b]))
            norm.statistics(dve, i, 1, post("o"), EPS)
            dve.wait_ge(norm.rstd_ready.sem, norm.rstd_ready.at(i, 2))
            for t in range(NT):
                ins = norm.apply(xn[:, t, :], post("o")(t), t)
                ins.then_inc(ring_d.free.sem, 1) if t % 2 else ins.then_inc(normed.sem, 1)
            dve.wait_ge(normed.sem, normed.at(i, NT // 2))
            dve.wait_ge(ring_d.free.sem, ring_d.free.at(i, du["o", 1] + 1))
            nc.vector.tensor_tensor(x3[:], xin[:], xn[:], ALU.add).then_inc(x3_ready.sem, 1)
            dve.wait_ge(x3_ready.sem, x3_ready.at(i, 1))
            norm.statistics(dve, i, 2, lambda t: x3[:, t, :], EPS)
            dve.wait_ge(norm.rstd_ready.sem, norm.rstd_ready.at(i, 3))
            for t in range(NT):
                norm.apply(xn[:, t, :], x3[:, t, :], t).then_inc(xn_ready.sem, 1)
            for c in range(NC):
                n = tu["x3", c]
                dve.wait_ge(ring_t.full.sem, ring_t.arrived(i, n))
                nc.vector.tensor_copy(xs[:, c, 1:T + 1], ring_t.bank(n)).then_inc(ring_t.free.sem, 1)
                dve.wait_ge(ring_t.free.sem, ring_t.free.at(i, n + 1))
                nc.vector.tensor_tensor(dx[:, c, :], xs[:, c, 1:T + 1], xs[:, c, 0:T], ALU.subtract).then_inc(dx_ready.sem, 1)
                dve.wait_ge(dx_ready.sem, dx_ready.at(i, c + 1))
                for k in range(2):
                    nc.vector.scalar_tensor_tensor(out=mix[k][:, c, :], in0=dx[:, c, :], scalar=mu[:, k, c:c + 1],
                                                   in1=xs[:, c, 0:T], op0=ALU.mult, op1=ALU.add).then_inc(mix_ready.sem, 1)
                for k, dst in enumerate((mixr, mixk)):
                    dve.wait_ge(mix_hi.sem, mix_hi.at(i, 2 * c + k + 1))
                    nc.vector.tensor_tensor(dst[1][:, c, :], mix[k][:, c, :], dst[0][:, c, :].bitcast(F32),
                                            ALU.subtract).then_inc(mix_split.sem, 1)
            for b in range(2):
                n = du["r", b]
                dve.wait_ge(ring_d.full.sem, ring_d.arrived(i, n))
                nc.vector.tensor_copy(sig_r[:, 2 * b:2 * b + 2, :].rearrange("p t d -> p (t d)"), ring_d.bank(n)).then_inc(ring_d.free.sem, 1)
            for c in range(NC):
                n = du["key", c]
                dve.wait_ge(ring_d.full.sem, ring_d.arrived(i, n))
                nc.vector.tensor_scalar(relu[:, c, :], ring_d.bank(n), 0.0, None, ALU.max).then_inc(ring_d.free.sem, 1)
                dve.wait_ge(ring_d.free.sem, ring_d.free.at(i, n + 1))
                nc.vector.tensor_tensor(relu[:, c, :], relu[:, c, :], relu[:, c, :], ALU.mult).then_inc(sq_ready.sem, 1)
            for c in range(NC):
                dve.wait_ge(kact_hi.sem, kact_hi.at(i, c + 1))
                nc.vector.tensor_tensor(kact[1][:, c, :], relu[:, c, :], kact[0][:, c, :].bitcast(F32),
                                        ALU.subtract).then_inc(kact_split.sem, 1)
            for b in range(2):
                n = du["out", b]
                dve.wait_ge(gate_ready.sem, gate_ready.at(i, b + 1))
                dve.wait_ge(ring_d.full.sem, ring_d.arrived(i, n))
                nc.vector.scalar_tensor_tensor(out=xn[:, 2 * b:2 * b + 2, :].rearrange("p t d -> p (t d)"),
                                                    in0=sig_r[:, 2 * b:2 * b + 2, :].rearrange("p t d -> p (t d)"), scalar=1.0,
                                                    in1=ring_d.bank(n), op0=ALU.add, op1=ALU.mult).then_inc(ring_d.free.sem, 1)
            dve.wait_ge(ring_d.free.sem, ring_d.free.at(i, du["out", 1] + 1))
            norm.statistics(dve, i, 3, lambda t: xn[:, t, :], 4 * EPS)
            dve.wait_ge(norm.rstd_ready.sem, norm.rstd_ready.at(i, 4))
            for t in range(NT):
                norm.apply(xn[:, t, :], xn[:, t, :], t).then_inc(normed.sem, 1)
            dve.wait_ge(normed.sem, normed.at(i, NT // 2 + NT))
            if not first:
                dve.wait_ge(x_stored.sem, x_stored.at(i, 0))
            nc.vector.tensor_tensor(x4[:], x3[:], xn[:], ALU.add).then_inc(x4_ready.sem, 1)

        body(0, first=True)
        with dve.Fori(1, BATCH) as i:
            body(i)

    @block.tensor
    def _(pe):
        pe.wait_ge(consts, 2)
        pe.wait_ge(w_sems[2], len(plan))

        def transposes(i, n, src, ready=lambda t: None):
            pe.wait_ge(ring_t.free.sem, ring_t.claim(i, n))
            for t in range(NT):
                ready(t)
                last = nc.tensor.transpose(ring_t.bank(n)[:, t * P:(t + 1) * P], src(t), ident[:])
            last.then_inc(ring_t.full.sem, 1)

        def body(i):
            for c in range(NC):
                transposes(i, tu["x", c], lambda t: xn[:, t, c * P:(c + 1) * P], lambda t: pe.wait_ge(xn_ready.sem, xn_ready.at(i, t + 1)))
            pe.wait_ge(ring_t.free.sem, ring_t.free.at(i, NC))
            for t in range(NT):
                for b in range(2):
                    n = du["v", t, b]
                    pe.wait_ge(ring_d.free.sem, ring_d.claim(i, n))
                    token_major(nc, ring_d.bank(n), xT, wv, t, slice(b * 512, b * 512 + 512), NC).then_inc(ring_d.full.sem, 1)
            for step in range(NP1 + 3):
                if step < NP1:
                    for name, w in (("q", wq), ("k", wk)):
                        n = du[name, step]
                        pe.wait_ge(ring_d.free.sem, ring_d.claim(i, n))
                        width_major(nc, ring_d.bank(n), xT, w, slice(step * P, (step + 1) * P), NC).then_inc(ring_d.full.sem, 1)
                if 1 <= step <= NP1:
                    p, slot = step - 1, (step - 1) % 2
                    pe.wait_ge(stack_ready.sem, stack_ready.at(i, 6 * p + 6))
                    for u in range(UNITS):
                        n = su["score", p, u]
                        pe.wait_ge(ring_s.free.sem, ring_s.claim(i, n))
                        for e in range(2):
                            for kt in range(NT):
                                unit, c0, c1 = unit_cols(e, kt)
                                if unit == u:
                                    out = ring_s.bank(n)[:, c0:c1]
                                    nc.tensor.matmul(out, ks[:, slot, e, kt * P:(kt + 1) * P], qs[:, slot, e, kt * P:T],
                                                     start=True, stop=False)
                                    last = nc.tensor.matmul(out, kl[:, slot, e, kt * P:(kt + 1) * P], qs[:, slot, e, kt * P:T],
                                                            start=False, stop=True)
                        last.then_inc(ring_s.full.sem, 1)
                if 2 <= step <= NP1 + 1:
                    p = step - 2
                    pe.wait_ge(masked.sem, masked.at(i, 3 * p + 3))
                    for e in range(2):
                        n = du["pv", p, e]
                        pe.wait_ge(ring_d.free.sem, ring_d.claim(i, n))
                        for qt in range(NT):
                            out = ring_d.bank(n)[:, qt * (HD1 + 1):(qt + 1) * (HD1 + 1)]
                            for kt in range(qt + 1):
                                u, c0, c1 = unit_cols(e, kt)
                                at = c0 + (qt - kt) * P
                                last = nc.tensor.matmul(out, probs[:, p % 2, u, at:at + P], v1[:, kt, 2 * p + e, :],
                                                        start=(kt == 0), stop=(kt == qt))
                        last.then_inc(ring_d.full.sem, 1)
                if step >= 3:
                    p = step - 3
                    pe.wait_ge(ring_d.free.sem, ring_d.free.at(i, du["pv", p, 1] + 1))
                    transposes(i, tu["att", p], lambda t: att[:, p % 2, t, :])
            pe.wait_ge(ring_t.free.sem, ring_t.free.at(i, tu["att", NP1 - 1] + 1))
            for b in range(2):
                n = du["o", b]
                pe.wait_ge(ring_d.free.sem, ring_d.claim(i, n))
                for t in (2 * b, 2 * b + 1):
                    last = token_major(nc, ring_d.bank(n)[:, (t % 2) * D:(t % 2 + 1) * D], attT, wo, t, slice(0, D), NP1)
                last.then_inc(ring_d.full.sem, 1)
            for c in range(NC):
                transposes(i, tu["x3", c], lambda t: xn[:, t, c * P:(c + 1) * P], lambda t: pe.wait_ge(xn_ready.sem, xn_ready.at(i, NT + t + 1)))
            pe.wait_ge(mix_split.sem, mix_split.at(i, 4))
            for b in range(2):
                n = du["r", b]
                pe.wait_ge(ring_d.free.sem, ring_d.claim(i, n))
                for t in (2 * b, 2 * b + 1):
                    last = token_major(nc, ring_d.bank(n)[:, (t % 2) * D:(t % 2 + 1) * D], mixr, wrkv, t, slice(0, D), NC)
                last.then_inc(ring_d.full.sem, 1)
            for c in range(NC):
                n = du["key", c]
                pe.wait_ge(ring_d.free.sem, ring_d.claim(i, n))
                width_major(nc, ring_d.bank(n), mixk, wrkv, slice(D + c * P, D + (c + 1) * P), NC).then_inc(ring_d.full.sem, 1)
            pe.wait_ge(kact_split.sem, kact_split.at(i, 2))
            for b in range(2):
                n = du["out", b]
                pe.wait_ge(ring_d.free.sem, ring_d.claim(i, n))
                for t in (2 * b, 2 * b + 1):
                    last = token_major(nc, ring_d.bank(n)[:, (t % 2) * D:(t % 2 + 1) * D], kact, wrkv, t, slice(2 * D, 3 * D), NC)
                last.then_inc(ring_d.full.sem, 1)

        with pe.Fori(0, BATCH) as i:
            body(i)


def kernel(**inputs):
    import concourse.bacc as bacc
    from concourse.bass_utils import run_bass_kernel_spmd

    x = {k: np.asarray(v) for k, v in inputs.items()}
    theta = (1.0 / np.float32(10000.0) ** (np.arange(0, HD0, 2, dtype=np.float32) / HD0)).astype(np.float32)
    angle = np.arange(1, T + 1, dtype=np.float32)[:, None] * theta[None, :]
    cos, sin = np.cos(angle), np.sin(angle)
    arrays = {
        "x": x["L0_attn_x"],
        "wqkv": np.concatenate([x["L0_attn_Wq"].T, x["L0_attn_Wk"].T, x["L0_attn_Wv"].T], axis=1),
        "b_qkv": np.concatenate([x["L0_attn_bq"], x["L0_attn_bk"], x["L0_attn_bv"]]),
        "wo": x["L0_attn_Wo"].T, "b_o": x["L0_attn_bo"],
        "cos": np.concatenate([cos, cos], axis=1), "sin": np.concatenate([-sin, sin], axis=1),
        "wgu": np.concatenate([x["L0_ffn_w_gate"].T, x["L0_ffn_w_up"].T], axis=1), "wd": x["L0_ffn_w_down"].T,
        "wq1": x["L1_attn_Wq"].T, "wk1": x["L1_attn_Wk"].T, "wv1": x["L1_attn_Wv"].T, "wo1": x["L1_attn_Wo"].T,
        "wrkv": np.concatenate([x["L1_ffn_W_r"].T, x["L1_ffn_W_k"].T, x["L1_ffn_W_v"].T], axis=1),
        "mu": np.stack([x["L1_ffn_mu_r"], x["L1_ffn_mu_k"]]).reshape(2, NC, P).transpose(2, 0, 1),
    }
    arrays = {f"in_{k}": np.ascontiguousarray(v) for k, v in arrays.items()}
    nc = bacc.Bacc("TRN2", target_bir_lowering=False, num_devices=1)
    a = {k[3:]: nc.dram_tensor(k, v.shape, mybir.dt.from_np(v.dtype), kind="ExternalInput").ap() for k, v in arrays.items()}
    a["out"] = nc.dram_tensor("out_x", (BATCH, T, D), F32, kind="ExternalOutput").ap()
    program(nc, a)
    return run_bass_kernel_spmd(nc, [arrays], core_ids=[0]).results[0]["out_x"]
```

```python
import numpy as np
import concourse.bass as bass
from concourse import mybir
from contextlib import ExitStack

F32 = mybir.dt.float32
F32R = mybir.dt.float32r
I32 = mybir.dt.int32
BF16 = mybir.dt.bfloat16
ALU = mybir.AluOpType
ACT = mybir.ActivationFunctionType

BATCH, T, D = 8, 512, 256
P = 128
NT = T // P
NC = D // P
EPS = 1e-5
BANK = 512

H0, HD0 = 16, 16
ROW0 = 64
KMAX = 3 * HD0
HID = 768
NM = HID // P
WSCALE = 1.0 / 127.0

H1, HD1 = 16, 64
F1 = H1 * HD1
NP1 = H1 // 2
CLAMP = 50.0

PAIRS = 8
PSLOTS = 3
UNITS = 5
MASKED = -1.0e30


class Signal:

    def __init__(self, sem, per, before=0):
        self.sem, self.per, self.before = sem, per, before

    def at(self, i, n):
        return i * self.per + n + self.before


class Ring:

    def __init__(self, banks, full, free, before=0):
        self.banks, self.full, self.free = banks, full, free
        full.before, free.before = before, before + len(banks)

    def bank(self, n):
        return self.banks[n % len(self.banks)]

    def claim(self, i, n):
        return self.free.at(i, n - len(self.banks) + 1)

    def arrived(self, i, n):
        return self.full.at(i, n + 1)


def unit_cols(e, kt):
    if kt == 0:
        return 2 * e, 0, 512
    if kt == 1:
        return 2 * e + 1, 0, 384
    if kt == 3:
        return 2 * e + 1, 384, 512
    return 4, 256 * e, 256 * e + 256


def split_terms(hi, lo, whi, wlo):
    return ((hi, whi), (lo, whi), (hi, wlo))


def uses(names):
    return {name: n for n, name in enumerate(names)}


def hold(nc, holder, ones):
    nc.gpsimd.tensor_tensor(holder, ones[:, 0:1], ones[:, 1:2], ALU.mult)


def mask_pair(pool, nc, probs, done):
    for part in (probs[:, :, 0:P], probs[:, 1:4:2, 384:512], probs[:, 4:5, 256:384]):
        n = part.shape[1]
        nc.gpsimd.affine_select(out=part, in_=part, compare_op=ALU.is_ge, fill=0.0, base=0,
                                pattern=[[0, n], [1, P]], channel_multiplier=-1).then_inc(done.sem, 1)


def program(nc, a):
    x_mid = nc.dram_tensor("x_mid", (BATCH, T, D), F32, kind="Internal").ap()
    tok = lambda ap, i: ap[i].rearrange("(t p) d -> p t d", p=P)
    with ExitStack() as ctx:
        psum = ctx.enter_context(nc.psum_tensor("psum", [P, 8, BANK], F32))
        banks = [psum[:, b, :] for b in range(8)]
        ident = ctx.enter_context(nc.sbuf_tensor("ident", [P, P], F32))
        expo = ctx.enter_context(nc.sbuf_tensor("expo", [P, NT], F32))
        block = ctx.enter_context(nc.Block())
        with ExitStack() as memory:
            tail = phase1(nc, block, ctx, memory, a, x_mid, tok, banks, ident, expo)
        with ExitStack() as memory:
            phase2(nc, block, ctx, memory, a, x_mid, tok, banks, ident, expo, tail)


class Weights:

    def __init__(self, nc, sem, plan, staging):
        self.nc, self.plan, self.staging, self.slots = nc, plan, staging, len(staging)
        self.loaded = [sem(f"w_loaded{n}") for n in range(self.slots)]
        self.high_done, self.low_done = sem("w_hi"), sem("w_lo")

    def raw(self, n):
        src, _, _, integer = self.plan[n]
        dst = self.staging[n % self.slots][:, :src.shape[1]]
        return dst.bitcast(I32) if integer else dst

    def load(self, sp, n):
        if n >= self.slots:
            sp.wait_ge(self.low_done, n - self.slots + 1)
        sp.dma_start(self.raw(n), self.plan[n][0]).then_inc(self.loaded[n % self.slots], 16)

    def high(self, act, n):
        act.wait_ge(self.loaded[n % self.slots], 16 * (n // self.slots + 1))
        self.nc.scalar.activation(self.plan[n][1], self.raw(n), ACT.Copy).then_inc(self.high_done, 1)

    def low(self, dve, n):
        dve.wait_ge(self.high_done, n + 1)
        self.nc.vector.tensor_tensor(self.plan[n][2], self.raw(n), self.plan[n][1].bitcast(F32),
                                     ALU.subtract).then_inc(self.low_done, 1)


class Norm:

    def __init__(self, nc, sb, sig, expo, name, count):
        self.nc, self.expo = nc, expo
        self.stats = sb(name + "_stats", [P, NT, 6])
        self.mv = sb(name + "_mv", [P, NT, 2])
        self.veps = sb(name + "_veps", [P, NT])
        self.rstd = sb(name + "_rstd", [P, NT])
        self.holder = sb(name + "_holder", [P, 1])
        self.stats_ready = sig(name + "_stats_ready", count * NT)
        self.mv_ready = sig(name + "_mv_ready", count * NT)
        self.var_ready = sig(name + "_var_ready", count)
        self.rstd_ready = sig(name + "_rstd_ready", count)

    def statistics(self, dve, i, n, src, eps):
        nc = self.nc
        for t in range(NT):
            nc.vector.bn_stats(self.stats[:, t, :], src(t)).then_inc(self.stats_ready.sem, 1)
        dve.wait_ge(self.stats_ready.sem, self.stats_ready.at(i, (n + 1) * NT))
        nc.vector.memset(self.holder[:], 0.0)
        for t in range(NT):
            nc.vector.bn_aggr(self.mv[:, t, :], self.stats[:, t, :]).then_inc(self.mv_ready.sem, 1)
        dve.wait_ge(self.mv_ready.sem, self.mv_ready.at(i, (n + 1) * NT))
        nc.vector.tensor_scalar(self.veps[:], self.mv[:, :, 1], eps, None,
                                ALU.add).then_inc(self.var_ready.sem, 1)

    def gpsimd(self, pool, i, n):
        pool.wait_ge(self.var_ready.sem, self.var_ready.at(i, n + 1))
        self.nc.gpsimd.tensor_tensor(self.rstd[:], self.veps[:], self.expo[:],
                                     ALU.pow).then_inc(self.rstd_ready.sem, 1)

    def apply(self, out, src, t):
        return self.nc.vector.tensor_scalar(out, src, self.mv[:, t, 0:1], self.rstd[:, t:t + 1],
                                            ALU.subtract, ALU.mult)


def product(nc, out, terms, chunks):
    todo = [(l, r, c) for c in range(chunks) for l, r in terms]
    for k, (l, r, c) in enumerate(todo):
        last = nc.tensor.matmul(out, l(c), r(c), start=(k == 0), stop=(k == len(todo) - 1))
    return last


def token_major(nc, out, x, w, t, cols, chunks):
    return product(nc, out, [(lambda c, p=p: p[:, c, t * P:(t + 1) * P], lambda c, q=q: q[:, c, cols])
                             for p, q in split_terms(*x, *w)], chunks)


def width_major(nc, out, x, w, cols, chunks):
    return product(nc, out, [(lambda c, q=q: q[:, c, cols], lambda c, p=p: p[:, c, :])
                             for p, q in split_terms(*x, *w)], chunks)


def phase1(nc, block, ctx, memory, a, x_mid, tok, banks, ident, expo):
    def sb(name, shape, dt=F32):
        return memory.enter_context(nc.sbuf_tensor("l0_" + name, shape, dt))

    def sbr(name, shape, dt=F32):
        return memory.enter_context(nc.sbuf_tensor("l0_" + name, shape, dt, side="right"))

    def sem(name):
        return ctx.enter_context(nc.semaphore("l0_" + name))

    def sig(name, per):
        return Signal(sem(name), per)

    wqkv = [sb("wqkv" + s, [P, NC, 3 * D], F32R) for s in ("_hi", "_lo")]
    wo = [sbr("wo" + s, [P, NC, D], F32R) for s in ("_hi", "_lo")]
    wgu = [sbr("wgu" + s, [P, NC, 2 * HID], F32R) for s in ("_hi", "_lo")]
    wd = [sbr("wd" + s, [P, NM, D], F32R) for s in ("_hi", "_lo")]
    b_qkv = sb("b_qkv", [P, 3 * D])
    b_o = sbr("b_o", [P, D])
    cos = sb("cos", [P, NT, HD0])
    sin = sb("sin", [P, NT, HD0])
    causal = sb("causal", [P, P], BF16)
    identb = sb("identb", [P, P], BF16)
    identr = sb("identr", [P, P], F32R)
    xin = sb("xin", [P, NT, D])
    stackq = sb("stackq", [P, 2, H0 * ROW0], F32R)
    stackk = sb("stackk", [P, 2, H0 * ROW0], F32R)
    qT = sb("qT", [P, PAIRS, T], F32R)
    kT = sb("kT", [P, PAIRS, T], F32R)
    v0 = sb("v0", [P, NT, H0, 32])
    rowmax = sb("rowmax", [P, NT, H0])
    maxT = sb("maxT", [4, 2, T], F32R)
    outT = sb("outT", [P, T])
    rden = sb("rden", [P, NT, 4])
    att = sbr("att", [P, NT, D])
    yT = [sbr("yT" + s, [P, NC, T], F32R) for s in ("_hi", "_lo")]
    xn = sbr("xn", [P, NT, D])
    x1 = sbr("x1", [P, NT, D])
    gated = sbr("gated", [P, 2, T])
    hid = sbr("hid", [P, 2, T])
    pool_holder = sb("pool_holder", [P, PAIRS])
    dve_holder = sb("dve_holder", [P, len(banks)])
    act_holder = sb("act_holder", [P, len(banks)])
    norm_x = Norm(nc, sb, sig, expo, "x", 1)
    norm_f = Norm(nc, sbr, sig, expo, "f", 3)
    with nc.sbuf_tensor("l0_staging", [P, 2 * NM, T], F32, side="right") as raw:
        pass
    hT = [sbr("hT" + s, [P, NM, T], F32R) for s in ("_hi", "_lo")]
    slots = 2 * NM * T // HID
    staging = [raw[:].rearrange("p a b -> p (a b)")[:, s * HID:(s + 1) * HID] for s in range(slots)]
    with nc.sbuf_tensor("l0_probs", [P, PSLOTS, UNITS, BANK], F32) as probs:
        pass
    qkb = sb("qkb", [P, NT, 2 * D])
    rot = sb("rot", [P, 2, 2 * D])
    rop = sb("rop", [P, NT, 2 * D])
    xT = [sb("xT" + s, [P, NC, T], F32R) for s in ("_hi", "_lo")]
    sb("probs_rest", [P, PSLOTS * UNITS * BANK - (4 + 4 * NT) * D - 2 * NC * T])

    front = [("qk", 0), ("qk", 1), ("bias", 0), ("bias", 1), ("att_T", 0), ("att_T", 1), ("rope", 0), ("parts", 0), ("qk", 2),
             ("bias", 2), ("rope", 1), ("qk", 3), ("parts", 1), ("bias", 3), ("rope", 2), ("o", 0), ("rope", 3), ("o", 1),
             ("stack", 0), ("parts", 2), ("v", 0), ("stack", 1), ("parts", 3), ("o_stats",), ("stack", 2), ("o_norm",),
             ("stack", 3), ("x1_stats",)]
    fill = [[] for _ in range(H0)]
    fill[0] = [("v", 1), ("x1_norm",)]
    fill[1] = [("x1_T", 0), ("x1_T", 1), ("v_bias", 0)]
    fill[3] = [("v_bias", 1)]
    for m in range(NM):
        fill[2 * m + 2] += [("gate", m)]
        fill[2 * m + 3] += [("gated", m), ("up", m)]
        fill[2 * m + 4] += [("hidden", m)]
        fill[min(2 * m + 5, H0 - 1)] += [("hidden_parts", m)]
    heads = []
    for step in range(4):
        for j in range(4):
            scores = [("score", 2 * (step - 1) + j - 2, u) for u in range(UNITS)] if j >= 2 and step >= 1 else []
            heads += [("max", 4 * step + j)]
            heads += scores[0:3]
            heads += [("maxT", step - 1)] if j == 0 and step >= 1 else []
            heads += fill[4 * step + j]
            heads += [("pv", step - 2)] if j == 1 and step >= 2 else []
            heads += [("outT", step - 2)] if j == 3 and step >= 2 else []
            heads += scores[3:5]
    last = [[("score", p, u) for u in range(UNITS)] for p in (6, 7)]
    heads += [("maxT", 3), ("x_stats",), ("down", 0), ("pv", 2), ("x_norm",)]
    heads += last[0][0:3] + [("down", 1), ("outT", 2)] + last[0][3:5] + last[1][0:3] + [("down", 2)] + last[1][3:5]
    heads += [("down", 3), ("x2_stats",), ("pv", 3), ("outT", 3)]
    loads = [("load", n) for n in range(NC, 2 * NC + 2 * NC + NM)]
    for n in range(0, len(loads), 2):
        front[7 + 2 * n:7 + 2 * n] = loads[n:n + 2]
    order = front + heads + [("x_T", t) for t in range(NT)] + [("x2_norm",), ("loaded",)]
    ffn = {"att_T", "o", "o_stats", "o_norm", "x1_stats", "x1_norm", "x1_T", "gate", "up", "gated", "hidden", "hidden_parts",
           "down", "x2_stats", "x2_norm"}
    first = {"x_stats", "x_norm", "x_T"}
    loading = {"load", "loaded"}
    attention = {name for name, *_ in order} - ffn - first - loading

    def run(pieces, stages):
        for name, *k in order:
            for names, i in stages:
                if name in names and name in pieces:
                    pieces[name](i, *k)

    def program(eng, pieces):
        run(pieces, [(first, 0)])
        run(pieces, [(first, 1), (attention, 0), (loading, 0)])
        with eng.Fori(1, BATCH - 1) as i:
            run(pieces, [(first, i + 1), (attention, i), (ffn, i - 1)])
        run(pieces, [(attention, BATCH - 1), (ffn, BATCH - 2)])
        tail_pieces[eng.engine] = pieces

    tail_pieces = {}

    d_names, s_names, e_names = [], [], []
    for name, *k in order:
        if name in ("x_T", "pv", "outT"):
            d_names.append((name, *k))
        elif name == "max":
            d_names += [("max", *k, b) for b in range(3)]
        elif name == "stack":
            s_names += [("stack", *k, which, half) for which in ("q", "k") for half in range(2)]
        elif name == "maxT":
            s_names.append(("maxT", *k))
        elif name in ("qk", "v", "score"):
            s_names.append((name, *k))
        elif name in ("att_T", "x1_T", "o", "gate", "up"):
            e_names.append((name, *k))
        elif name == "down" and k[0] % 2 == 0:
            e_names.append(("down", k[0] // 2))
    du, su, eu = uses(d_names), uses(s_names), uses(e_names)
    ring_d = Ring(banks[0:3], sig("d_full", len(du)), sig("d_free", len(du)), before=NT)
    ring_s = Ring(banks[3:6], sig("s_full", len(su)), sig("s_free", len(su)))
    ring_e = Ring(banks[6:8], sig("e_full", len(eu)), sig("e_free", len(eu)))
    max_tiles = (((0, 0), (1, P)), ((2, 0),), ((3, 0),))
    assert all(len(u) % len(r.banks) == 0 for u, r in ((du, ring_d), (su, ring_s), (eu, ring_e)))
    x_loaded = sig("x_loaded", 16)
    res_loaded = sig("res_loaded", 16)
    x_stored = sig("x_stored", 16)
    xn_ready = sig("xn_ready", NT)
    xT_hi = sig("xT_hi", NT)
    yn_ready = sig("yn_ready", NT)
    yT_hi = sig("yT_hi", 2 * NC)
    x1_ready = sig("x1_ready", 1)
    x2_ready = Signal(sem("x2_ready"), 1, before=1)
    biased = sig("biased", NT)
    v_biased = sig("v_biased", 2)
    rope_cos = sig("rope_cos", NT)
    rot_ready = sig("rot_ready", 2 * NT)
    rop_ready = sig("rop_ready", NT)
    stack_hi = sig("stack_hi", 2 * NT)
    stack_ready = sig("stack_ready", 2 * NT)
    first_max = sig("first_max", H0)
    max_placed = sig("max_placed", 64 * 4)
    masked = sig("masked", 3 * PAIRS)
    rden_ready = sig("rden_ready", 4)
    normed = sig("normed", NT + NT // 2)
    th_ready = sig("th_ready", NM)
    hid_hi = sig("hid_hi", NM)
    hid_split = sig("hid_split", NM)

    c_loaded = sem("c_loaded")
    consts = sem("consts")
    identr_ready = sem("identr_ready")
    plan = []
    for c in range(NC):
        plan.append((a["wqkv"][c * P:(c + 1) * P, :], wqkv[0][:, c, :], wqkv[1][:, c, :], False))
    for c in range(NC):
        plan.append((a["wo"][c * P:(c + 1) * P, :], wo[0][:, c, :], wo[1][:, c, :], False))
    for c in range(NC):
        for g in range(2):
            cols = slice(g * HID, (g + 1) * HID)
            plan.append((a["wgu"][c * P:(c + 1) * P, cols], wgu[0][:, c, cols], wgu[1][:, c, cols], True))
    for m in range(NM):
        plan.append((a["wd"][m * P:(m + 1) * P, :], wd[0][:, m, :], wd[1][:, m, :], True))
    weights = Weights(nc, sem, plan, staging)

    @block.sync
    def _(sp):
        sp.dma_start(xin[:], tok(a["x"], 0)).then_inc(x_loaded.sem, 16)
        for n in range(len(plan)):
            weights.load(sp, n)

        def maxima(i):
            for g in range(4):
                sp.wait_ge(ring_s.free.sem, ring_s.free.at(i, su["maxT", g] + 1))
                for j in range(4):
                    row = ROW0 * (j % 2) + KMAX
                    sp.dma_start(qT[row:row + 1, 2 * g + j // 2, :].bitcast(F32),
                                 maxT[j:j + 1, g % 2, :].bitcast(F32)).then_inc(max_placed.sem, 16)

        def next_x(i):
            sp.wait_ge(ring_d.full.sem, ring_d.arrived(i - 1, du["x_T", NT - 1]))
            sp.dma_start(xin[:], tok(a["x"], i + 1)).then_inc(x_loaded.sem, 16)

        def store(i):
            sp.wait_ge(x2_ready.sem, x2_ready.at(i, 1))
            sp.dma_start(tok(x_mid, i), x1[:]).then_inc(x_stored.sem, 16)

        def residual(i, first=False):
            if not first:
                sp.wait_ge(x_stored.sem, x_stored.at(i, 0))
            sp.dma_start(x1[:], tok(a["x"], i)).then_inc(res_loaded.sem, 16)

        next_x(0)
        maxima(0)
        residual(0, first=True)
        with sp.Fori(1, BATCH - 1) as i:
            next_x(i)
            maxima(i)
            store(i - 1)
            residual(i)
        maxima(BATCH - 1)
        store(BATCH - 2)
        residual(BATCH - 1)
        tail_pieces[sp.engine] = {"attended": lambda: sp.wait_ge(ring_d.full.sem, ring_d.arrived(BATCH - 1, du["outT", 3])),
                                  "store": lambda: store(BATCH - 1),
                                  "stored": lambda: sp.wait_ge(x_stored.sem, x_stored.at(BATCH, 0))}

    @block.gpsimd
    def _(pool):
        nc.gpsimd.memset(ident[:], 0.0).then_inc(consts, 1)
        nc.gpsimd.memset(causal[:], 0.0).then_inc(consts, 1)
        nc.gpsimd.memset(identb[:], 0.0).then_inc(consts, 1)
        nc.gpsimd.memset(expo[:], -0.5).then_inc(consts, 1)
        nc.gpsimd.memset(v0[:], 1.0).then_inc(consts, 1)
        nc.gpsimd.memset(stackq[:].bitcast(F32), 0.0).then_inc(consts, 1)
        nc.gpsimd.memset(stackk[:].bitcast(F32), 0.0).then_inc(consts, 1)
        pool.wait_ge(consts, 7)
        for eye in (ident, identb):
            nc.gpsimd.affine_select(out=eye[:], in_=eye[:], compare_op=ALU.not_equal, fill=1.0, base=0,
                                    pattern=[[-1, P]], channel_multiplier=1).then_inc(consts, 1)
        nc.gpsimd.affine_select(out=causal[:], in_=causal[:], compare_op=ALU.is_ge, fill=MASKED, base=0,
                                pattern=[[-1, P]], channel_multiplier=1).then_inc(consts, 1)
        ones = stackk[:].rearrange("p s (h r) -> p (s h) r", r=ROW0)[:, :, KMAX:KMAX + 1]
        nc.gpsimd.memset(ones.bitcast(F32), 1.0).then_inc(consts, 1)
        nc.gpsimd.memset(pool_holder[:, 0:1], 0.0).then_inc(x2_ready.sem, 1)
        pool.wait_ge(c_loaded, 64)

        def bias(i, t):
            pool.wait_ge(biased.sem, biased.at(i, t + 1))
            if t >= 2:
                pool.wait_ge(rop_ready.sem, rop_ready.at(i, t - 1))
            x = qkb[:, t, :].rearrange("p (h e r) -> p h e r", e=2, r=HD0 // 2)
            r = rot[:, t % 2, :].rearrange("p (h e r) -> p h e r", e=2, r=HD0 // 2)
            for e in range(2):
                s = sin[:, t, 8 * e:8 * e + 8].unsqueeze(1).broadcast_to([P, 2 * H0, 8])
                nc.gpsimd.tensor_tensor(r[:, :, e, :], x[:, :, 1 - e, :], s, ALU.mult).then_inc(rot_ready.sem, 1)

        def parts(i, t):
            pool.wait_ge(stack_hi.sem, stack_hi.at(i, 2 * t + 2))
            for k, (stack, lo) in enumerate(((stackq, 1), (stackk, 2))):
                st = stack[:, t % 2, :].rearrange("p (h r) -> p h r", r=ROW0)
                full = rop[:, t, k * D:(k + 1) * D].rearrange("p (h r) -> p h r", r=HD0)
                nc.gpsimd.tensor_tensor(st[:, :, lo * HD0:(lo + 1) * HD0], full,
                                        st[:, :, 0:HD0].bitcast(F32), ALU.subtract).then_inc(stack_ready.sem, 1)

        def score(i, p, u):
            if u == UNITS - 1:
                pool.wait_ge(ring_s.free.sem, ring_s.free.at(i, su["score", p, u] + 1))
                hold(nc, pool_holder[:, p:p + 1], expo)
                mask_pair(pool, nc, probs[:, p % PSLOTS, :, :], masked)

        def hidden(i, m):
            pool.wait_ge(hid_hi.sem, hid_hi.at(i, m + 1))
            nc.gpsimd.tensor_tensor(hT[1][:, m, :], hid[:, m % 2, :], hT[0][:, m, :].bitcast(F32),
                                    ALU.subtract).then_inc(hid_split.sem, 1)

        def x2(i):
            pool.wait_ge(normed.sem, normed.at(i, NT + NT // 2))
            pool.wait_ge(ring_e.free.sem, ring_e.free.at(i, eu["down", 1] + 1))
            nc.gpsimd.tensor_tensor(x1[:], x1[:], xn[:], ALU.add).then_inc(x2_ready.sem, 1)

        program(pool, {
            "x_stats": lambda i: norm_x.gpsimd(pool, i, 0), "bias": bias, "parts": parts, "score": score,
            "o_stats": lambda i: norm_f.gpsimd(pool, i, 0), "x1_stats": lambda i: norm_f.gpsimd(pool, i, 1),
            "hidden_parts": hidden, "x2_stats": lambda i: norm_f.gpsimd(pool, i, 2), "x2_norm": x2})
        tail_pieces[pool.engine]["hidden_done"] = lambda: pool.wait_ge(hid_split.sem, hid_split.at(BATCH, 0))

    @block.scalar
    def _(act):
        act.dma_start(b_qkv[:], a["b_qkv"].partition_broadcast(P)).then_inc(c_loaded, 16)
        act.dma_start(b_o[:], a["b_o"].partition_broadcast(P)).then_inc(c_loaded, 16)
        act.dma_start(cos[:], a["cos"].rearrange("(t p) r -> p t r", p=P)).then_inc(c_loaded, 16)
        act.dma_start(sin[:], a["sin"].rearrange("(t p) r -> p t r", p=P)).then_inc(c_loaded, 16)
        for n in range(NC):
            weights.high(act, n)
        act.wait_ge(consts, 11)
        nc.scalar.activation(identr[:], ident[:], ACT.Copy).then_inc(identr_ready, 1)
        for b in range(len(ring_s.banks)):
            nc.scalar.activation(act_holder[:, b:b + 1], expo[:, 0:1], ACT.Copy).then_inc(ring_s.free.sem, 1)

        def x_T(i, t):
            n = du["x_T", t]
            act.wait_ge(ring_d.full.sem, ring_d.arrived(i - 1, n))
            nc.scalar.activation(xT[0][:, :, t * P:(t + 1) * P],
                                 ring_d.bank(n)[:, 0:NC * P].rearrange("p (c q) -> p c q", c=NC),
                                 ACT.Copy).then_inc(xT_hi.sem, 1)

        def qk(i, t):
            n = su["qk", t]
            act.wait_ge(ring_s.full.sem, ring_s.arrived(i, n))
            nc.scalar.activation(qkb[:, t, :], ring_s.bank(n), ACT.Copy).then_inc(ring_s.free.sem, 1)

        def v(i, b):
            n = su["v", b]
            act.wait_ge(ring_s.full.sem, ring_s.arrived(i, n))
            nc.scalar.activation(v0[:, 2 * b:2 * b + 2, :, 0:HD0].rearrange("p t h r -> p (t h) r"),
                                 ring_s.bank(n).rearrange("p (h r) -> p h r", r=HD0), ACT.Copy).then_inc(ring_s.free.sem, 1)

        def parts(i, t):
            act.wait_ge(rop_ready.sem, rop_ready.at(i, t + 1))
            if t >= 2:
                act.wait_ge(ring_s.full.sem, ring_s.arrived(i, su["stack", t - 2, "k", 1]))
            for k, (stack, step) in enumerate(((stackq, 2), (stackk, 1))):
                st = stack[:, t % 2, :].rearrange("p (h s r) -> p h s r", s=ROW0 // HD0, r=HD0)
                full = rop[:, t, k * D:(k + 1) * D].rearrange("p (h r) -> p h r", r=HD0)
                nc.scalar.activation(st[:, :, 0:step + 1:step, :],
                                     full.unsqueeze(2).broadcast_to([P, H0, 2, HD0]),
                                     ACT.Copy).then_inc(stack_hi.sem, 1)

        def stack(i, t):
            for k, dst in (("q", qT), ("k", kT)):
                for half in range(2):
                    n = su["stack", t, k, half]
                    act.wait_ge(ring_s.full.sem, ring_s.arrived(i, n))
                    nc.scalar.activation(dst[:, 4 * half:4 * half + 4, t * P:(t + 1) * P],
                                         ring_s.bank(n).rearrange("p (a b) -> p a b", b=P),
                                         ACT.Copy).then_inc(ring_s.free.sem, 1)

        def row_max(i, g):
            n = su["maxT", g]
            act.wait_ge(ring_s.full.sem, ring_s.arrived(i, n))
            nc.scalar.activation(maxT[:, g % 2, :], ring_s.bank(n)[0:4, :], ACT.Copy,
                                 scale=-1.0).then_inc(ring_s.free.sem, 1)

        def score(i, p, u):
            if u == 0 and p >= PSLOTS:
                act.wait_ge(ring_d.full.sem, ring_d.arrived(i, du["pv", (p - PSLOTS) // 2]))
            n = su["score", p, u]
            act.wait_ge(ring_s.full.sem, ring_s.arrived(i, n))
            nc.scalar.activation(probs[:, p % PSLOTS, u, :], ring_s.bank(n), ACT.Exp,
                                 scale=HD0 ** -0.5).then_inc(ring_s.free.sem, 1)

        def y_T(name):
            def high(i, c):
                n = eu[name, c]
                act.wait_ge(ring_e.full.sem, ring_e.arrived(i, n))
                nc.scalar.activation(yT[0][:, c, :], ring_e.bank(n), ACT.Copy).then_inc(yT_hi.sem, 1)
            return high

        def hidden_high(i, m):
            act.wait_ge(ring_e.free.sem, ring_e.free.at(i, eu["up", m] + 1))
            nc.scalar.activation(hT[0][:, m, :], hid[:, m % 2, :], ACT.Copy).then_inc(hid_hi.sem, 1)

        def gate(i, m):
            n = eu["gate", m]
            act.wait_ge(ring_e.full.sem, ring_e.arrived(i, n))
            if m >= 2:
                act.wait_ge(ring_e.free.sem, ring_e.free.at(i, eu["up", m - 2] + 1))
            nc.scalar.activation(gated[:, m % 2, :], ring_e.bank(n), ACT.Tanh,
                                 scale=0.5 * WSCALE).then_inc(th_ready.sem, 1)

        program(act, {"load": lambda i, n: weights.high(act, n), "x_T": x_T, "qk": qk, "v": v, "parts": parts, "stack": stack,
                      "maxT": row_max, "score": score,
                      "att_T": y_T("att_T"), "x1_T": y_T("x1_T"), "gate": gate, "hidden_parts": hidden_high})

    @block.vector
    def _(dve):
        for n in range(NC):
            weights.low(dve, n)
        dve.wait_ge(c_loaded, 64)
        dve.wait_ge(consts, 11)

        for b in range(len(ring_d.banks)):
            nc.vector.memset(dve_holder[:, b:b + 1], 0.0).then_inc(ring_d.free.sem, 1)
        for b in range(len(ring_d.banks), len(ring_d.banks) + len(ring_e.banks)):
            nc.vector.memset(dve_holder[:, b:b + 1], 0.0).then_inc(ring_e.free.sem, 1)

        def x_stats(i):
            dve.wait_ge(x_loaded.sem, x_loaded.at(i, 16))
            norm_x.statistics(dve, i, 0, lambda t: xin[:, t, :], EPS)

        def x_norm(i):
            dve.wait_ge(norm_x.rstd_ready.sem, norm_x.rstd_ready.at(i, 1))
            for t in range(NT):
                norm_x.apply(xin[:, t, :], xin[:, t, :], t).then_inc(xn_ready.sem, 1)

        def x_T(i, t):
            n = du["x_T", t]
            dve.wait_ge(xT_hi.sem, xT_hi.at(i, t + 1))
            cols = slice(t * P, (t + 1) * P)
            nc.vector.tensor_tensor(xT[1][:, :, cols], ring_d.bank(n)[:, 0:NC * P].rearrange("p (c q) -> p c q", c=NC),
                                    xT[0][:, :, cols].bitcast(F32), ALU.subtract).then_inc(ring_d.free.sem, 1)

        def bias(i, t):
            dve.wait_ge(ring_s.free.sem, ring_s.free.at(i, su["qk", t] + 1))
            nc.vector.tensor_tensor(qkb[:, t, :], qkb[:, t, :], b_qkv[:, 0:2 * D], ALU.add).then_inc(biased.sem, 1)
            dve.wait_ge(biased.sem, biased.at(i, t + 1))
            c16 = cos[:, t, :].unsqueeze(1).broadcast_to([P, 2 * H0, HD0])
            nc.vector.tensor_tensor(rop[:, t, :].rearrange("p (h r) -> p h r", r=HD0),
                                    qkb[:, t, :].rearrange("p (h r) -> p h r", r=HD0),
                                    c16, ALU.mult).then_inc(rope_cos.sem, 1)

        def v_bias(i, b):
            dve.wait_ge(ring_s.free.sem, ring_s.free.at(i, su["v", b] + 1))
            values = v0[:, 2 * b:2 * b + 2, :, 0:HD0]
            bias_v = b_qkv[:, 2 * D:3 * D].rearrange("p (h r) -> p h r", r=HD0)
            nc.vector.tensor_tensor(values, values, bias_v.unsqueeze(1).broadcast_to([P, 2, H0, HD0]),
                                    ALU.add).then_inc(v_biased.sem, 1)

        def rope(i, t):
            dve.wait_ge(rot_ready.sem, rot_ready.at(i, 2 * t + 2))
            dve.wait_ge(rope_cos.sem, rope_cos.at(i, t + 1))
            nc.vector.tensor_tensor(rop[:, t, :], rop[:, t, :], rot[:, t % 2, :], ALU.add).then_inc(rop_ready.sem, 1)

        def row_max(i, h):
            for b, tiles in enumerate(max_tiles):
                n = du["max", h, b]
                dve.wait_ge(ring_d.full.sem, ring_d.arrived(i, n))
                for t, c0 in tiles:
                    nc.vector.tensor_reduce(rowmax[:, t, h:h + 1], ring_d.bank(n)[:, c0:c0 + (t + 1) * P],
                                            mybir.AxisListType.X, ALU.max).then_inc((ring_d.free if t else first_max).sem, 1)

        def pv(i, g):
            n = du["pv", g]
            dve.wait_ge(ring_d.full.sem, ring_d.arrived(i, n))
            nc.vector.tensor_copy(outT[:], ring_d.bank(n)).then_inc(ring_d.free.sem, 1)

        def out_T(i, g):
            n = du["outT", g]
            dve.wait_ge(ring_d.full.sem, ring_d.arrived(i, n))
            view = ring_d.bank(n).rearrange("p (t j r) -> p t j r", t=NT, r=32)
            nc.vector.reciprocal(rden[:].unsqueeze(3), view[:, :, :, HD0:HD0 + 1]).then_inc(rden_ready.sem, 1)
            dve.wait_ge(rden_ready.sem, rden_ready.at(i, g + 1))
            dst = att[:, :, 64 * g:64 * g + 64].rearrange("p t (j r) -> p t j r", r=HD0)
            nc.vector.tensor_tensor(dst, view[:, :, :, 0:HD0], rden[:].unsqueeze(3).broadcast_to([P, NT, 4, HD0]),
                                    ALU.mult).then_inc(ring_d.free.sem, 1)

        def y_T(name):
            def low(i, c):
                n = eu[name, c]
                dve.wait_ge(yT_hi.sem, yT_hi.at(i, (0 if name == "att_T" else NC) + c + 1))
                nc.vector.tensor_tensor(yT[1][:, c, :], ring_e.bank(n), yT[0][:, c, :].bitcast(F32),
                                        ALU.subtract).then_inc(ring_e.free.sem, 1)
            return low

        def o(i, b):
            n = eu["o", b]
            dve.wait_ge(ring_e.full.sem, ring_e.arrived(i, n))
            if b == 0:
                dve.wait_ge(x2_ready.sem, x2_ready.at(i, 0))
            nc.vector.tensor_tensor(xn[:, 2 * b:2 * b + 2, :], ring_e.bank(n).rearrange("p (t d) -> p t d", d=D),
                                    b_o[:].unsqueeze(1).broadcast_to([P, 2, D]), ALU.add).then_inc(ring_e.free.sem, 1)

        def o_stats(i):
            dve.wait_ge(ring_e.free.sem, ring_e.free.at(i, eu["o", 1] + 1))
            norm_f.statistics(dve, i, 0, lambda t: xn[:, t, :], EPS)

        def o_norm(i):
            dve.wait_ge(norm_f.rstd_ready.sem, norm_f.rstd_ready.at(i, 1))
            for t in range(NT):
                norm_f.apply(xn[:, t, :], xn[:, t, :], t).then_inc(normed.sem, 1)
            dve.wait_ge(normed.sem, normed.at(i, NT))
            dve.wait_ge(res_loaded.sem, res_loaded.at(i, 16))
            nc.vector.tensor_tensor(x1[:], x1[:], xn[:], ALU.add).then_inc(x1_ready.sem, 1)

        def x1_stats(i):
            dve.wait_ge(x1_ready.sem, x1_ready.at(i, 1))
            norm_f.statistics(dve, i, 1, lambda t: x1[:, t, :], EPS)

        def x1_norm(i):
            dve.wait_ge(norm_f.rstd_ready.sem, norm_f.rstd_ready.at(i, 2))
            for t in range(NT):
                norm_f.apply(xn[:, t, :], x1[:, t, :], t).then_inc(yn_ready.sem, 1)

        def gate(i, m):
            dve.wait_ge(th_ready.sem, th_ready.at(i, m + 1))
            nc.vector.scalar_tensor_tensor(out=gated[:, m % 2, :], in0=gated[:, m % 2, :], scalar=1.0,
                                           in1=ring_e.bank(eu["gate", m]), op0=ALU.add,
                                           op1=ALU.mult).then_inc(ring_e.free.sem, 1)

        def hidden(i, m):
            n = eu["up", m]
            dve.wait_ge(ring_e.full.sem, ring_e.arrived(i, n))
            if m >= 2:
                dve.wait_ge(hid_split.sem, hid_split.at(i, m - 1))
            dve.wait_ge(ring_e.free.sem, ring_e.free.at(i, eu["gate", m] + 1))
            nc.vector.tensor_tensor(hid[:, m % 2, :], ring_e.bank(n), gated[:, m % 2, :], ALU.mult).then_inc(ring_e.free.sem, 1)

        unit = 2.0 / WSCALE ** 3
        half = lambda t: ring_e.bank(eu["down", t // 2])[:, (t % 2) * D:(t % 2 + 1) * D]

        def x2_stats(i):
            dve.wait_ge(ring_e.full.sem, ring_e.arrived(i, eu["down", 1]))
            norm_f.statistics(dve, i, 2, half, EPS * unit * unit)

        def x2_norm(i):
            dve.wait_ge(norm_f.rstd_ready.sem, norm_f.rstd_ready.at(i, 3))
            for t in range(NT):
                norm_f.apply(xn[:, t, :], half(t), t).then_inc((normed, ring_e.free)[t % 2].sem, 1)

        program(dve, {
            "load": lambda i, n: weights.low(dve, n), "x_stats": x_stats, "x_norm": x_norm, "x_T": x_T, "bias": bias, "v_bias": v_bias, "rope": rope, "max": row_max, "pv": pv,
            "outT": out_T, "att_T": y_T("att_T"), "x1_T": y_T("x1_T"), "o": o, "o_stats": o_stats, "o_norm": o_norm,
            "x1_stats": x1_stats, "x1_norm": x1_norm, "gated": gate, "hidden": hidden,
            "x2_stats": x2_stats, "x2_norm": x2_norm})

    @block.tensor
    def _(pe):
        pe.wait_ge(consts, 11)
        pe.wait_ge(identr_ready, 1)
        pe.wait_ge(weights.low_done, NC)

        def x_T(i, t):
            n = du["x_T", t]
            pe.wait_ge(ring_d.free.sem, ring_d.claim(i - 1, n))
            pe.wait_ge(xn_ready.sem, xn_ready.at(i, t + 1))
            for c in range(NC):
                last = nc.tensor.transpose(ring_d.bank(n)[:, c * P:(c + 1) * P], xin[:, t, c * P:(c + 1) * P], ident[:])
            last.then_inc(ring_d.full.sem, 1)

        def qk(i, t):
            n = su["qk", t]
            pe.wait_ge(ring_d.free.sem, ring_d.free.at(i - 1, du["x_T", t] + 1))
            pe.wait_ge(ring_s.free.sem, ring_s.claim(i, n))
            token_major(nc, ring_s.bank(n), xT, wqkv, t, slice(0, 2 * D), NC).then_inc(ring_s.full.sem, 1)

        def v(i, b):
            n = su["v", b]
            pe.wait_ge(ring_s.free.sem, ring_s.claim(i, n))
            for t in (2 * b, 2 * b + 1):
                last = token_major(nc, ring_s.bank(n)[:, (t % 2) * D:(t % 2 + 1) * D], xT, wqkv, t, slice(2 * D, 3 * D), NC)
            last.then_inc(ring_s.full.sem, 1)

        def stack(i, t):
            pe.wait_ge(stack_ready.sem, stack_ready.at(i, 2 * t + 2))
            for k, st in (("q", stackq), ("k", stackk)):
                for half in range(2):
                    n = su["stack", t, k, half]
                    pe.wait_ge(ring_s.free.sem, ring_s.claim(i, n))
                    for b in range(4):
                        p = 4 * half + b
                        last = nc.tensor.matmul(ring_s.bank(n)[:, b * P:(b + 1) * P], st[:, t % 2, p * P:(p + 1) * P], identr[:],
                                                start=True, stop=True)
                    last.then_inc(ring_s.full.sem, 1)

        def row_max(i, h):
            if h == 0:
                pe.wait_ge(ring_s.free.sem, ring_s.free.at(i, su["stack", NT - 1, "k", 1] + 1))
            rows = slice(ROW0 * (h % 2), ROW0 * (h % 2) + KMAX)
            for b, tiles in enumerate(max_tiles):
                n = du["max", h, b]
                pe.wait_ge(ring_d.free.sem, ring_d.claim(i, n))
                for t, c0 in tiles:
                    nc.tensor.matmul(ring_d.bank(n)[:, c0:c0 + (t + 1) * P], qT[rows, h // 2, t * P:(t + 1) * P],
                                     kT[rows, h // 2, 0:(t + 1) * P], start=True, stop=False)
                    last = nc.tensor.matmul(ring_d.bank(n)[:, c0 + t * P:c0 + (t + 1) * P], identb[:], causal[:],
                                            start=False, stop=True)
                last.then_inc(ring_d.full.sem, 1)

        def max_T(i, g):
            n = su["maxT", g]
            pe.wait_ge(ring_s.free.sem, ring_s.claim(i, n))
            pe.wait_ge(first_max.sem, first_max.at(i, 4 * g + 4))
            pe.wait_ge(ring_d.free.sem, ring_d.free.at(i, du["max", 4 * g + 3, 2] + 1))
            for t in range(NT):
                last = nc.tensor.transpose(ring_s.bank(n)[0:4, t * P:(t + 1) * P], rowmax[:, t, 4 * g:4 * g + 4], ident[:])
            last.then_inc(ring_s.full.sem, 1)

        def score(i, p, u):
            if u == 0:
                pe.wait_ge(max_placed.sem, max_placed.at(i, 64 * (p // 2 + 1)))
            n = su["score", p, u]
            pe.wait_ge(ring_s.free.sem, ring_s.claim(i, n))
            rows = slice(ROW0 * (p % 2), ROW0 * (p % 2) + KMAX + 1)
            for e in range(2):
                at = 2 * (p // 2) + e
                for kt in range(NT):
                    unit, c0, c1 = unit_cols(e, kt)
                    if unit == u:
                        last = nc.tensor.matmul(ring_s.bank(n)[:, c0:c1], kT[rows, at, kt * P:(kt + 1) * P],
                                                qT[rows, at, kt * P:T], start=True, stop=True)
            last.then_inc(ring_s.full.sem, 1)

        def pv(i, g):
            n = du["pv", g]
            pe.wait_ge(ring_d.free.sem, ring_d.claim(i, n))
            pe.wait_ge(masked.sem, masked.at(i, 3 * (2 * g + 2)))
            for kt in range(NT):
                for j in range(4):
                    h = 4 * g + j
                    u, c0, c1 = unit_cols(j // 2, kt)
                    last = nc.tensor.matmul(ring_d.bank(n)[32 * j:32 * j + 32, kt * P:T], v0[:, kt, h, :],
                                            probs[:, (2 * g + j % 2) % PSLOTS, u, c0:c1], start=(kt == 0),
                                            stop=(kt == NT - 1), tile_position=(0, 32 * j))
            last.then_inc(ring_d.full.sem, 1)

        def out_T(i, g):
            n = du["outT", g]
            pe.wait_ge(ring_d.free.sem, ring_d.claim(i, n))
            pe.wait_ge(ring_d.free.sem, ring_d.free.at(i, du["pv", g] + 1))
            for t in range(NT):
                last = nc.tensor.transpose(ring_d.bank(n)[:, t * P:(t + 1) * P], outT[:, t * P:(t + 1) * P], ident[:])
            last.then_inc(ring_d.full.sem, 1)

        def y_T(name, src):
            def transposes(i, c):
                n = eu[name, c]
                pe.wait_ge(ring_e.free.sem, ring_e.claim(i, n))
                if name == "att_T":
                    pe.wait_ge(ring_d.free.sem, ring_d.free.at(i, du["outT", 3] + 1))
                else:
                    pe.wait_ge(yn_ready.sem, yn_ready.at(i, NT))
                for t in range(NT):
                    last = nc.tensor.transpose(ring_e.bank(n)[:, t * P:(t + 1) * P], src[:, t, c * P:(c + 1) * P], ident[:])
                last.then_inc(ring_e.full.sem, 1)
            return transposes

        def o(i, b):
            n = eu["o", b]
            pe.wait_ge(ring_e.free.sem, ring_e.claim(i, n))
            pe.wait_ge(ring_e.free.sem, ring_e.free.at(i, eu["att_T", NC - 1] + 1))
            for t in (2 * b, 2 * b + 1):
                last = token_major(nc, ring_e.bank(n)[:, (t % 2) * D:(t % 2 + 1) * D], yT, wo, t, slice(0, D), NC)
            last.then_inc(ring_e.full.sem, 1)

        def hidden_half(name, k):
            def products(i, m):
                n = eu[name, m]
                if name == "gate" and m == 0:
                    pe.wait_ge(ring_e.free.sem, ring_e.free.at(i, eu["x1_T", NC - 1] + 1))
                else:
                    pe.wait_ge(ring_e.free.sem, ring_e.claim(i, n))
                cols = slice(k * HID + m * P, k * HID + (m + 1) * P)
                width_major(nc, ring_e.bank(n), yT, wgu, cols, NC).then_inc(ring_e.full.sem, 1)
            return products

        def down(i, t):
            n = eu["down", t // 2]
            if t == 0:
                pe.wait_ge(hid_split.sem, hid_split.at(i, NM))
            if t % 2 == 0:
                pe.wait_ge(ring_e.free.sem, ring_e.claim(i, n))
            last = token_major(nc, ring_e.bank(n)[:, (t % 2) * D:(t % 2 + 1) * D], hT, wd, t, slice(0, D), NM)
            if t % 2:
                last.then_inc(ring_e.full.sem, 1)

        program(pe, {"loaded": lambda i: pe.wait_ge(weights.low_done, len(plan)), "x_T": x_T, "qk": qk, "v": v, "stack": stack,
                     "max": row_max, "maxT": max_T, "score": score, "pv": pv,
                     "outT": out_T, "att_T": y_T("att_T", att), "x1_T": y_T("x1_T", xn), "o": o, "gate": hidden_half("gate", 0),
                     "up": hidden_half("up", 1), "down": down})

    return [piece for piece in order if piece[0] in ffn], tail_pieces


def phase2(nc, block, ctx, memory, a, x_mid, tok, banks, ident, expo, tail):
    def sb(name, shape, dt=F32):
        return memory.enter_context(nc.sbuf_tensor("l1_" + name, shape, dt))

    def sbr(name, shape, dt=F32):
        return memory.enter_context(nc.sbuf_tensor("l1_" + name, shape, dt, side="right"))

    def sem(name):
        return ctx.enter_context(nc.semaphore("l1_" + name))

    def sig(name, per):
        return Signal(sem(name), per)

    wq = [sb("wq" + s, [P, NC, F1], F32R) for s in ("_hi", "_lo")]
    wk = [sb("wk" + s, [P, NC, F1], F32R) for s in ("_hi", "_lo")]
    wv = [sb("wv" + s, [P, NC, F1], F32R) for s in ("_hi", "_lo")]
    wo = [sb("wo" + s, [P, NP1, D], F32R) for s in ("_hi", "_lo")]
    wrkv = [sb("wrkv" + s, [P, NC, 3 * D], F32R) for s in ("_hi", "_lo")]
    mu = sb("mu", [P, 2, NC])
    xin = sb("xin", [P, NT, D])
    xT = [sb("xT" + s, [P, NC, T], F32R) for s in ("_hi", "_lo")]
    qs = sbr("qs", [P, 2, 2, T], F32R)
    ks = sbr("ks", [P, 2, 2, T], F32R)
    kl = sbr("kl", [P, 2, 2, T], F32R)
    v1 = sbr("v1", [P, NT, H1, HD1])
    ones = sb("ones", [P, HD1])
    probs = sb("probs", [P, 2, UNITS, BANK])
    keysum = sbr("keysum", [P, 2, 2, T - P])
    att = (sbr("att0", [P, T]), sb("att1", [P, T]))
    attT = [sbr("attT" + s, [P, 2, T], F32R) for s in ("_hi", "_lo")]
    xn = sbr("xn", [P, NT, D])
    x3 = sbr("x3", [P, NT, D])
    xs = sbr("xs", [P, NC, T + 1])
    dx = sbr("dx", [P, NC, T])
    mix = sbr("mix", [P, 2, T])
    mixk = [sbr("mixk" + s, [P, NC, T], F32R) for s in ("_hi", "_lo")]
    with ExitStack() as shared:
        mixr = [shared.enter_context(nc.sbuf_tensor("l1_mixr" + s, [P, NC, T], F32R, side="right")) for s in ("_hi", "_lo")]
    kact = [sbr("kact" + s, [P, NC, T], F32R) for s in ("_hi", "_lo")]
    sig_r = sbr("sig_r", [P, NT, D])
    relu = dx
    pool_holder = sb("pool_holder", [P, NP1])
    dve_holder = sb("dve_holder", [P, len(banks)])
    act_holder = sb("act_holder", [P, len(banks)])
    norm_x = Norm(nc, sb, sig, expo, "x", 1)
    norm_f = Norm(nc, sb, sig, expo, "f", 3)
    flat = probs[:].rearrange("p a b c -> p (a b c)")
    staging = [flat[:, s * F1:(s + 1) * F1] for s in range(2 * UNITS * BANK // F1)]

    values = [("v", t, b) for t in range(NT) for b in range(2)]
    order = [("den_last",), ("o_second_last",)] + values[0:1] + [("pv_last",)] + values[1:2] + [("q", 0)] + values[2:3] + [("k", 0)] + values[3:4]
    order += [("att_last",)] + values[4:6] + [("o_last",)] + [("o_stats",)]
    early = {3: [("x3_T", 0)], 6: [("r", 1)]}
    fill = {1: values[7:8] + [("o_norm",), ("x3_stats",)], 2: [("x3_norm",)], 3: [("x3_T", 1), ("mix", 0)], 4: [("mix", 1)],
            5: [("r", 0), ("x_stats",)], 6: [("key", 0), ("x_norm",)], 7: [("key", 1)]}
    for step in range(1, NP1 + 1):
        scores = [("score", step - 1, u) for u in range(UNITS)]
        projected = [("q", step), ("k", step)] if step < NP1 else []
        order += scores[0:2] + projected[0:1] + scores[2:4]
        order += [("kact", step - 7)] if step >= 7 else []
        order += [("att", step - 3)] if step >= 3 else []
        order += [("o", step - 4)] if step >= 4 else []
        order += early.get(step, [])
        order += projected[1:2] + (values[6:7] if step == 1 else []) + scores[4:5]
        order += fill.get(step, [])
        order += [("den", step - 2)] if step >= 2 else []
        order += [("pv", step - 2)] if step >= 2 else []
        order += [("out", 0)] if step == NP1 else []
    order += [("att", NP1 - 2), ("out", 1), ("x_T", 0), ("x_T", 1), ("x_T", 2), ("o", NP1 - 3), ("x_T", 3)]
    order += [("x4_stats",), ("x4_norm",)]
    mixing = {"o_second_last", "pv_last", "den_last", "att_last", "o_last", "o_stats", "o_norm", "x3_stats", "x3_norm", "x3_T",
              "mix", "r", "key", "kact", "out", "x4_stats", "x4_norm"}
    first = {"x_stats", "x_norm", "x_T"}
    attention = {name for name, *_ in order} - mixing - first

    def run(pieces, stages):
        for name, *k in order:
            for names, i in stages:
                if name in names and name in pieces:
                    pieces[name](i, *k)

    tail_order, tail_pieces = tail
    high = lambda *numbers: [("high", n) for n in numbers]
    low = lambda *numbers: [("low", n) for n in numbers]
    between = {("att_T", NC - 1): [("credit",)] + high(0, 1, 2, 3, 4), ("x1_T", 0): low(0), ("x1_T", NC - 1): low(1) + high(5, 6),
               ("hidden_parts", 0): low(2), ("hidden_parts", 1): low(3) + high(7), ("hidden_parts", 2): low(4) + high(8),
               ("hidden_parts", 3): low(5) + high(9), ("hidden_parts", 4): [("x_stats",)] + high(10),
               ("hidden_parts", 5): [("constants",), ("x_norm",)], ("down", 0): low(6, 7) + [("x_T", t) for t in range(NT)],
               ("down", 1): low(8, 9, 10) + high(11, 12, 13) + low(11, 12, 13) + high(14, 15) + low(14, 15)}

    def program(eng, pieces):
        for name, *k in tail_order:
            if name in tail_pieces[eng.engine]:
                tail_pieces[eng.engine][name](BATCH - 1, *k)
            for added, *k in between.get((name, *k), []):
                if added in pieces:
                    pieces[added](0, *k)
        if "ready" in pieces:
            pieces["ready"]()
        run(pieces, [(first, 1), (attention, 0)])
        with eng.Fori(1, BATCH - 1) as i:
            run(pieces, [(first, i + 1), (attention, i), (mixing, i - 1)])
        run(pieces, [(attention, BATCH - 1), (mixing, BATCH - 2)])
        run(pieces, [(mixing, BATCH - 1)])

    du = uses([u for u in order if u[0] in ("x_T", "q", "k", "pv", "den")] + [("den", NP1 - 1), ("pv", NP1 - 1)])
    s_uses = [u for u in order if u[0] in ("v", "score", "x3_T", "r", "key", "out")]
    s_uses += [("none",)] * (-len(s_uses) % 3)
    su = uses(s_uses)
    ou = uses([("o", 0), ("o", 1)])
    ring_d = Ring(banks[0:3], sig("d_full", len(du)), sig("d_free", len(du)), before=NT + 2)

    def skipped(i, name, k):
        if not isinstance(i, int):
            return 0
        return {(0, "x_T", NT - 1): 2, (BATCH - 1, "pv", NP1 - 2): NT}.get((i, name, k), 0)

    ring_s = Ring(banks[3:6], sig("s_full", len(s_uses)), sig("s_free", len(s_uses)))

    def counted(j, *use):
        count = 1
        following = [(j, name) for name, *_ in s_uses[su[use] + 1:]]
        if isinstance(j, int):
            following += [(j + 1, name) for name, *_ in s_uses]
        for it, name in following:
            if name == "none" or isinstance(it, int) and name in {0: mixing, BATCH: attention}.get(it, ()):
                count += 1
            else:
                break
        return count

    ring_o = Ring(banks[6:8], sig("o_full", len(ou)), sig("o_free", len(ou)))
    x_loaded = sig("x_loaded", 16)
    res_loaded = sig("res_loaded", 16)
    x_stored = sig("x_stored", 16)
    xn_ready = sig("xn_ready", NT)
    xT_hi = sig("xT_hi", NT)
    yn_ready = sig("yn_ready", NT)
    x3_ready = sig("x3_ready", 1)
    x4_ready = sig("x4_ready", 1)
    proj_hi = sig("proj_hi", 4 * NP1)
    k_twice = sig("k_twice", 2 * NP1)
    exped = sig("exped", 2 * NP1)
    masked = sig("masked", 3 * NP1)
    summed = sig("summed", 3 * NP1)
    attT_hi = sig("attT_hi", NP1)
    att_split = sig("att_split", NP1)
    att_used = sig("att_used", NP1 - 2)
    normed = sig("normed", NT // 2 + NT)
    dx_ready = sig("dx_ready", NC)
    mix_ready = sig("mix_ready", 2 * NC)
    mix_hi = sig("mix_hi", 2 * NC)
    mix_split = sig("mix_split", 2 * NC)
    gated = sig("gated", 2)
    sq_ready = sig("sq_ready", NC)
    kact_hi = sig("kact_hi", NC)
    kact_split = sig("kact_split", NC)
    c_loaded = sem("c_loaded")
    consts = sem("consts")
    plan = []
    for name, dst in (("wv1", wv), ("wq1", wq), ("wk1", wk), ("wrkv", wrkv)):
        for c in range(NC):
            plan.append((a[name][c * P:(c + 1) * P, :], dst[0][:, c, :], dst[1][:, c, :], False))
    for c in range(NP1):
        plan.append((a["wo1"][c * P:(c + 1) * P, :], wo[0][:, c, :], wo[1][:, c, :], False))
    weights = Weights(nc, sem, plan, staging)

    @block.sync
    def _(sp):
        tail_pieces[sp.engine]["attended"]()
        sp.dma_start(xin[:], tok(x_mid, 0)).then_inc(x_loaded.sem, 16)
        for n in range(len(plan)):
            weights.load(sp, n)
        tail_pieces[sp.engine]["store"]()
        tail_pieces[sp.engine]["stored"]()

        def next_x(i):
            sp.wait_ge(ring_d.full.sem, ring_d.arrived(i - 1, du["x_T", NT - 1]))
            sp.dma_start(xin[:], tok(x_mid, i + 1)).then_inc(x_loaded.sem, 16)

        def store(i):
            sp.wait_ge(x4_ready.sem, x4_ready.at(i, 1))
            sp.dma_start(tok(a["out"], i), x3[:]).then_inc(x_stored.sem, 16)

        def residual(i, first=False):
            if not first:
                sp.wait_ge(x_stored.sem, x_stored.at(i, 0))
            sp.dma_start(x3[:], tok(x_mid, i)).then_inc(res_loaded.sem, 16)

        next_x(0)
        residual(0, first=True)
        with sp.Fori(1, BATCH - 1) as i:
            next_x(i)
            store(i - 1)
            residual(i)
        store(BATCH - 2)
        residual(BATCH - 1)
        store(BATCH - 1)
        sp.wait_ge(x_stored.sem, x_stored.at(BATCH, 0))

    @block.gpsimd
    def _(pool):
        def score(i, p, u):
            if u == UNITS - 1:
                pool.wait_ge(exped.sem, exped.at(i, 2 * p + 2))
                hold(nc, pool_holder[:, p:p + 1], expo)
                mask_pair(pool, nc, probs[:, p % 2, :, :], masked)
                tile0, tile1 = probs[:, p % 2, 0:3:2, P:T], probs[:, p % 2, 1:4:2, 0:T - P]
                tile2 = probs[:, p % 2, 4, :].rearrange("p (e q) -> p e q", e=2)
                tile3 = probs[:, p % 2, 1:4:2, T - P:T]
                total = keysum[:, p % 2, :, :]
                if p >= 2:
                    pool.wait_ge(ring_d.full.sem, ring_d.arrived(i, du["den", p - 2]))
                pool.wait_ge(masked.sem, masked.at(i, 3 * p + 3))
                nc.gpsimd.tensor_tensor(total, tile0, tile1, ALU.add).then_inc(summed.sem, 1)
                pool.wait_ge(summed.sem, summed.at(i, 3 * p + 1))
                nc.gpsimd.tensor_tensor(total[:, :, P:3 * P], total[:, :, P:3 * P], tile2, ALU.add).then_inc(summed.sem, 1)
                pool.wait_ge(summed.sem, summed.at(i, 3 * p + 2))
                nc.gpsimd.tensor_tensor(total[:, :, 2 * P:3 * P], total[:, :, 2 * P:3 * P], tile3, ALU.add).then_inc(summed.sem, 1)

        def att_low(i, p):
            pool.wait_ge(attT_hi.sem, attT_hi.at(i, p + 1))
            nc.gpsimd.tensor_tensor(attT[1][:, p % 2, :], att[p % 2][:], attT[0][:, p % 2, :].bitcast(F32),
                                    ALU.subtract).then_inc(att_split.sem, 1)

        def mixed(i, c):
            for k, dst in enumerate((mixr, mixk)):
                pool.wait_ge(mix_hi.sem, mix_hi.at(i, 2 * c + k + 1))
                nc.gpsimd.tensor_tensor(dst[1][:, c, :], mix[:, k, :], dst[0][:, c, :].bitcast(F32),
                                        ALU.subtract).then_inc(mix_split.sem, 1)

        def key(i, c):
            pool.wait_ge(kact_hi.sem, kact_hi.at(i, c + 1))
            nc.gpsimd.tensor_tensor(kact[1][:, c, :], relu[:, c, :], kact[0][:, c, :].bitcast(F32),
                                    ALU.subtract).then_inc(kact_split.sem, 1)

        def constants(i):
            tail_pieces[pool.engine]["hidden_done"]()
            nc.gpsimd.memset(ones[:], 1.0).then_inc(consts, 1)
            nc.gpsimd.memset(kl[:].bitcast(F32), 0.0).then_inc(consts, 1)
            nc.gpsimd.memset(xs[:, :, 0:1], 0.0).then_inc(consts, 1)

        program(pool, {
            "constants": constants, "x_stats": lambda i: norm_x.gpsimd(pool, i, 0), "score": score, "att": att_low,
            "att_last": lambda i: att_low(i, NP1 - 1),
            "o_stats": lambda i: norm_f.gpsimd(pool, i, 0), "x3_stats": lambda i: norm_f.gpsimd(pool, i, 1),
            "mix": mixed, "kact": key, "x4_stats": lambda i: norm_f.gpsimd(pool, i, 2)})

    @block.scalar
    def _(act):
        def credit(i):
            act.dma_start(mu[:], a["mu"]).then_inc(c_loaded, 16)
            for b in range(len(ring_s.banks)):
                nc.scalar.activation(act_holder[:, b:b + 1], expo[:, 0:1], ACT.Copy).then_inc(ring_s.free.sem, 1)

        def x_T(i, t):
            n = du["x_T", t]
            act.wait_ge(ring_d.full.sem, ring_d.arrived(i - 1, n))
            nc.scalar.activation(xT[0][:, :, t * P:(t + 1) * P],
                                 ring_d.bank(n)[:, 0:NC * P].rearrange("p (c q) -> p c q", c=NC),
                                 ACT.Copy).then_inc(xT_hi.sem, 1)

        def v(i, t, b):
            n = su["v", t, b]
            act.wait_ge(ring_s.full.sem, ring_s.arrived(i, n))
            nc.scalar.activation(v1[:, t, 8 * b:8 * b + 8, 0:HD1], ring_s.bank(n).rearrange("p (h r) -> p h r", r=HD1),
                                 ACT.Copy).then_inc(ring_s.free.sem, counted(i, "v", t, b))

        def projected(name, dst):
            def high(i, p):
                n = du[name, p]
                act.wait_ge(ring_d.full.sem, ring_d.arrived(i, n))
                for e in range(2):
                    half = slice(64 * e, 64 * e + 64)
                    nc.scalar.activation(dst[half, p % 2, e, :], ring_d.bank(n)[half, :], ACT.Copy).then_inc(proj_hi.sem, 1)
            return high

        def score(i, p, u):
            if u == 0 and p >= 2:
                act.wait_ge(ring_d.full.sem, ring_d.arrived(i, du["pv", p - 2]))
            n = su["score", p, u]
            act.wait_ge(ring_s.full.sem, ring_s.arrived(i, n))
            nc.scalar.activation(probs[:, p % 2, u, :], ring_s.bank(n), ACT.Tanh,
                                 scale=HD1 ** -0.5 / CLAMP).then_inc(ring_s.free.sem, counted(i, "score", p, u))
            if u >= UNITS - 2:
                part = probs[:, p % 2, 0:3, :] if u == UNITS - 2 else probs[:, p % 2, 3:5, :]
                act.wait_ge(ring_s.free.sem, ring_s.free.at(i, su["score", p, 2 if u == UNITS - 2 else u] + 1))
                nc.scalar.activation(part, part, ACT.Exp, scale=CLAMP).then_inc(exped.sem, 1)

        def att_high(i, p):
            act.wait_ge(ring_d.free.sem, ring_d.free.at(i, du["pv", p] + 1))
            if p >= 2:
                act.wait_ge(att_used.sem, att_used.at(i, p - 1))
            nc.scalar.activation(attT[0][:, p % 2, :], att[p % 2][:], ACT.Copy).then_inc(attT_hi.sem, 1)

        def mixed(i, c):
            for k, dst in enumerate((mixr, mixk)):
                act.wait_ge(mix_ready.sem, mix_ready.at(i, 2 * c + k + 1))
                nc.scalar.activation(dst[0][:, c, :], mix[:, k, :], ACT.Copy).then_inc(mix_hi.sem, 1)

        def receptance(i, b):
            n = su["r", b]
            act.wait_ge(ring_s.full.sem, ring_s.arrived(i + 1, n))
            nc.scalar.activation(sig_r[:, 2 * b:2 * b + 2, :].rearrange("p t d -> p (t d)"), ring_s.bank(n), ACT.Tanh,
                                 scale=0.5).then_inc(ring_s.free.sem, counted(i + 1, "r", b))

        def x3_T(i, c):
            n = su["x3_T", c]
            act.wait_ge(ring_s.full.sem, ring_s.arrived(i + 1, n))
            nc.scalar.activation(xs[:, c, 1:T + 1], ring_s.bank(n), ACT.Copy).then_inc(ring_s.free.sem, counted(i + 1, "x3_T", c))

        def out(i, b):
            n = su["out", b]
            act.wait_ge(ring_s.full.sem, ring_s.arrived(i + 1, n))
            nc.scalar.activation(mix[:, b, :], ring_s.bank(n), ACT.Copy).then_inc(ring_s.free.sem, counted(i + 1, "out", b))

        def relu_key(i, c):
            n = su["key", c]
            act.wait_ge(ring_s.full.sem, ring_s.arrived(i + 1, n))
            nc.scalar.activation(relu[:, c, :], ring_s.bank(n), ACT.Relu).then_inc(ring_s.free.sem, counted(i + 1, "key", c))

        def key(i, c):
            act.wait_ge(sq_ready.sem, sq_ready.at(i, c + 1))
            nc.scalar.activation(kact[0][:, c, :], relu[:, c, :], ACT.Copy).then_inc(kact_hi.sem, 1)

        program(act, {"credit": credit, "high": lambda i, n: weights.high(act, n), "x_T": x_T, "v": v, "q": projected("q", qs),
                      "k": projected("k", ks), "score": score, "att": att_high,
                      "att_last": lambda i: att_high(i, NP1 - 1),
                      "x3_T": x3_T, "mix": mixed, "r": receptance, "key": relu_key, "kact": key, "out": out})

    @block.vector
    def _(dve):
        def credit(i):
            for b, ring in enumerate((ring_d, ring_d, ring_d, ring_o, ring_o)):
                nc.vector.memset(dve_holder[:, b:b + 1], 0.0).then_inc(ring.free.sem, 1)

        def ready():
            dve.wait_ge(c_loaded, 16)
            dve.wait_ge(consts, 3)

        def x_stats(i):
            dve.wait_ge(x_loaded.sem, x_loaded.at(i, 16))
            norm_x.statistics(dve, i, 0, lambda t: xin[:, t, :], EPS)

        def x_norm(i):
            dve.wait_ge(norm_x.rstd_ready.sem, norm_x.rstd_ready.at(i, 1))
            for t in range(NT):
                norm_x.apply(xin[:, t, :], xin[:, t, :], t).then_inc(xn_ready.sem, 1)

        def x_T(i, t):
            n = du["x_T", t]
            dve.wait_ge(xT_hi.sem, xT_hi.at(i, t + 1))
            cols = slice(t * P, (t + 1) * P)
            nc.vector.tensor_tensor(xT[1][:, :, cols], ring_d.bank(n)[:, 0:NC * P].rearrange("p (c q) -> p c q", c=NC),
                                    xT[0][:, :, cols].bitcast(F32), ALU.subtract).then_inc(ring_d.free.sem, 1 + skipped(i, "x_T", t))

        def q(i, p):
            n, slot = du["q", p], p % 2
            dve.wait_ge(proj_hi.sem, proj_hi.at(i, 4 * p + 2))
            for e in range(2):
                half, other = slice(64 * e, 64 * e + 64), slice(64 - 64 * e, 128 - 64 * e)
                low = nc.vector.tensor_tensor(qs[other, slot, e, :], ring_d.bank(n)[half, :], qs[half, slot, e, :].bitcast(F32),
                                              ALU.subtract)
            low.then_inc(ring_d.free.sem, 1)

        def k(i, p):
            n, slot = du["k", p], p % 2
            halves = [(slice(64 * e, 64 * e + 64), slice(64 - 64 * e, 128 - 64 * e)) for e in range(2)]
            dve.wait_ge(proj_hi.sem, proj_hi.at(i, 4 * p + 4))
            for e, (half, other) in enumerate(halves):
                low = nc.vector.tensor_tensor(kl[half, slot, e, :], ring_d.bank(n)[half, :], ks[half, slot, e, :].bitcast(F32),
                                              ALU.subtract)
            low.then_inc(ring_d.free.sem, 1)
            for e, (half, other) in enumerate(halves):
                nc.vector.tensor_copy(ks[other, slot, e, :], ks[half, slot, e, :].bitcast(F32)).then_inc(k_twice.sem, 1)

        def den(i, p):
            n = du["den", p]
            if p >= 2:
                dve.wait_ge(att_split.sem, att_split.at(i, p - 1))
            dve.wait_ge(ring_d.full.sem, ring_d.arrived(i, n))
            nc.vector.reciprocal(att[p % 2][:], ring_d.bank(n)).then_inc(ring_d.free.sem, 1)

        def pv(i, p):
            n = du["pv", p]
            dve.wait_ge(ring_d.free.sem, ring_d.free.at(i, n))
            dve.wait_ge(ring_d.full.sem, ring_d.arrived(i, n))
            nc.vector.tensor_tensor(att[p % 2][:], att[p % 2][:], ring_d.bank(n), ALU.mult).then_inc(ring_d.free.sem, 1 + skipped(i, "pv", p))

        o_half = lambda t: ring_o.bank(t // 2)[:, (t % 2) * D:(t % 2 + 1) * D]

        def o_stats(i):
            dve.wait_ge(ring_o.full.sem, ring_o.arrived(i, 1))
            norm_f.statistics(dve, i, 0, o_half, EPS)

        def o_norm(i):
            dve.wait_ge(norm_f.rstd_ready.sem, norm_f.rstd_ready.at(i, 1))
            for t in range(NT):
                norm_f.apply(xn[:, t, :], o_half(t), t).then_inc((normed, ring_o.free)[t % 2].sem, 1)
            dve.wait_ge(res_loaded.sem, res_loaded.at(i, 16))
            dve.wait_ge(normed.sem, normed.at(i, NT // 2))
            dve.wait_ge(ring_o.free.sem, ring_o.free.at(i, 2))
            nc.vector.tensor_tensor(x3[:], x3[:], xn[:], ALU.add).then_inc(x3_ready.sem, 1)

        def x3_stats(i):
            dve.wait_ge(x3_ready.sem, x3_ready.at(i, 1))
            norm_f.statistics(dve, i, 1, lambda t: x3[:, t, :], EPS)

        def x3_norm(i):
            dve.wait_ge(norm_f.rstd_ready.sem, norm_f.rstd_ready.at(i, 2))
            for t in range(NT):
                norm_f.apply(xn[:, t, :], x3[:, t, :], t).then_inc(yn_ready.sem, 1)

        def mixed(i, c):
            dve.wait_ge(ring_s.free.sem, ring_s.free.at(i + 1, su["x3_T", c] + 1))
            nc.vector.tensor_tensor(dx[:, c, :], xs[:, c, 1:T + 1], xs[:, c, 0:T], ALU.subtract).then_inc(dx_ready.sem, 1)
            dve.wait_ge(dx_ready.sem, dx_ready.at(i, c + 1))
            if c >= 1:
                dve.wait_ge(mix_split.sem, mix_split.at(i, 2 * c))
            for k in range(2):
                nc.vector.scalar_tensor_tensor(out=mix[:, k, :], in0=dx[:, c, :], scalar=mu[:, k, c:c + 1],
                                               in1=xs[:, c, 0:T], op0=ALU.mult, op1=ALU.add).then_inc(mix_ready.sem, 1)

        def key(i, c):
            dve.wait_ge(ring_s.free.sem, ring_s.free.at(i + 1, su["key", c] + 1))
            nc.vector.tensor_tensor(relu[:, c, :], relu[:, c, :], relu[:, c, :], ALU.mult).then_inc(sq_ready.sem, 1)

        def out(i, b):
            dve.wait_ge(ring_s.free.sem, ring_s.free.at(i + 1, su["out", b] + 1))
            nc.vector.scalar_tensor_tensor(out=xn[:, 2 * b:2 * b + 2, :].rearrange("p t d -> p (t d)"),
                                           in0=sig_r[:, 2 * b:2 * b + 2, :].rearrange("p t d -> p (t d)"), scalar=1.0,
                                           in1=mix[:, b, :], op0=ALU.add, op1=ALU.mult).then_inc(gated.sem, 1)

        def x4_stats(i):
            dve.wait_ge(gated.sem, gated.at(i, 2))
            norm_f.statistics(dve, i, 2, lambda t: xn[:, t, :], 4 * EPS)

        def x4_norm(i):
            dve.wait_ge(norm_f.rstd_ready.sem, norm_f.rstd_ready.at(i, 3))
            for t in range(NT):
                norm_f.apply(xn[:, t, :], xn[:, t, :], t).then_inc(normed.sem, 1)
            dve.wait_ge(normed.sem, normed.at(i, NT // 2 + NT))
            nc.vector.tensor_tensor(x3[:], x3[:], xn[:], ALU.add).then_inc(x4_ready.sem, 1)

        program(dve, {"credit": credit, "ready": ready, "low": lambda i, n: weights.low(dve, n), "x_stats": x_stats,
                      "x_norm": x_norm, "x_T": x_T, "q": q, "k": k, "den": den, "den_last": lambda i: den(i, NP1 - 1),
                      "pv": pv, "pv_last": lambda i: pv(i, NP1 - 1), "o_stats": o_stats, "o_norm": o_norm, "x3_stats": x3_stats, "x3_norm": x3_norm,
                      "mix": mixed, "key": key, "out": out, "x4_stats": x4_stats, "x4_norm": x4_norm})

    @block.tensor
    def _(pe):
        def ready():
            pe.wait_ge(consts, 3)
            pe.wait_ge(weights.low_done, len(plan))

        def x_T(i, t):
            n = du["x_T", t]
            pe.wait_ge(ring_d.free.sem, ring_d.claim(i - 1, n))
            pe.wait_ge(xn_ready.sem, xn_ready.at(i, t + 1))
            for c in range(NC):
                last = nc.tensor.transpose(ring_d.bank(n)[:, c * P:(c + 1) * P], xin[:, t, c * P:(c + 1) * P], ident[:])
            last.then_inc(ring_d.full.sem, 1 + skipped(i, "x_T", t))

        def v(i, t, b):
            n = su["v", t, b]
            if n == 0:
                pe.wait_ge(ring_d.free.sem, ring_d.free.at(i - 1, du["x_T", NT - 1] + 1))
            pe.wait_ge(ring_s.free.sem, ring_s.claim(i, n))
            token_major(nc, ring_s.bank(n), xT, wv, t, slice(b * BANK, (b + 1) * BANK), NC).then_inc(ring_s.full.sem, counted(i, "v", t, b))

        def projected(name, w):
            def products(i, p):
                n = du[name, p]
                pe.wait_ge(ring_d.free.sem, ring_d.claim(i, n))
                width_major(nc, ring_d.bank(n), xT, w, slice(p * P, (p + 1) * P), NC).then_inc(ring_d.full.sem, 1)
            return products

        def score(i, p, u):
            slot, n = p % 2, su["score", p, u]
            if u == 0:
                pe.wait_ge(k_twice.sem, k_twice.at(i, 2 * p + 2))
            pe.wait_ge(ring_s.free.sem, ring_s.claim(i, n))
            for e in range(2):
                for kt in range(NT):
                    unit, c0, c1 = unit_cols(e, kt)
                    if unit == u:
                        bank = ring_s.bank(n)[:, c0:c1]
                        nc.tensor.matmul(bank, ks[:, slot, e, kt * P:(kt + 1) * P], qs[:, slot, e, kt * P:T],
                                         start=True, stop=False)
                        last = nc.tensor.matmul(bank, kl[:, slot, e, kt * P:(kt + 1) * P], qs[:, slot, e, kt * P:T],
                                                start=False, stop=True)
            last.then_inc(ring_s.full.sem, counted(i, "score", p, u))

        def pv(i, p):
            n = du["pv", p]
            pe.wait_ge(masked.sem, masked.at(i, 3 * p + 3))
            pe.wait_ge(ring_d.free.sem, ring_d.claim(i, n))
            for kt in range(NT):
                for e in range(2):
                    u, c0, c1 = unit_cols(e, kt)
                    last = nc.tensor.matmul(ring_d.bank(n)[64 * e:64 * e + 64, kt * P:T], v1[:, kt, 2 * p + e, :],
                                            probs[:, p % 2, u, c0:c1], start=(kt == 0), stop=(kt == NT - 1),
                                            tile_position=(0, 64 * e))
            last.then_inc(ring_d.full.sem, 1 + skipped(i, "pv", p))

        def den(i, p):
            n = du["den", p]
            pe.wait_ge(summed.sem, summed.at(i, 3 * p + 3))
            pe.wait_ge(ring_d.free.sem, ring_d.claim(i, n))
            for cols in (slice(0, P), slice(P, T)):
                for e in range(2):
                    weights = keysum[:, p % 2, e, :] if cols.start else probs[:, p % 2, unit_cols(e, 0)[0], cols]
                    last = nc.tensor.matmul(ring_d.bank(n)[64 * e:64 * e + 64, cols], ones[:], weights,
                                            start=True, stop=True, tile_position=(0, 64 * e))
            last.then_inc(ring_d.full.sem, 1)

        def o(i, p):
            if p == 0:
                pe.wait_ge(ring_o.free.sem, ring_o.claim(i, 1))
            pe.wait_ge(att_split.sem, att_split.at(i, p + 1))
            for t in range(NT):
                terms = split_terms(*attT, *wo)
                for k, (l, r) in enumerate(terms):
                    ends = p == NP1 - 1 and t % 2 == 1 and k == len(terms) - 1
                    last = nc.tensor.matmul(ring_o.bank(t // 2)[:, (t % 2) * D:(t % 2 + 1) * D],
                                            l[:, p % 2, t * P:(t + 1) * P], r[:, p, :],
                                            start=(p == 0 and t % 2 == 0 and k == 0), stop=ends)
                if ends:
                    last.then_inc(ring_o.full.sem, 1)
            if p < NP1 - 2:
                last.then_inc(att_used.sem, 1)

        def x3_T(i, c):
            n = su["x3_T", c]
            pe.wait_ge(ring_s.free.sem, ring_s.claim(i + 1, n))
            pe.wait_ge(yn_ready.sem, yn_ready.at(i, NT))
            for t in range(NT):
                last = nc.tensor.transpose(ring_s.bank(n)[:, t * P:(t + 1) * P], xn[:, t, c * P:(c + 1) * P], ident[:])
            last.then_inc(ring_s.full.sem, counted(i + 1, "x3_T", c))

        def tokens(name, x, cols, ready, count):
            def products(i, b):
                n = su[name, b]
                pe.wait_ge(ring_s.free.sem, ring_s.claim(i + 1, n))
                pe.wait_ge(ready.sem, ready.at(i, count))
                for t in (2 * b, 2 * b + 1):
                    last = token_major(nc, ring_s.bank(n)[:, (t % 2) * D:(t % 2 + 1) * D], x, wrkv, t, cols, NC)
                last.then_inc(ring_s.full.sem, counted(i + 1, name, b))
            return products

        def key(i, c):
            n = su["key", c]
            pe.wait_ge(ring_s.free.sem, ring_s.claim(i + 1, n))
            width_major(nc, ring_s.bank(n), mixk, wrkv, slice(D + c * P, D + (c + 1) * P), NC).then_inc(ring_s.full.sem, counted(i + 1, "key", c))

        program(pe, {"ready": ready, "x_T": x_T, "v": v, "q": projected("q", wq), "k": projected("k", wk), "score": score, "pv": pv,
                     "den": den, "pv_last": lambda i: pv(i, NP1 - 1), "den_last": lambda i: den(i, NP1 - 1),
                     "o": o, "o_second_last": lambda i: o(i, NP1 - 2), "o_last": lambda i: o(i, NP1 - 1), "x3_T": x3_T, "key": key,
                     "r": tokens("r", mixr, slice(0, D), mix_split, 2 * NC),
                     "out": tokens("out", kact, slice(2 * D, 3 * D), kact_split, NC)})


def kernel(**inputs):
    import concourse.bacc as bacc
    from concourse.bass_utils import run_bass_kernel_spmd

    x = {k: np.asarray(v) for k, v in inputs.items()}
    theta = (1.0 / np.float32(10000.0) ** (np.arange(0, HD0, 2, dtype=np.float32) / HD0)).astype(np.float32)
    angle = np.arange(1, T + 1, dtype=np.float32)[:, None] * theta[None, :]
    cos, sin = np.cos(angle), np.sin(angle)
    arrays = {
        "x": x["L0_attn_x"],
        "wqkv": np.concatenate([x["L0_attn_Wq"].T, x["L0_attn_Wk"].T, x["L0_attn_Wv"].T], axis=1),
        "b_qkv": np.concatenate([x["L0_attn_bq"], x["L0_attn_bk"], x["L0_attn_bv"]]),
        "wo": x["L0_attn_Wo"].T, "b_o": x["L0_attn_bo"],
        "cos": np.concatenate([cos, cos], axis=1), "sin": np.concatenate([-sin, sin], axis=1),
        "wgu": np.concatenate([x["L0_ffn_w_gate"].T, x["L0_ffn_w_up"].T], axis=1), "wd": x["L0_ffn_w_down"].T,
        "wq1": x["L1_attn_Wq"].T, "wk1": x["L1_attn_Wk"].T, "wv1": x["L1_attn_Wv"].T, "wo1": x["L1_attn_Wo"].T,
        "wrkv": np.concatenate([x["L1_ffn_W_r"].T, x["L1_ffn_W_k"].T, x["L1_ffn_W_v"].T], axis=1),
        "mu": np.stack([x["L1_ffn_mu_r"], x["L1_ffn_mu_k"]]).reshape(2, NC, P).transpose(2, 0, 1),
    }
    arrays = {f"in_{k}": np.ascontiguousarray(v) for k, v in arrays.items()}
    nc = bacc.Bacc("TRN2", target_bir_lowering=False, num_devices=1)
    a = {k[3:]: nc.dram_tensor(k, v.shape, mybir.dt.from_np(v.dtype), kind="ExternalInput").ap() for k, v in arrays.items()}
    a["out"] = nc.dram_tensor("out_x", (BATCH, T, D), F32, kind="ExternalOutput").ap()
    program(nc, a)
    return run_bass_kernel_spmd(nc, [arrays], core_ids=[0]).results[0]["out_x"]
```
